# Optimizing a Trainium2 kernel written in Bass

```python
import numpy as np
import jax
import jax.numpy as jnp

def _softmax(x, axis=-1):
    return jax.nn.softmax(x, axis=axis)

def _gelu(x):
    return jax.nn.gelu(x, approximate=True)

def _silu(x):
    return jax.nn.silu(x)

def _sigmoid(x):
    return jax.nn.sigmoid(x)

def _layernorm(x, axis=-1, eps=1e-05):
    m = jnp.mean(x, axis=axis, keepdims=True)
    v = jnp.var(x, axis=axis, keepdims=True)
    return (x - m) / jnp.sqrt(v + eps)

def _scatter_add(tgt, idx, src, axis=0):
    return tgt.at[idx].add(src)

def _segment_sum(src, seg, n):
    return jax.ops.segment_sum(src, seg, n)
kernel_name = 'mk_metaformer_d2_conv_nchw256_r2_81959d'

def setup_inputs(seed: int=0):
    np.random.seed(seed)
    _w = jnp.asarray

    def _rec_inputs():
        import jax
        import jax.numpy as jnp
        _gk = jax.random.key(seed)
        x = -0.000125 + 0.9999 * jax.random.normal(jax.random.fold_in(_gk, 1), (8, 128, 64, 64), jnp.float32)
        return x
    x = _rec_inputs()

    def _L0_conv_setup():
        import math
        import jax, jax.numpy as jnp
        import numpy as np
        B, C_IN, C_MID, H, W = (8, 128, 16, 64, 64)
        N_ANGLES = 8
        RADIUS_WIDTH = 8
        OVERLAP_RATIO = 1.5
        EPS = 1e-08

        def _build_masks(H, W):
            cy, cx = (H // 2, W // 2)
            y = jnp.arange(H, dtype=jnp.float32)[:, None] - cy
            x = jnp.arange(W, dtype=jnp.float32)[None, :] - cx
            r = jnp.sqrt(y * y + x * x)
            theta = (jnp.arctan2(y, x) + math.pi) % math.pi
            max_r = max(cy, cx)
            n_radii = int(max_r // RADIUS_WIDTH) + 1
            radius_idx = jnp.clip(jnp.floor(r / RADIUS_WIDTH).astype(jnp.int32), 0, n_radii - 1)
            delta = math.pi / N_ANGLES
            half_width = OVERLAP_RATIO * delta / 2.0
            centers = (jnp.arange(N_ANGLES, dtype=jnp.float32) * delta + delta / 2.0)[:, None, None]
            dist = jnp.abs(theta[None] - centers)
            w = jnp.clip(1.0 - dist / half_width, 0.0) * (dist < half_width)
            angle_weights = w / (w.sum(axis=0, keepdims=True) + EPS)
            return (radius_idx, angle_weights, n_radii)

        def _forward(x, w_in, w_out, bin_weights):
            Hh, Ww = x.shape[-2:]
            radius_idx, angle_weights, _ = _build_masks(Hh, Ww)
            x_proj = jnp.einsum('bchw,mc->bmhw', x, w_in)
            x_fft = jnp.fft.fftshift(jnp.fft.fft2(x_proj, norm='ortho'), axes=(-2, -1))
            mag = jnp.abs(x_fft) + EPS
            wt = bin_weights[:, :, radius_idx]
            gain = jnp.einsum('ahw,cahw->chw', angle_weights, wt)
            phase = jnp.angle(x_fft)
            enh = mag * gain[None] * (jnp.cos(phase) + 1j * jnp.sin(phase))
            x_enh = jnp.fft.ifft2(jnp.fft.ifftshift(enh, axes=(-2, -1)), norm='ortho').real
            x_enh = jnp.einsum('bmhw,cm->bchw', x_enh, w_out)
            return x + x_enh
        key = jax.random.key(seed)
        k1, k2, k3, k4 = jax.random.split(key, 4)
        _, _, n_radii = _build_masks(H, W)
        x = jax.random.normal(k1, (B, C_IN, H, W), dtype=jnp.float32)
        w_in = jax.random.normal(k2, (C_MID, C_IN), dtype=jnp.float32) * math.sqrt(2.0 / C_MID)
        w_out = jax.random.normal(k3, (C_IN, C_MID), dtype=jnp.float32) * math.sqrt(2.0 / C_IN)
        bin_weights = 1.0 + 0.1 * jax.random.normal(k4, (C_MID, N_ANGLES, n_radii), dtype=jnp.float32)
        return {'x': x, 'w_in': w_in, 'w_out': w_out, 'bin_weights': bin_weights}
    _L0_conv_all = _L0_conv_setup()
    _L0_conv_in = {k: v for k, v in _L0_conv_all.items() if k in ('w_in', 'w_out', 'bin_weights')}
    del _L0_conv_all

    def _L0_ffn_setup():
        import math
        import jax, jax.numpy as jnp
        import numpy as np
        CAPACITY_FACTOR = 1.25
        TOP_K = 2
        LN_EPS = 1e-05

        def _layer_norm(x, gamma, beta):
            mu = jnp.mean(x, axis=-1, keepdims=True)
            var = jnp.var(x, axis=-1, keepdims=True)
            return (x - mu) * jax.lax.rsqrt(var + LN_EPS) * gamma + beta
        key = jax.random.key(seed)
        ks = jax.random.split(key, 4)
        B, S, D, F, E = (8, 2048, 128, 256, 8)
        x = jax.random.normal(ks[0], (B, S, D), dtype=jnp.float32)
        Wr = jax.random.normal(ks[1], (D, E), dtype=jnp.float32) / np.sqrt(D)
        br = jnp.zeros((E,), jnp.float32)
        W1 = jax.random.normal(ks[2], (E, D, F), dtype=jnp.float32) / np.sqrt(D)
        b1 = jnp.zeros((E, F), jnp.float32)
        W2 = jax.random.normal(ks[3], (E, F, D), dtype=jnp.float32) / np.sqrt(F)
        b2 = jnp.zeros((E, D), jnp.float32)
        gamma = jnp.ones((D,), jnp.float32)
        beta = jnp.zeros((D,), jnp.float32)
        return {'x': x, 'Wr': Wr, 'br': br, 'W1': W1, 'b1': b1, 'W2': W2, 'b2': b2, 'gamma': gamma, 'beta': beta}
    _L0_ffn_all = _L0_ffn_setup()
    _L0_ffn_in = {k: v for k, v in _L0_ffn_all.items() if k in ('Wr', 'br', 'W1', 'b1', 'W2', 'b2', 'gamma', 'beta')}
    del _L0_ffn_all

    def _L1_conv_setup():
        import jax, jax.numpy as jnp
        import numpy as np
        DIM = 8
        HEADS = 32
        TOTAL = 128
        EPS = 1e-15
        BN_EPS = 1e-05

        def _conv1x1(x, w):
            return jnp.einsum('bchw,oc->bohw', x, w[:, :, 0, 0])

        def _relu_linear_att(qkv):
            B, C, H, W = qkv.shape
            G = C // (3 * DIM)
            N = H * W
            qkv = qkv.reshape(B, G, 3 * DIM, N).transpose(0, 1, 3, 2)
            q = jax.nn.relu(qkv[..., :DIM])
            k = jax.nn.relu(qkv[..., DIM:2 * DIM])
            v = qkv[..., 2 * DIM:]
            v1 = jnp.concatenate([v, jnp.ones((B, G, N, 1), qkv.dtype)], axis=-1)
            kv = jnp.einsum('bgnd,bgne->bgde', k, v1)
            out = jnp.einsum('bgnd,bgde->bgne', q, kv)
            out = out[..., :DIM] / (out[..., DIM:] + EPS)
            return out.transpose(0, 1, 3, 2).reshape(B, G * DIM, H, W)
        key = jax.random.key(seed)
        ks = jax.random.split(key, 6)
        B, C, H, W = (16, 128, 32, 32)
        x = jax.random.normal(ks[0], (B, C, H, W), jnp.float32)
        w_qkv = jax.random.normal(ks[1], (3 * TOTAL, C, 1, 1), jnp.float32) * 0.05
        w_dw = jax.random.normal(ks[2], (3 * TOTAL, 1, 5, 5), jnp.float32) * 0.05
        w_pw = jax.random.normal(ks[3], (3 * TOTAL, 3 * TOTAL // (3 * HEADS), 1, 1), jnp.float32) * 0.05
        w_proj = jax.random.normal(ks[4], (128, 2 * TOTAL, 1, 1), jnp.float32) * 0.05
        bn_gamma = jnp.ones((128,), jnp.float32)
        bn_beta = jnp.zeros((128,), jnp.float32)
        bn_mean = jnp.zeros((128,), jnp.float32)
        bn_var = jnp.ones((128,), jnp.float32)
        return {'x': x, 'w_qkv': w_qkv, 'w_dw': w_dw, 'w_pw': w_pw, 'w_proj': w_proj, 'bn_gamma': bn_gamma, 'bn_beta': bn_beta, 'bn_mean': bn_mean, 'bn_var': bn_var}
    _L1_conv_all = _L1_conv_setup()
    _L1_conv_in = {k: v for k, v in _L1_conv_all.items() if k in ('w_qkv', 'w_dw', 'w_pw', 'w_proj', 'bn_gamma', 'bn_beta', 'bn_mean', 'bn_var')}
    del _L1_conv_all

    def _L1_ffn_setup():
        import jax, jax.numpy as jnp
        import numpy as np
        NUM_EXPERTS = 8
        TOP_K = 2
        B, S, D = (8, 4096, 128)

        def _moe(tokens, router_w, w1, b1, w2, b2):
            N = tokens.shape[0]
            E = router_w.shape[0]
            logits = tokens.astype(jnp.float32) @ router_w.astype(jnp.float32).T
            probs = jax.nn.softmax(logits, axis=-1)
            rw, re = jax.lax.top_k(probs, TOP_K)
            if TOP_K > 1:
                rw = rw / jnp.maximum(rw.sum(-1, keepdims=True), 1e-12)
            rw = rw.astype(tokens.dtype)
            combine = jnp.zeros((N, E), tokens.dtype).at[jnp.arange(N)[:, None], re].set(rw)
            out = tokens
            for e in range(E):
                h = jax.nn.gelu(tokens @ w1[e] + b1[e], approximate=False)
                y = h @ w2[e] + b2[e]
                out = out + combine[:, e:e + 1] * y
            return out
        key = jax.random.key(seed)
        ks = jax.random.split(key, 4)
        scale = 1.0 / np.sqrt(D).astype(np.float32)
        return {'input_embeddings': jax.random.normal(ks[0], (B, S, D), jnp.float32), 'router_w': jax.random.normal(ks[1], (NUM_EXPERTS, D), jnp.float32) * scale, 'w1': jax.random.normal(ks[2], (NUM_EXPERTS, D, D), jnp.float32) * scale, 'b1': jnp.zeros((NUM_EXPERTS, D), jnp.float32), 'w2': jax.random.normal(ks[3], (NUM_EXPERTS, D, D), jnp.float32) * scale, 'b2': jnp.zeros((NUM_EXPERTS, D), jnp.float32)}
    _L1_ffn_all = _L1_ffn_setup()
    _L1_ffn_in = {k: v for k, v in _L1_ffn_all.items() if k in ('router_w', 'w1', 'b1', 'w2', 'b2')}
    del _L1_ffn_all
    return {'x': x, 'L0_conv_w_in': _L0_conv_in['w_in'], 'L0_conv_w_out': _L0_conv_in['w_out'], 'L0_conv_bin_weights': _L0_conv_in['bin_weights'], 'L0_ffn_Wr': _L0_ffn_in['Wr'], 'L0_ffn_br': _L0_ffn_in['br'], 'L0_ffn_W1': _L0_ffn_in['W1'], 'L0_ffn_b1': _L0_ffn_in['b1'], 'L0_ffn_W2': _L0_ffn_in['W2'], 'L0_ffn_b2': _L0_ffn_in['b2'], 'L0_ffn_gamma': _L0_ffn_in['gamma'], 'L0_ffn_beta': _L0_ffn_in['beta'], 'L1_conv_w_qkv': _L1_conv_in['w_qkv'], 'L1_conv_w_dw': _L1_conv_in['w_dw'], 'L1_conv_w_pw': _L1_conv_in['w_pw'], 'L1_conv_w_proj': _L1_conv_in['w_proj'], 'L1_conv_bn_gamma': _L1_conv_in['bn_gamma'], 'L1_conv_bn_beta': _L1_conv_in['bn_beta'], 'L1_conv_bn_mean': _L1_conv_in['bn_mean'], 'L1_conv_bn_var': _L1_conv_in['bn_var'], 'L1_ffn_router_w': _L1_ffn_in['router_w'], 'L1_ffn_w1': _L1_ffn_in['w1'], 'L1_ffn_b1': _L1_ffn_in['b1'], 'L1_ffn_w2': _L1_ffn_in['w2'], 'L1_ffn_b2': _L1_ffn_in['b2']}

def reference(x, L0_conv_w_in, L0_conv_w_out, L0_conv_bin_weights, L0_ffn_Wr, L0_ffn_br, L0_ffn_W1, L0_ffn_b1, L0_ffn_W2, L0_ffn_b2, L0_ffn_gamma, L0_ffn_beta, L1_conv_w_qkv, L1_conv_w_dw, L1_conv_w_pw, L1_conv_w_proj, L1_conv_bn_gamma, L1_conv_bn_beta, L1_conv_bn_mean, L1_conv_bn_var, L1_ffn_router_w, L1_ffn_w1, L1_ffn_b1, L1_ffn_w2, L1_ffn_b2):
    import jax
    import jax.numpy as jnp

    def _L0_conv_ref(x, w_in, w_out, bin_weights):
        import math
        import jax, jax.numpy as jnp
        import numpy as np
        B, C_IN, C_MID, H, W = (8, 128, 16, 64, 64)
        N_ANGLES = 8
        RADIUS_WIDTH = 8
        OVERLAP_RATIO = 1.5
        EPS = 1e-08

        def _build_masks(H, W):
            cy, cx = (H // 2, W // 2)
            y = jnp.arange(H, dtype=jnp.float32)[:, None] - cy
            x = jnp.arange(W, dtype=jnp.float32)[None, :] - cx
            r = jnp.sqrt(y * y + x * x)
            theta = (jnp.arctan2(y, x) + math.pi) % math.pi
            max_r = max(cy, cx)
            n_radii = int(max_r // RADIUS_WIDTH) + 1
            radius_idx = jnp.clip(jnp.floor(r / RADIUS_WIDTH).astype(jnp.int32), 0, n_radii - 1)
            delta = math.pi / N_ANGLES
            half_width = OVERLAP_RATIO * delta / 2.0
            centers = (jnp.arange(N_ANGLES, dtype=jnp.float32) * delta + delta / 2.0)[:, None, None]
            dist = jnp.abs(theta[None] - centers)
            w = jnp.clip(1.0 - dist / half_width, 0.0) * (dist < half_width)
            angle_weights = w / (w.sum(axis=0, keepdims=True) + EPS)
            return (radius_idx, angle_weights, n_radii)

        def _forward(x, w_in, w_out, bin_weights):
            Hh, Ww = x.shape[-2:]
            radius_idx, angle_weights, _ = _build_masks(Hh, Ww)
            x_proj = jnp.einsum('bchw,mc->bmhw', x, w_in)
            x_fft = jnp.fft.fftshift(jnp.fft.fft2(x_proj, norm='ortho'), axes=(-2, -1))
            mag = jnp.abs(x_fft) + EPS
            wt = bin_weights[:, :, radius_idx]
            gain = jnp.einsum('ahw,cahw->chw', angle_weights, wt)
            phase = jnp.angle(x_fft)
            enh = mag * gain[None] * (jnp.cos(phase) + 1j * jnp.sin(phase))
            x_enh = jnp.fft.ifft2(jnp.fft.ifftshift(enh, axes=(-2, -1)), norm='ortho').real
            x_enh = jnp.einsum('bmhw,cm->bchw', x_enh, w_out)
            return x + x_enh
        return _forward(x, w_in, w_out, bin_weights)

    def _L0_ffn_ref(x, Wr, br, W1, b1, W2, b2, gamma, beta):
        import math
        import jax, jax.numpy as jnp
        import numpy as np
        CAPACITY_FACTOR = 1.25
        TOP_K = 2
        LN_EPS = 1e-05

        def _layer_norm(x, gamma, beta):
            mu = jnp.mean(x, axis=-1, keepdims=True)
            var = jnp.var(x, axis=-1, keepdims=True)
            return (x - mu) * jax.lax.rsqrt(var + LN_EPS) * gamma + beta
        B, S, D = x.shape
        E = Wr.shape[1]
        N = B * S
        K = TOP_K
        logits = jnp.mean(x, axis=1) @ Wr + br
        routing_weights = jax.nn.softmax(logits, axis=-1)
        capacity = float(math.ceil(N * CAPACITY_FACTOR / E))
        expected_loads = routing_weights.sum(axis=0) * (N / B)
        scale = jnp.where(expected_loads > capacity, capacity / expected_loads, 1.0)
        routing_weights = jax.nn.softmax(routing_weights * scale, axis=-1)
        rw_tok = jnp.broadcast_to(routing_weights[:, None, :], (B, S, E)).reshape(N, E)
        top_w, top_i = jax.lax.top_k(rw_tok, K)
        top_w = jax.nn.softmax(top_w, axis=-1)
        xf = x.reshape(N, D)
        h = jax.nn.gelu(jnp.einsum('nd,edf->enf', xf, W1) + b1[:, None, :], approximate=False)
        y = jnp.einsum('enf,efd->end', h, W2) + b2[:, None, :]
        w_dense = jnp.zeros((N, E), x.dtype).at[jnp.arange(N)[:, None], top_i].add(top_w)
        out = jnp.einsum('ne,end->nd', w_dense, y).reshape(B, S, D)
        out = _layer_norm(out + x, gamma, beta)
        return out

    def _L1_conv_ref(x, w_qkv, w_dw, w_pw, w_proj, bn_gamma, bn_beta, bn_mean, bn_var):
        import jax, jax.numpy as jnp
        import numpy as np
        DIM = 8
        HEADS = 32
        TOTAL = 128
        EPS = 1e-15
        BN_EPS = 1e-05

        def _conv1x1(x, w):
            return jnp.einsum('bchw,oc->bohw', x, w[:, :, 0, 0])

        def _relu_linear_att(qkv):
            B, C, H, W = qkv.shape
            G = C // (3 * DIM)
            N = H * W
            qkv = qkv.reshape(B, G, 3 * DIM, N).transpose(0, 1, 3, 2)
            q = jax.nn.relu(qkv[..., :DIM])
            k = jax.nn.relu(qkv[..., DIM:2 * DIM])
            v = qkv[..., 2 * DIM:]
            v1 = jnp.concatenate([v, jnp.ones((B, G, N, 1), qkv.dtype)], axis=-1)
            kv = jnp.einsum('bgnd,bgne->bgde', k, v1)
            out = jnp.einsum('bgnd,bgde->bgne', q, kv)
            out = out[..., :DIM] / (out[..., DIM:] + EPS)
            return out.transpose(0, 1, 3, 2).reshape(B, G * DIM, H, W)
        B = x.shape[0]
        qkv = _conv1x1(x, w_qkv)
        agg = jax.lax.conv_general_dilated(qkv, w_dw, window_strides=(1, 1), padding=((2, 2), (2, 2)), dimension_numbers=('NCHW', 'OIHW', 'NCHW'), feature_group_count=3 * TOTAL)
        Gp = 3 * HEADS
        cg = 3 * TOTAL // Gp
        Bh, _, H, W = agg.shape
        agg_g = agg.reshape(Bh, Gp, cg, H, W)
        w_pw_g = w_pw[:, :, 0, 0].reshape(Gp, cg, cg)
        agg = jnp.einsum('bgchw,goc->bgohw', agg_g, w_pw_g).reshape(Bh, 3 * TOTAL, H, W)
        ms_qkv = jnp.concatenate([qkv, agg], axis=1)
        out = _relu_linear_att(ms_qkv)
        out = _conv1x1(out, w_proj)
        inv = bn_gamma / jnp.sqrt(bn_var + BN_EPS)
        out = out * inv[None, :, None, None] + (bn_beta - bn_mean * inv)[None, :, None, None]
        return out

    def _L1_ffn_ref(input_embeddings, router_w, w1, b1, w2, b2):
        import jax, jax.numpy as jnp
        import numpy as np
        NUM_EXPERTS = 8
        TOP_K = 2
        B, S, D = (8, 4096, 128)

        def _moe(tokens, router_w, w1, b1, w2, b2):
            N = tokens.shape[0]
            E = router_w.shape[0]
            logits = tokens.astype(jnp.float32) @ router_w.astype(jnp.float32).T
            probs = jax.nn.softmax(logits, axis=-1)
            rw, re = jax.lax.top_k(probs, TOP_K)
            if TOP_K > 1:
                rw = rw / jnp.maximum(rw.sum(-1, keepdims=True), 1e-12)
            rw = rw.astype(tokens.dtype)
            combine = jnp.zeros((N, E), tokens.dtype).at[jnp.arange(N)[:, None], re].set(rw)
            out = tokens
            for e in range(E):
                h = jax.nn.gelu(tokens @ w1[e] + b1[e], approximate=False)
                y = h @ w2[e] + b2[e]
                out = out + combine[:, e:e + 1] * y
            return out
        b, s, d = input_embeddings.shape
        tokens = input_embeddings.reshape(b * s, d)
        return _moe(tokens, router_w, w1, b1, w2, b2).reshape(b, s, d)

    def _gn(v, G=32, eps=1e-05):
        B_, C_, H_, W_ = v.shape
        g = v.reshape(B_, G, C_ // G, H_, W_)
        m = jnp.mean(g, axis=(2, 3, 4), keepdims=True)
        s = jnp.var(g, axis=(2, 3, 4), keepdims=True)
        return ((g - m) / jnp.sqrt(s + eps)).reshape(v.shape)

    def _ln_c(v, eps=1e-06):
        m = jnp.mean(v, axis=1, keepdims=True)
        s = jnp.var(v, axis=1, keepdims=True)
        return (v - m) / jnp.sqrt(s + eps)

    def _ln_t(v, eps=1e-05):
        m = jnp.mean(v, axis=-1, keepdims=True)
        s = jnp.var(v, axis=-1, keepdims=True)
        return (v - m) / jnp.sqrt(s + eps)

    def _to_tokens(v):
        B_, C_, H_, W_ = v.shape
        return v.reshape(B_, C_, H_ * W_).transpose(0, 2, 1)

    def _from_tokens(t, like):
        B_, C_, H_, W_ = like.shape
        return t.transpose(0, 2, 1).reshape(B_, C_, H_, W_)
    x = x + _L0_conv_ref(_ln_c(x), L0_conv_w_in, L0_conv_w_out, L0_conv_bin_weights)
    t = _to_tokens(x)
    t = t + _L0_ffn_ref(_ln_t(t), L0_ffn_Wr, L0_ffn_br, L0_ffn_W1, L0_ffn_b1, L0_ffn_W2, L0_ffn_b2, L0_ffn_gamma, L0_ffn_beta)
    x = _from_tokens(t, x)
    x = x + _L1_conv_ref(_ln_c(x), L1_conv_w_qkv, L1_conv_w_dw, L1_conv_w_pw, L1_conv_w_proj, L1_conv_bn_gamma, L1_conv_bn_beta, L1_conv_bn_mean, L1_conv_bn_var)
    t = _to_tokens(x)
    t = t + _L1_ffn_ref(_ln_t(t), L1_ffn_router_w, L1_ffn_w1, L1_ffn_b1, L1_ffn_w2, L1_ffn_b2)
    x = _from_tokens(t, x)
    return x

_drawn_inputs = setup_inputs


def setup_inputs(seed=0):
    import zlib

    import numpy as np

    out = dict(_drawn_inputs(seed))
    spreads = {'L0_ffn_br': (0.0, 0.1),
     'L0_ffn_b1': (0.0, 0.597),
     'L0_ffn_b2': (0.0, 0.458),
     'L0_ffn_gamma': (1.0, 0.2),
     'L0_ffn_beta': (0.0, 0.1),
     'L1_conv_bn_gamma': (1.0, 0.6),
     'L1_conv_bn_beta': (0.0, 0.269),
     'L1_conv_bn_mean': (0.0, 0.27),
     'L1_conv_bn_var': (1.0, 0.6),
     'L1_ffn_b1': (0.0, 0.764),
     'L1_ffn_b2': (0.0, 0.511)}
    factors = {'L0_ffn_Wr': 8.0,
     'L1_conv_w_qkv': 3.76,
     'L1_conv_w_dw': 8.0,
     'L1_conv_w_pw': 8.0,
     'L1_conv_w_proj': 3.772}
    for name, (base, spread) in spreads.items():
        noise = np.random.default_rng([zlib.crc32(name.encode()), seed]).standard_normal(out[name].shape)
        drawn = base * np.exp(spread * noise) if base else spread * noise
        out[name] = jnp.asarray(drawn.astype(out[name].dtype))
    for name, factor in factors.items():
        out[name] = (out[name] * factor).astype(out[name].dtype)
    return out
```

```python
from contextlib import ExitStack

import concourse.bass as bass
from concourse import mybir
from concourse.alu_op_type import AluOpType as ALU

F32 = mybir.dt.float32
F32R = mybir.dt.float32r
BF16 = mybir.dt.bfloat16
ACT = mybir.ActivationFunctionType
AX = mybir.AxisListType

B, C, HW, SIDE = 8, 128, 4096, 64
MID = 16
E = 8
F0 = 256
CH = 512
NCH = HW // CH
PH = 4
HB = SIDE // PH
PADW = SIDE + 4
ROWS = CH // SIDE
GROUPS = 12
GC = 32
TAPS = 10
EPS_C, EPS_T, EPS_MAG, EPS_ATT = 1e-6, 1e-5, 1e-8, 1e-15


def chunk(buf, c):
    return buf[:, bass.ds(c * CH, CH)]


class Norm:

    def __init__(self, nc, ctx, tag, ones, banks):
        sb = lambda name: [ctx.enter_context(nc.sbuf_tensor(f"{tag}_{name}{k}", [128, CH], F32)) for k in range(2)]
        sem = lambda name: ctx.enter_context(nc.semaphore(f"{tag}_{name}"))
        self.nc, self.ones = nc, ones
        self.mean, self.var = banks[0:2], banks[2:4]
        self.centred, self.square, self.std, self.rstd = sb("centred"), sb("square"), sb("std"), sb("rstd")
        self.mean_done, self.var_done = sem("mean_done"), sem("var_done")
        self.centred_done, self.square_done = sem("centred_done"), sem("square_done")
        self.std_done, self.rstd_done, self.out_done = sem("std_done"), sem("rstd_done"), sem("out_done")

    def start(self, dve):
        dve.sem_inc(self.centred_done, 2)
        dve.sem_inc(self.out_done, 2)

    def pair_pe(self, pe, n, src):
        for k in range(2):
            pe.wait_ge(self.centred_done, n + k + 1)
            self.nc.tensor.matmul(self.mean[k], self.ones[:, :], src(k), start=True, stop=True).then_inc(self.mean_done, 1)
        for k in range(2):
            pe.wait_ge(self.square_done, n + k + 1)
            self.nc.tensor.matmul(self.var[k], self.ones[:, :], self.square[k][:, :], start=True, stop=True).then_inc(self.var_done, 1)

    def pair_act(self, act, n, eps):
        for k in range(2):
            act.wait_ge(self.centred_done, n + k + 3)
            self.nc.scalar.activation(self.square[k][:, :], self.centred[k][:, :], ACT.Square).then_inc(self.square_done, 1)
        for k in range(2):
            act.wait_ge(self.var_done, n + k + 1)
            self.nc.scalar.activation(self.std[k][:, :], self.var[k], ACT.Sqrt, bias=eps).then_inc(self.std_done, 1)

    def pair_dve(self, dve, n, src, out, total=None):
        for k in range(2):
            dve.wait_ge(self.mean_done, n + k + 1)
            dve.wait_ge(self.out_done, n + k + 1)
            self.nc.vector.tensor_tensor(self.centred[k][:, :], src(k), self.mean[k], ALU.subtract).then_inc(self.centred_done, 1)
        for k in range(2):
            dve.wait_ge(self.std_done, n + k + 1)
            self.nc.vector.reciprocal(self.rstd[k][:, :], self.std[k][:, :]).then_inc(self.rstd_done, 1)
        for k in range(2):
            dve.wait_ge(self.rstd_done, n + k + 1)
            if total is None:
                self.nc.vector.tensor_tensor(out(k), self.centred[k][:, :], self.rstd[k][:, :], ALU.mult).then_inc(self.out_done, 1)
            else:
                self.nc.vector.scalar_tensor_tensor(out=out(k), in0=self.centred[k][:, :], scalar=1.0, in1=self.rstd[k][:, :],
                                                    op0=ALU.mult, op1=ALU.mult, accum_out=total(k)).then_inc(self.out_done, 1)


def passing(sem):
    return lambda eng: eng.sem_inc(sem, 1)


class Chain:

    def __init__(self, eng, sem, base=0):
        self.eng, self.sem, self.base, self.count = eng, sem, base, 0

    def __call__(self, ins):
        self.count += 1
        ins.then_inc(self.sem, 1)
        self.eng.wait_ge(self.sem, self.base + self.count)


def phase_spectral(nc, d):
    with ExitStack() as ctx:
        sb = lambda name, shape: ctx.enter_context(nc.sbuf_tensor("a_" + name, shape, F32))
        sem = lambda name: ctx.enter_context(nc.semaphore("a_" + name))
        ps = ctx.enter_context(nc.psum_tensor("a_ps", [128, 8 * CH], F32))
        bank = lambda i: ps[:, i * CH:(i + 1) * CH]
        low, high = ps[0:SIDE, 0:4 * CH], ps[0:SIDE, 4 * CH:8 * CH]

        ones, w_in, w_out = sb("ones", [128, 128]), sb("w_in", [128, MID]), sb("w_out", [MID, 128])
        dft = sb("dft", [SIDE, 9 * SIDE + 4 * SIDE])
        mask, binw = sb("mask", [40, HW]), sb("binw", [40, MID])
        gain = sb("gain", [SIDE, MID, SIDE])
        X, XN, XE = sb("X", [128, HW]), sb("XN", [128, HW]), sb("XE", [MID, HW])
        proj, rows, enh, back = (sb("proj", [SIDE, MID, SIDE]), sb("rows", [SIDE, MID, 128]),
                                 sb("enh", [SIDE, MID, 128]), sb("back", [SIDE, MID, 128]))
        image = sb("image", [SIDE, MID, SIDE])
        sqz = sb("sqz", [SIDE, MID, 128])
        r2, mag, zero, den, rec, num, fac, shifted = [sb(n, [SIDE, MID, SIDE]) for n in
                                                      ("r2", "mag", "zero", "den", "rec", "num", "fac", "shifted")]
        mixed = [sb(f"mixed{k}", [128, CH]) for k in range(2)]
        sums, eps_c, eps_t = sb("sums", [128, B * NCH]), sb("eps_c", [128, 1]), sb("eps_t", [128, 1])
        total = sb("total", [128, B])

        g1, g2a, g2b = dft[:, 0:128], dft[:, 128:256], dft[:, 256:384]
        g3a, g3b = dft[:, 384:512], dft[:, 512:640]
        g4a, g4b = dft[:, 640:704], dft[:, 704:768]

        norm = Norm(nc, ctx, "a_norm", ones, [bank(i) for i in range(4)])
        const_loaded, eps_set, x_loaded = sem("const_loaded"), sem("eps_set"), sem("x_loaded")
        x1_stored, tn_stored, xe_stored, xe_loaded = sem("x1_stored"), sem("tn_stored"), sem("xe_stored"), sem("xe_loaded")
        gain_pe, gain_ready = sem("gain_pe"), sem("gain_ready")
        proj_pe, proj_ready, rows_pe, rows_ready = sem("proj_pe"), sem("proj_ready"), sem("rows_pe"), sem("rows_ready")
        freq_pe, sqz_done, r2_done, mag_done, enh_ready = sem("freq_pe"), sem("sqz_done"), sem("r2_done"), sem("mag_done"), sem("enh_ready")
        back_pe, back_ready, image_pe, image_ready = sem("back_pe"), sem("back_ready"), sem("image_pe"), sem("image_ready")
        y_pe, mixed_done, x1_done, own = sem("y_pe"), sem("mixed_done"), sem("x1_done"), sem("own")
        total_done, total_stored = sem("total_done"), sem("total_stored")
        passed = passing(sem("passed"))
        consts = [(ones, "ones"), (w_in, "w_in"), (w_out, "w_out"), (dft[:, 0:768], "dft"), (mask, "mask"), (binw, "binw")]

        with nc.Block() as block:
            @block.sync
            def _(sp):
                for dst, name in consts:
                    sp.dma_start(dst if name == "dft" else dst[:, :], d[name]).then_inc(const_loaded, 16)
                sp.sem_inc(x1_stored, 16)
                sp.sem_inc(tn_stored, 16)
                with sp.Fori(0, B) as b:
                    sp.wait_ge(x1_stored, b * 16 + 16)
                    sp.dma_start(X[:, :], d["x"][bass.ds(b, 1), :, :].rearrange("a p n -> p (a n)")).then_inc(x_loaded, 16)
                    sp.wait_ge(image_ready, b + 1)
                    sp.dma_start(d["xe"].rearrange("m h w -> h m w"), image[:, :, :]).then_inc(xe_stored, 16)
                    sp.wait_ge(xe_stored, b * 16 + 16)
                    sp.dma_start(XE[:, :], d["xe"].rearrange("m h w -> m (h w)")).then_inc(xe_loaded, 16)
                    sp.wait_ge(norm.out_done, b * 2 * NCH + 2 * NCH + 2)
                    sp.dma_start(d["x1"][bass.ds(b, 1), :, :].rearrange("a p n -> p (a n)"), X[:, :]).then_inc(x1_stored, 16)
                    sp.dma_start(d["tn"][bass.ds(b, 1), :, :].rearrange("a p n -> p (a n)"), XN[:, :]).then_inc(tn_stored, 16)
                sp.wait_ge(total_done, 1)
                sp.dma_start(d["total"], total[:, :]).then_inc(total_stored, 16)
                sp.wait_ge(x1_stored, B * 16 + 16)
                sp.wait_ge(tn_stored, B * 16 + 16)
                sp.wait_ge(total_stored, 16)

            @block.tensor
            def _(pe):
                pe.wait_ge(const_loaded, 16 * len(consts))
                for kx in range(SIDE):
                    last = nc.tensor.matmul(high[:, kx * MID:(kx + 1) * MID], mask[:, kx * SIDE:(kx + 1) * SIDE], binw[:, :],
                                            start=True, stop=True)
                last.then_inc(gain_pe, 1)
                pe.wait_ge(gain_ready, 1)
                passed(pe)
                with pe.Fori(0, B) as b:
                    pe.wait_ge(x_loaded, b * 16 + 16)
                    passed(pe)
                    with pe.Fori(0, NCH // 2) as p:
                        norm.pair_pe(pe, b * 2 * NCH + p * 2, lambda k: chunk(X, p * 2 + k))
                    pe.wait_ge(norm.out_done, b * 2 * NCH + NCH + 2)
                    cols = XN[:, :].rearrange("p (h w) -> p w h", w=SIDE)
                    for w in range(SIDE):
                        last = nc.tensor.matmul(high[:, w * MID:(w + 1) * MID], cols[:, w, :], w_in[:, :], start=True, stop=True)
                    last.then_inc(proj_pe, 1)
                    pe.wait_ge(proj_ready, b + 1)
                    passed(pe)
                    for m in range(MID):
                        last = nc.tensor.matmul(low[:, m * 128:(m + 1) * 128], proj[:, m, :], g1, start=True, stop=True)
                    last.then_inc(rows_pe, 1)
                    pe.wait_ge(rows_ready, b + 1)
                    passed(pe)
                    for m in range(MID):
                        nc.tensor.matmul(high[:, m * 128:(m + 1) * 128], rows[:, m, 0:SIDE], g2a, start=True, stop=False)
                        last = nc.tensor.matmul(high[:, m * 128:(m + 1) * 128], rows[:, m, SIDE:128], g2b, start=False, stop=True)
                    last.then_inc(freq_pe, 1)
                    pe.wait_ge(enh_ready, b + 1)
                    passed(pe)
                    for m in range(MID):
                        nc.tensor.matmul(low[:, m * 128:(m + 1) * 128], enh[:, m, 0:SIDE], g3a, start=True, stop=False)
                        last = nc.tensor.matmul(low[:, m * 128:(m + 1) * 128], enh[:, m, SIDE:128], g3b, start=False, stop=True)
                    last.then_inc(back_pe, 1)
                    pe.wait_ge(back_ready, b + 1)
                    passed(pe)
                    for m in range(MID):
                        nc.tensor.matmul(high[:, m * SIDE:(m + 1) * SIDE], back[:, m, 0:SIDE], g4a, start=True, stop=False)
                        last = nc.tensor.matmul(high[:, m * SIDE:(m + 1) * SIDE], back[:, m, SIDE:128], g4b, start=False, stop=True)
                    last.then_inc(image_pe, 1)
                    pe.wait_ge(xe_loaded, b * 16 + 16)
                    passed(pe)
                    with pe.Fori(0, NCH // 2) as p:
                        for k in range(2):
                            pe.wait_ge(x1_done, b * NCH + p * 2 + k + 1)
                            passed(pe)
                            nc.tensor.matmul(bank(4 + k), w_out[:, :], XE[:, bass.ds((p * 2 + k) * CH, CH)],
                                             start=True, stop=True).then_inc(y_pe, 1)
                    pe.wait_ge(x1_done, b * NCH + NCH + 2)
                    passed(pe)
                    with pe.Fori(0, NCH // 2) as p:
                        norm.pair_pe(pe, b * 2 * NCH + NCH + p * 2, lambda k: chunk(X, p * 2 + k))

            @block.scalar
            def _(act):
                act.wait_ge(eps_set, 2)
                with act.Fori(0, B) as b:
                    with act.Fori(0, NCH // 2) as p:
                        norm.pair_act(act, b * 2 * NCH + p * 2, eps_c[:, :])
                    act.wait_ge(rows_pe, b + 1)
                    nc.scalar.activation(rows[:, :, :].rearrange("p m k -> p (m k)"), low, ACT.Copy).then_inc(rows_ready, 1)
                    act.wait_ge(freq_pe, b + 1)
                    nc.scalar.activation(sqz[:, :, :].rearrange("p m k -> p (m k)"), high, ACT.Square).then_inc(sqz_done, 1)
                    act.wait_ge(r2_done, b + 1)
                    nc.scalar.activation(mag[:, :, :], r2[:, :, :], ACT.Sqrt).then_inc(mag_done, 1)
                    act.wait_ge(back_pe, b + 1)
                    nc.scalar.activation(back[:, :, :].rearrange("p m k -> p (m k)"), low, ACT.Copy).then_inc(back_ready, 1)
                    with act.Fori(0, NCH // 2) as p:
                        norm.pair_act(act, b * 2 * NCH + NCH + p * 2, eps_t[:, :])

            @block.vector
            def _(dve):
                nc.vector.memset(eps_c[:, :], EPS_C).then_inc(eps_set, 1)
                nc.vector.memset(eps_t[:, :], EPS_T).then_inc(eps_set, 1)
                norm.start(dve)
                dve.wait_ge(const_loaded, 16 * len(consts))
                dve.sem_inc(x1_done, 2)
                dve.wait_ge(gain_pe, 1)
                nc.vector.tensor_copy(gain[:, :, :], high[:, 0:SIDE * MID].rearrange("p (x m) -> p m x", m=MID)).then_inc(gain_ready, 1)
                dve.wait_ge(gain_ready, 1)
                passed(dve)
                with dve.Fori(0, B) as b:
                    dve.wait_ge(x_loaded, b * 16 + 16)
                    dve.wait_ge(tn_stored, b * 16 + 16)
                    passed(dve)
                    with dve.Fori(0, NCH // 2) as p:
                        norm.pair_dve(dve, b * 2 * NCH + p * 2, lambda k: chunk(X, p * 2 + k), lambda k: chunk(XN, p * 2 + k))
                    dve.wait_ge(proj_pe, b + 1)
                    nc.vector.tensor_copy(proj[:, :, :], high[:, 0:SIDE * MID].rearrange("p (w m) -> p m w", m=MID)).then_inc(proj_ready, 1)
                    link = Chain(dve, own, b * 8)
                    dve.wait_ge(sqz_done, b + 1)
                    nc.vector.tensor_tensor(r2[:, :, :], sqz[:, :, 0:SIDE], sqz[:, :, SIDE:128], ALU.add).then_inc(r2_done, 1)
                    dve.wait_ge(mag_done, b + 1)
                    link(nc.vector.tensor_scalar(zero[:, :, :], mag[:, :, :], 0.0, None, ALU.is_equal))
                    link(nc.vector.tensor_tensor(den[:, :, :], mag[:, :, :], zero[:, :, :], ALU.add))
                    link(nc.vector.reciprocal(rec[:, :, :], den[:, :, :]))
                    link(nc.vector.scalar_tensor_tensor(out=num[:, :, :], in0=mag[:, :, :], scalar=EPS_MAG, in1=gain[:, :, :],
                                                        op0=ALU.add, op1=ALU.mult))
                    link(nc.vector.tensor_tensor(fac[:, :, :], num[:, :, :], rec[:, :, :], ALU.mult))
                    z = high.rearrange("p (m k) -> p m k", k=128)
                    link(nc.vector.tensor_tensor(shifted[:, :, :], z[:, :, 0:SIDE], zero[:, :, :], ALU.add))
                    link(nc.vector.tensor_tensor(enh[:, :, 0:SIDE], shifted[:, :, :], fac[:, :, :], ALU.mult))
                    link(nc.vector.tensor_tensor(enh[:, :, SIDE:128], z[:, :, SIDE:128], fac[:, :, :], ALU.mult))
                    dve.sem_inc(enh_ready, 1)
                    dve.wait_ge(image_pe, b + 1)
                    nc.vector.tensor_copy(image[:, :, :].rearrange("p m w -> p (m w)"), high[:, 0:SIDE * MID]).then_inc(image_ready, 1)
                    with dve.Fori(0, NCH // 2) as p:
                        for k in range(2):
                            n = b * NCH + p * 2 + k
                            dve.wait_ge(y_pe, n + 1)
                            dve.wait_ge(x1_done, n + 1)
                            nc.vector.tensor_tensor(mixed[k][:, :], bank(4 + k), chunk(XN, p * 2 + k), ALU.add).then_inc(mixed_done, 1)
                            dve.wait_ge(mixed_done, n + 1)
                            nc.vector.tensor_tensor(chunk(X, p * 2 + k), chunk(X, p * 2 + k), mixed[k][:, :], ALU.add).then_inc(x1_done, 1)
                    dve.wait_ge(x1_done, b * NCH + NCH + 2)
                    passed(dve)
                    with dve.Fori(0, NCH // 2) as p:
                        norm.pair_dve(dve, b * 2 * NCH + NCH + p * 2, lambda k: chunk(X, p * 2 + k), lambda k: chunk(XN, p * 2 + k),
                                      total=lambda k: sums[:, bass.ds(b * NCH + p * 2 + k, 1)])
                dve.wait_ge(norm.out_done, B * 2 * NCH + 2)
                nc.vector.tensor_reduce(total[:, :], sums[:, :].rearrange("p (b c) -> p b c", c=NCH), AX.X, ALU.add).then_inc(total_done, 1)


def phase_route0(nc, d, route):
    pick, pickw, dense = route
    with ExitStack() as ctx:
        sb = lambda name, shape: ctx.enter_context(nc.sbuf_tensor("r_" + name, shape, F32))
        sem = lambda name: ctx.enter_context(nc.semaphore("r_" + name))
        total, wide = sb("total", [128, B]), sb("wide", [128, B, 128])
        wr, br, before = sb("wr", [128, E]), sb("br", [128, E]), sb("before", [128, E * E])
        logit, ex, rw, sel = [sb(n, [128, B, E]) for n in ("logit", "ex", "rw", "sel")]
        top, low = sb("top", [128, B]), sb("low", [128, B])
        load, scale = sb("load", [128, E]), sb("scale", [128, E])
        more, same, rank = sb("more", [128, B, E, E]), sb("same", [128, B, E, E]), sb("rank", [128, B, E])
        ps = ctx.enter_context(nc.psum_tensor("r_ps", [128, B * E], F32))
        loaded, wide_ready, logit_pe, own, exp_in, exp_done = [sem(n) for n in
                                                              ("loaded", "wide_ready", "logit_pe", "own", "exp_in", "exp_done")]
        per_e = lambda t: t[:, :].unsqueeze(2).broadcast_to([128, B, E])
        per_b = lambda t: t[:, :].unsqueeze(1).broadcast_to([128, B, E])
        with nc.Block() as block:
            @block.sync
            def _(sp):
                for dst, name in ((total, "total"), (wr, "wr"), (br, "br"), (before, "before")):
                    sp.dma_start(dst[:, :], d[name]).then_inc(loaded, 16)

            @block.tensor
            def _(pe):
                pe.wait_ge(wide_ready, 1)
                for b in range(B):
                    last = nc.tensor.matmul(ps[:, b * E:(b + 1) * E], wide[:, b, :], wr[:, :], start=True, stop=True)
                last.then_inc(logit_pe, 1)

            @block.scalar
            def _(act):
                for i in range(3):
                    act.wait_ge(exp_in, i + 1)
                    nc.scalar.activation(ex[:, :, :], ex[:, :, :], ACT.Exp).then_inc(exp_done, 1)

            @block.vector
            def _(dve):
                link = Chain(dve, own)
                dve.wait_ge(loaded, 64)
                nc.vector.tensor_copy(wide[:, :, :], total[:, :].unsqueeze(2).broadcast_to([128, B, 128])).then_inc(wide_ready, 1)
                dve.wait_ge(logit_pe, 1)
                link(nc.vector.scalar_tensor_tensor(out=logit[:, :, :], in0=ps[:, :].rearrange("p (b e) -> p b e", e=E), scalar=1.0 / HW,
                                                    in1=per_b(br), op0=ALU.mult, op1=ALU.add))

                def softmax(src, dst, i):
                    link(nc.vector.tensor_reduce(top[:, :], src[:, :, :], AX.X, ALU.max))
                    link(nc.vector.tensor_tensor(ex[:, :, :], src[:, :, :], per_e(top), ALU.subtract))
                    dve.sem_inc(exp_in, 1)
                    dve.wait_ge(exp_done, i + 1)
                    if dst is not None:
                        link(nc.vector.tensor_reduce(low[:, :], ex[:, :, :], AX.X, ALU.add))
                        link(nc.vector.reciprocal(low[:, :], low[:, :]))
                        link(nc.vector.tensor_tensor(dst[:, :, :], ex[:, :, :], per_e(low), ALU.mult))

                softmax(logit, rw, 0)
                link(nc.vector.tensor_reduce(load[:, :], rw[:, :, :].rearrange("p b e -> p e b"), AX.X, ALU.add))
                link(nc.vector.tensor_scalar(load[:, :], load[:, :], float(HW), None, ALU.mult))
                link(nc.vector.reciprocal(load[:, :], load[:, :]))
                link(nc.vector.tensor_scalar(scale[:, :], load[:, :], float(-(-B * HW * 5 // (4 * E))), 1.0, ALU.mult, ALU.min))
                link(nc.vector.tensor_tensor(logit[:, :, :], rw[:, :, :], per_b(scale), ALU.mult))
                softmax(logit, rw, 1)
                mine = rw[:, :, :].unsqueeze(3).broadcast_to([128, B, E, E])
                other = rw[:, :, :].unsqueeze(2).broadcast_to([128, B, E, E])
                first = before[:, :].rearrange("p (e f) -> p e f", f=E)
                link(nc.vector.tensor_tensor(more[:, :, :, :], other, mine, ALU.is_gt))
                link(nc.vector.tensor_tensor(same[:, :, :, :], other, mine, ALU.is_equal))
                for b in range(B):
                    link(nc.vector.tensor_tensor(same[:, b, :, :], same[:, b, :, :], first, ALU.mult))
                link(nc.vector.tensor_tensor(more[:, :, :, :], more[:, :, :, :], same[:, :, :, :], ALU.add))
                link(nc.vector.tensor_reduce(rank[:, :, :], more[:, :, :, :], AX.X, ALU.add))
                softmax(rw, None, 2)
                link(nc.vector.tensor_scalar(sel[:, :, :], rank[:, :, :], 1.5, None, ALU.is_lt))
                link(nc.vector.tensor_tensor(ex[:, :, :], ex[:, :, :], sel[:, :, :], ALU.mult))
                link(nc.vector.tensor_reduce(low[:, :], ex[:, :, :], AX.X, ALU.add))
                link(nc.vector.reciprocal(low[:, :], low[:, :]))
                link(nc.vector.tensor_tensor(dense[:, :, :], ex[:, :, :], per_e(low), ALU.mult))
                for j in range(2):
                    link(nc.vector.tensor_scalar(pick[:, :, j, :], rank[:, :, :], float(j), None, ALU.is_equal))
                    link(nc.vector.tensor_tensor(pickw[:, :, j, :], pick[:, :, j, :], dense[:, :, :], ALU.mult))


def phase_ffn0(nc, d, route):
    pick, pickw, dense = route
    with ExitStack() as ctx:
        sb = lambda name, shape: ctx.enter_context(nc.sbuf_tensor("b_" + name, shape, F32))
        sem = lambda name: ctx.enter_context(nc.semaphore("b_" + name))
        banks = [ctx.enter_context(nc.psum_tensor(f"b_ps{i}", [128, CH], F32)) for i in range(8)]
        ones, wq = sb("ones", [128, 128]), sb("wq", [128, 3, 128])
        w1, w2 = sb("w1", [128, E, F0]), sb("w2", [128, E, F0])
        b1, b2, gb = sb("b1", [128, E, 2]), sb("b2", [128, E]), sb("gb", [128, 2])
        w1s, w2s, b1s, b2s = sb("w1s", [128, 2, F0]), sb("w2s", [128, 2, F0]), sb("b1s", [128, 2, 2]), sb("b2s", [128, 1])
        X, TN, Z = sb("X", [128, HW]), sb("TN", [128, HW]), sb("Z", [128, HW])
        hid = [[sb(f"hid{k}{i}", [128, CH]) for i in range(4)] for k in range(2)]
        qkv = [sb(f"qkv{k}", [128, 3, CH]) for k in range(2)]
        eps_c, eps_t = sb("eps_c", [128, 1]), sb("eps_t", [128, 1])
        norm = Norm(nc, ctx, "b_norm", ones, [banks[i][:, :] for i in range(4)])
        const_loaded, set_done, xt_loaded, x2_stored = [sem(n) for n in ("const_loaded", "set_done", "xt_loaded", "x2_stored")]
        qkv_stored = [sem(f"qkv_stored{k}") for k in range(2)]
        chosen, hid_pe, hid_done, y_pe, z_done = [sem(n) for n in ("chosen", "hid_pe", "hid_done", "y_pe", "z_done")]
        affine_done, x2_done, qkv_pe, qkv_act, qkv_dve = [sem(n) for n in ("affine_done", "x2_done", "qkv_pe", "qkv_act", "qkv_dve")]
        consts = [(ones[:, :], "ones"), (wq[:, :, :], "wq"), (w1[:, :, :], "w1"), (w2[:, :, :], "w2"), (b1[:, :, :], "b1"),
                  (b2[:, :], "b2"), (gb[:, :], "gb")]
        passed = passing(sem("passed"))
        CHOICES = 2 * 3 * E + E
        qkv_bank = lambda k, j: banks[(5, 1)[k] + j][:, :]

        with nc.Block() as block:
            @block.sync
            def _(sp):
                for dst, name in consts:
                    sp.dma_start(dst, d[name]).then_inc(const_loaded, 16)
                sp.sem_inc(x2_stored, 16)
                sp.sem_inc(qkv_stored[0], 16)
                sp.sem_inc(qkv_stored[1], 16)
                with sp.Fori(0, B) as b:
                    sp.wait_ge(x2_stored, b * 16 + 16)
                    sp.dma_start(X[:, :], d["x1"][bass.ds(b, 1), :, :].rearrange("a p n -> p (a n)")).then_inc(xt_loaded, 16)
                    sp.wait_ge(qkv_pe, b * NCH + 1)
                    sp.dma_start(TN[:, :], d["tn"][bass.ds(b, 1), :, :].rearrange("a p n -> p (a n)")).then_inc(xt_loaded, 16)
                    sp.wait_ge(x2_done, b * NCH + NCH)
                    sp.dma_start(d["x2"][bass.ds(b, 1), :, :].rearrange("a p n -> p (a n)"), X[:, :]).then_inc(x2_stored, 16)
                    with sp.Fori(0, NCH // 2) as p:
                        for k in range(2):
                            n = b * NCH + p * 2 + k
                            sp.wait_ge(qkv_act, n + 3)
                            sp.wait_ge(qkv_dve, n + 3)
                            dst = d["qkv"][bass.ds(b, 1), :, :, bass.ds((p * 2 + k) * CH, CH)].rearrange("a j c n -> c (a j) n")
                            sp.dma_start(dst, qkv[k][:, :, :]).then_inc(qkv_stored[k], 16)
                sp.wait_ge(x2_stored, B * 16 + 16)
                for k in range(2):
                    sp.wait_ge(qkv_stored[k], B * NCH // 2 * 16 + 16)

            @block.tensor
            def _(pe):
                pe.sem_inc(qkv_pe, 1)
                pe.sem_inc(y_pe, 2)
                pe.wait_ge(const_loaded, 16 * len(consts))

                def up(n, src, k):
                    for i in range(4):
                        pe.wait_ge(hid_done, (n - 1) * 4 + i + 1 + 4)
                        nc.tensor.matmul(banks[i][:, :], w1s[:, i // 2, (i % 2) * 128:(i % 2) * 128 + 128], src,
                                         start=True, stop=True).then_inc(hid_pe, 1)

                def down(n, k):
                    pe.wait_ge(z_done, n + 1)
                    for i in range(4):
                        pe.wait_ge(hid_done, n * 4 + i + 1 + 4)
                        last = nc.tensor.matmul(banks[4 + k][:, :], w2s[:, i // 2, (i % 2) * 128:(i % 2) * 128 + 128], hid[k][i][:, :],
                                                start=(i == 0), stop=(i == 3))
                    last.then_inc(y_pe, 1)

                with pe.Fori(0, B) as b:
                    pe.wait_ge(xt_loaded, b * 32 + 32)
                    pe.wait_ge(chosen, b * CHOICES + CHOICES)
                    up(b * NCH, chunk(TN, 0), 0)
                    up(b * NCH + 1, chunk(TN, 1), 1)
                    down(b * NCH, 0)
                    with pe.Fori(1, NCH // 2) as p:
                        n = b * NCH + p * 2
                        up(n, chunk(TN, p * 2), 0)
                        down(n - 1, 1)
                        up(n + 1, chunk(TN, p * 2 + 1), 1)
                        down(n, 0)
                    down(b * NCH + NCH - 1, 1)
                    pe.wait_ge(z_done, b * NCH + NCH + 2)
                    passed(pe)
                    with pe.Fori(0, NCH // 2) as p:
                        norm.pair_pe(pe, b * 2 * NCH + p * 2, lambda k: chunk(Z, p * 2 + k))
                    pe.wait_ge(x2_done, b * NCH + NCH)
                    passed(pe)
                    with pe.Fori(0, NCH // 2) as p:
                        norm.pair_pe(pe, b * 2 * NCH + NCH + p * 2, lambda k: chunk(X, p * 2 + k))
                    pe.wait_ge(norm.out_done, b * 2 * NCH + 2 * NCH + 2)
                    passed(pe)
                    with pe.Fori(0, NCH // 2) as p:
                        for k in range(2):
                            n = b * NCH + p * 2 + k
                            pe.wait_ge(qkv_act, n + 1)
                            pe.wait_ge(qkv_dve, n + 1)
                            for j in range(3):
                                last = nc.tensor.matmul(qkv_bank(k, j), wq[:, j, :], chunk(TN, p * 2 + k), start=True, stop=True)
                            last.then_inc(qkv_pe, 1)
                    pe.wait_ge(qkv_act, b * NCH + NCH + 2)
                    pe.wait_ge(qkv_dve, b * NCH + NCH + 2)

            @block.scalar
            def _(act):
                act.sem_inc(hid_done, 4)
                act.sem_inc(qkv_act, 2)
                act.wait_ge(set_done, 2)
                with act.Fori(0, B) as b:
                    with act.Fori(0, NCH // 2) as p:
                        for k in range(2):
                            n = b * NCH + p * 2 + k
                            act.wait_ge(y_pe, n + 1)
                            for i in range(4):
                                act.wait_ge(hid_pe, n * 4 + i + 1)
                                nc.scalar.activation(hid[k][i][:, :], banks[i][:, :], ACT.Gelu,
                                                     bias=b1s[:, i // 2, i % 2:i % 2 + 1]).then_inc(hid_done, 1)
                    with act.Fori(0, NCH // 2) as p:
                        norm.pair_act(act, b * 2 * NCH + p * 2, eps_t[:, :])
                    with act.Fori(0, NCH) as c:
                        act.wait_ge(norm.out_done, b * 2 * NCH + c + 3)
                        nc.scalar.activation(chunk(Z, c), chunk(Z, c), ACT.Identity, bias=gb[:, 1:2], scale=gb[:, 0:1]).then_inc(affine_done, 1)
                    with act.Fori(0, NCH // 2) as p:
                        norm.pair_act(act, b * 2 * NCH + NCH + p * 2, eps_c[:, :])
                    with act.Fori(0, NCH // 2) as p:
                        for k in range(2):
                            n = b * NCH + p * 2 + k
                            act.wait_ge(qkv_pe, n + 2)
                            act.wait_ge(qkv_stored[k], (b * (NCH // 2) + p) * 16 + 16)
                            nc.scalar.activation(qkv[k][:, 0, :], qkv_bank(k, 0), ACT.Copy)
                            nc.scalar.activation(qkv[k][:, 1, :], qkv_bank(k, 1), ACT.Copy).then_inc(qkv_act, 1)

            @block.gpsimd
            def _(pool):
                pool.wait_ge(const_loaded, 16 * len(consts))
                with pool.Fori(0, B) as b:
                    with pool.Fori(0, NCH) as c:
                        pool.wait_ge(affine_done, b * NCH + c + 1)
                        nc.gpsimd.tensor_tensor(chunk(X, c), chunk(X, c), chunk(Z, c), ALU.add).then_inc(x2_done, 1)

            @block.vector
            def _(dve):
                nc.vector.memset(eps_c[:, :], EPS_C).then_inc(set_done, 1)
                nc.vector.memset(eps_t[:, :], EPS_T).then_inc(set_done, 1)
                norm.start(dve)
                dve.sem_inc(z_done, 2)
                dve.sem_inc(qkv_dve, 2)
                dve.wait_ge(const_loaded, 16 * len(consts))
                picks = pick[:, :, :, :].rearrange("p b j e -> p (b j e)")
                pickws = pickw[:, :, :, :].rearrange("p b j e -> p (b j e)")
                denses = dense[:, :, :].rearrange("p b e -> p (b e)")
                with dve.Fori(0, B) as b:
                    dve.wait_ge(y_pe, b * NCH + 2)
                    for e in range(E):
                        if e:
                            dve.wait_ge(chosen, b * CHOICES + 7 * e)
                        for j in range(2):
                            for dst, src, by in ((w1s[:, j, :], w1[:, e, :], picks), (w2s[:, j, :], w2[:, e, :], pickws),
                                                 (b1s[:, j, :], b1[:, e, :], picks)):
                                f = by[:, bass.ds(b * 2 * E + j * E + e, 1)]
                                if e:
                                    nc.vector.scalar_tensor_tensor(out=dst, in0=src, scalar=f, in1=dst, op0=ALU.mult, op1=ALU.add).then_inc(chosen, 1)
                                else:
                                    nc.vector.tensor_scalar(dst, src, f, None, ALU.mult).then_inc(chosen, 1)
                        f = denses[:, bass.ds(b * E + e, 1)]
                        if e:
                            nc.vector.scalar_tensor_tensor(out=b2s[:, :], in0=b2[:, e:e + 1], scalar=f, in1=b2s[:, :],
                                                           op0=ALU.mult, op1=ALU.add).then_inc(chosen, 1)
                        else:
                            nc.vector.tensor_scalar(b2s[:, :], b2[:, 0:1], f, None, ALU.mult).then_inc(chosen, 1)
                    dve.wait_ge(chosen, b * CHOICES + CHOICES)
                    dve.wait_ge(xt_loaded, b * 32 + 32)
                    passed(dve)
                    with dve.Fori(0, NCH // 2) as p:
                        for k in range(2):
                            n = b * NCH + p * 2 + k
                            dve.wait_ge(y_pe, n + 3)
                            nc.vector.scalar_tensor_tensor(out=chunk(Z, p * 2 + k), in0=banks[4 + k][:, :], scalar=b2s[:, :],
                                                           in1=chunk(TN, p * 2 + k), op0=ALU.add, op1=ALU.add).then_inc(z_done, 1)
                    dve.wait_ge(z_done, b * NCH + NCH + 2)
                    passed(dve)
                    with dve.Fori(0, NCH // 2) as p:
                        norm.pair_dve(dve, b * 2 * NCH + p * 2, lambda k: chunk(Z, p * 2 + k), lambda k: chunk(Z, p * 2 + k))
                    dve.wait_ge(x2_done, b * NCH + NCH)
                    passed(dve)
                    with dve.Fori(0, NCH // 2) as p:
                        norm.pair_dve(dve, b * 2 * NCH + NCH + p * 2, lambda k: chunk(X, p * 2 + k), lambda k: chunk(TN, p * 2 + k))
                    with dve.Fori(0, NCH // 2) as p:
                        for k in range(2):
                            n = b * NCH + p * 2 + k
                            dve.wait_ge(qkv_pe, n + 2)
                            dve.wait_ge(qkv_stored[k], (b * (NCH // 2) + p) * 16 + 16)
                            nc.vector.tensor_copy(qkv[k][:, 2, :], qkv_bank(k, 2)).then_inc(qkv_dve, 1)


def phase_conv(nc, d):
    N_IN, N_OUT = HB * SIDE, (HB + 1) * SIDE
    SPANS = [(0, ROWS), (ROWS, ROWS), (2 * ROWS, 1)]
    with ExitStack() as ctx:
        sb = lambda name, shape, dt=F32: ctx.enter_context(nc.sbuf_tensor("c_" + name, shape, dt))
        sem = lambda name: ctx.enter_context(nc.semaphore("c_" + name))
        banks = [ctx.enter_context(nc.psum_tensor(f"c_ps{i}", [128, CH], F32)) for i in range(6)]
        pw, dw = sb("pw", [128, GROUPS, GC]), sb("dw", [128, GROUPS, TAPS * PH])
        prod = sb("prod", [128, TAPS * PH, GC])
        w_hi = [sb(f"w_hi{k}", [128, TAPS, 128], F32R) for k in range(2)]
        w_lo = [sb(f"w_lo{k}", [128, TAPS, 128], F32R) for k in range(2)]
        P = [sb(f"P{k}", [128, N_IN]) for k in range(2)]
        p_hi = [sb(f"p_hi{k}", [128, HB + 2, PADW], F32R) for k in range(2)]
        p_lo = [sb(f"p_lo{k}", [128, HB + 2, PADW], F32R) for k in range(2)]
        out = [sb(f"out{k}", [128, N_OUT]) for k in range(2)]
        const_loaded, cleared, prod_done, whi_done, wlo_done = [sem(n) for n in
            ("const_loaded", "cleared", "prod_done", "whi_done", "wlo_done")]
        hi_done, lo_done, span_pe, out_done = [sem(n) for n in ("hi_done", "lo_done", "span_pe", "out_done")]
        loaded = [sem(f"loaded{k}") for k in range(2)]
        stored = [sem(f"stored{k}") for k in range(2)]
        passed = passing(sem("passed"))
        flat = lambda t: t[:, :, :].rearrange("p a b -> p (a b)")
        inner = lambda t: t[:, 1:1 + HB, 2:2 + SIDE]
        rows_of = lambda t: t[:, :].rearrange("p (h w) -> p h w", w=SIDE)

        with nc.Block() as block:
            @block.sync
            def _(sp):
                sp.dma_start(pw[:, :, :], d["pw"]).then_inc(const_loaded, 16)
                sp.dma_start(dw[:, :, :], d["dw"]).then_inc(const_loaded, 16)
                by_phase = lambda name: d[name].rearrange("b j c (r n) -> (b j c) r n", r=PH)
                for k in range(2):
                    sp.sem_inc(stored[k], 64)

                def first_row(n):
                    return (n % B) * 3 * C + (n // B) * GC

                def load(n, k):
                    sp.wait_ge(lo_done, n + 1)
                    for r in range(PH):
                        sp.dma_start(P[k][r * GC:(r + 1) * GC, :], by_phase("qkv")[bass.ds(first_row(n), GC), r, :]).then_inc(loaded[k], 16)

                def store(n, k):
                    sp.wait_ge(out_done, n * 3 + 3 + 6)
                    for f in range(PH):
                        skip = SIDE if f >= 2 else 0
                        sp.dma_start(by_phase("agg")[bass.ds(first_row(n), GC), f, :],
                                     out[k][f * GC:(f + 1) * GC, skip:skip + HB * SIDE]).then_inc(stored[k], 16)

                U = GROUPS * B // 2
                load(0, 0)
                load(1, 1)
                with sp.Fori(0, U - 1) as u:
                    for k in range(2):
                        store(u * 2 + k, k)
                        load(u * 2 + k + 2, k)
                for k in range(2):
                    store(2 * U - 2 + k, k)
                for k in range(2):
                    sp.wait_ge(stored[k], U * 64 + 64)

            @block.scalar
            def _(act):
                act.wait_ge(cleared, 4)
                with act.Fori(0, GROUPS * B // 2) as u:
                    for k in range(2):
                        act.wait_ge(loaded[k], u * 64 + 64)
                        act.wait_ge(span_pe, (u * 2 + k) * 3 + 3)
                        nc.scalar.activation(inner(p_hi[k]), rows_of(P[k]), ACT.Copy).then_inc(hi_done, 1)

            @block.gpsimd
            def _(pool):
                for k in range(2):
                    nc.gpsimd.memset(p_hi[k][:, :, :].bitcast(F32), 0.0).then_inc(cleared, 1)
                    nc.gpsimd.memset(p_lo[k][:, :, :].bitcast(F32), 0.0).then_inc(cleared, 1)
                pool.wait_ge(const_loaded, 32)

                def weights(g, k):
                    taps = dw[:, bass.ds(g, 1), :].rearrange("p a t -> p (a t)").unsqueeze(2).broadcast_to([128, TAPS * PH, GC])
                    mix = pw[:, bass.ds(g, 1), :].broadcast_to([128, TAPS * PH, GC])
                    if not isinstance(g, int) or g:
                        pool.wait_ge(span_pe, (g - 1) * B * 3 + 6)
                    nc.gpsimd.tensor_tensor(prod[:, :, :], taps, mix, ALU.mult).then_inc(prod_done, 1)
                    pool.wait_ge(prod_done, g + 1)
                    passed(pool)
                    nc.gpsimd.tensor_copy(flat(w_hi[k]), flat(prod)).then_inc(whi_done, 1)
                    pool.wait_ge(whi_done, g + 1)
                    nc.gpsimd.tensor_tensor(flat(w_lo[k]), flat(prod), flat(w_hi[k]).bitcast(F32), ALU.subtract).then_inc(wlo_done, 1)
                    pool.wait_ge(wlo_done, g + 1)

                weights(0, 0)
                weights(1, 1)
                with pool.Fori(1, GROUPS // 2) as gg:
                    for k in range(2):
                        weights(gg * 2 + k, k)

            @block.tensor
            def _(pe):
                pe.sem_inc(span_pe, 6)
                with pe.Fori(0, GROUPS // 2) as gg:
                    for gk in range(2):
                        g = gg * 2 + gk
                        pe.wait_ge(wlo_done, g + 1)
                        passed(pe)
                        with pe.Fori(0, B // 2) as h:
                            for k in range(2):
                                n = g * B + h * 2 + k
                                pe.wait_ge(lo_done, n + 3)
                                for q, (s0, ns) in enumerate(SPANS):
                                    pe.wait_ge(out_done, n * 3 + q + 1)
                                    i = 0
                                    for wt, src in ((w_hi, p_hi), (w_hi, p_lo), (w_lo, p_hi)):
                                        for t in range(TAPS):
                                            s, x = s0 + t // 5, t % 5
                                            last = nc.tensor.matmul(banks[3 * k + q][:, 0:ns * SIDE], wt[gk][:, t, :],
                                                                    src[k][:, s:s + ns, x:x + SIDE],
                                                                    start=(i == 0), stop=(i == 3 * TAPS - 1))
                                            i += 1
                                    last.then_inc(span_pe, 1)

            @block.vector
            def _(dve):
                dve.sem_inc(lo_done, 2)
                dve.sem_inc(out_done, 6)

                def low(n, k):
                    dve.wait_ge(hi_done, n + 1)
                    nc.vector.tensor_tensor(inner(p_lo[k]), rows_of(P[k]), inner(p_hi[k]).bitcast(F32), ALU.subtract).then_inc(lo_done, 1)

                def read(n, u, k):
                    dve.wait_ge(stored[k], u * 64 + 64)
                    for q, (s0, ns) in enumerate(SPANS):
                        dve.wait_ge(span_pe, n * 3 + q + 1 + 6)
                        nc.vector.tensor_copy(out[k][:, s0 * SIDE:(s0 + ns) * SIDE], banks[3 * k + q][:, 0:ns * SIDE]).then_inc(out_done, 1)

                U = GROUPS * B // 2
                low(0, 0)
                with dve.Fori(0, U - 1) as u:
                    low(u * 2 + 1, 1)
                    read(u * 2, u, 0)
                    low(u * 2 + 2, 0)
                    read(u * 2 + 1, u, 1)
                low(2 * U - 1, 1)
                read(2 * U - 2, U - 1, 0)
                read(2 * U - 1, U - 1, 1)


def phase_attention(nc, d):
    TPC = CH // 128
    NT = HW // 128
    with ExitStack() as ctx:
        sb = lambda name, shape, dt=F32: ctx.enter_context(nc.sbuf_tensor("d_" + name, shape, dt))
        two = lambda name, shape, dt=F32: [sb(f"{name}{k}", shape, dt) for k in range(2)]
        sem = lambda name: ctx.enter_context(nc.semaphore("d_" + name))
        ps = ctx.enter_context(nc.psum_tensor("d_ps", [128, 8 * CH], F32))
        bank = lambda i: ps[:, i * CH:(i + 1) * CH]
        ones, ident, heads = sb("ones", [128, 128]), sb("ident", [128, 128]), sb("heads", [128, 128])
        ident_bf = sb("ident_bf", [128, 128], BF16)
        wp, bn, bnv = sb("wp", [128, 2, 128]), sb("bn", [128, 4]), sb("bnv", [128, 4])
        wr, before = sb("wr", [128, E]), sb("before", [128, E * E])
        w1, w2, b1 = sb("w1", [128, E, 128]), sb("w2", [128, E, 128]), sb("b1", [128, E])
        b2, b2r = sb("b2", [3 * E, 128]), sb("b2r", [3 * E, 128])
        b2s = sb("b2s", [3 * E, 3, 128], BF16)
        spread, spread_bf = sb("spread", [3 * E, E * 128]), sb("spread_bf", [3 * E, E, 128], BF16)
        X, TN = sb("X", [128, HW]), sb("TN", [128, HW])
        kc, vc = two("kc", [128, CH]), two("vc", [128, CH])
        qc = [two(f"qc{s}", [128, CH]) for s in range(2)]
        qr = [two(f"qr{s}", [128, CH]) for s in range(2)]
        kt, vt = two("kt", [128, TPC, 128]), two("vt", [128, TPC, 132])
        kv = sb("kv", [128, 129])
        num_w, den_w = two("num_w", [128, 128]), two("den_w", [128, 128])
        den, rec, att = two("den", [128, CH]), two("rec", [128, CH]), [two(f"att{s}", [128, CH]) for s in range(2)]
        fix = two("fix", [128, CH])
        prob, comb, rest, exl = [sb(n, [128, NT, E]) for n in ("prob", "comb", "rest", "exl")]
        top, tot = sb("top", [128, NT]), sb("tot", [128, NT])
        more, same = sb("more", [128, NT, E * E]), sb("same", [128, NT, E * E])
        parts, parts_t = sb("parts", [128, NT, 3 * E], BF16), sb("parts_t", [3 * E, HW], BF16)
        hid, scaled = two("hid", [128, CH]), two("scaled", [128, CH])
        eps_t, eps_a = sb("eps_t", [128, 1]), sb("eps_a", [128, 1])
        norm = Norm(nc, ctx, "d_norm", ones, [bank(i) for i in range(4)])
        const_loaded, set_done, own, small_ready, bn_in, bn_act = [sem(n) for n in
            ("const_loaded", "set_done", "own", "small_ready", "bn_in", "bn_act")]
        x2_loaded, out_stored = sem("x2_loaded"), sem("out_stored")
        kv_loaded, q_loaded = [sem(f"kv_loaded{k}") for k in range(2)], [sem(f"q_loaded{k}") for k in range(2)]
        turn_pe, kt_done, vt_done, kv_pe, kv_added, kv_zero, kv_ready = [sem(n) for n in
            ("turn_pe", "kt_done", "vt_done", "kv_pe", "kv_added", "kv_zero", "kv_ready")]
        qr_done, nd_pe, den_done, rec_done, att_done, y_pe, fix_done, x3_done = [sem(n) for n in
            ("qr_done", "nd_pe", "den_done", "rec_done", "att_done", "y_pe", "fix_done", "x3_done")]
        logit_pe, exp_in, exp_done, parts_done, parts_pe, parts_t_done = [sem(n) for n in
            ("logit_pe", "exp_in", "exp_done", "parts_done", "parts_pe", "parts_t_done")]
        up_pe, spread_pe, hid_done, scaled_done, moe_pe, fin_done, out_done = [sem(n) for n in
            ("up_pe", "spread_pe", "hid_done", "scaled_done", "moe_pe", "fin_done", "out_done")]
        consts = [(ones[:, :], "ones"), (ident[:, :], "ident"), (heads[:, :], "heads"), (wp[:, :, :], "wp"), (bn[:, :], "bn"),
                  (wr[:, :], "wr1"), (before[:, :], "before"), (w1[:, :, :], "m1"), (w2[:, :, :], "m2"), (b1[:, :], "mb1"),
                  (b2[:, :], "mb2"), (spread[:, :], "spread")]
        passed = passing(sem("passed"))
        LINKS = 20
        turned = ps[0:3 * E, 0:HW // 2].bitcast(BF16)

        with nc.Block() as block:
            @block.sync
            def _(sp):
                for dst, name in consts:
                    sp.dma_start(dst, d[name]).then_inc(const_loaded, 16)
                sp.sem_inc(out_stored, 16)

                def load(dst, b, j, s, c, sm):
                    src = d["agg"] if s else d["qkv"]
                    sp.dma_start(dst[:, :], src[bass.ds(b, 1), j, :, bass.ds(c * CH, CH)].rearrange("a c n -> c (a n)")).then_inc(sm, 16)

                with sp.Fori(0, B) as b:
                    sp.wait_ge(out_stored, b * 16 + 16)
                    sp.dma_start(X[:, :], d["x2"][bass.ds(b, 1), :, :].rearrange("a p n -> p (a n)")).then_inc(x2_loaded, 16)
                    for s in range(2):
                        with sp.Fori(0, NCH // 2) as p:
                            for k in range(2):
                                sp.wait_ge(turn_pe, b * 2 * NCH + s * NCH + p * 2 + k + 1)
                                load(kc[k], b, 1, s, p * 2 + k, kv_loaded[k])
                                load(vc[k], b, 2, s, p * 2 + k, kv_loaded[k])
                    with sp.Fori(0, NCH // 2) as p:
                        for k in range(2):
                            sp.wait_ge(qr_done, (b * NCH + p * 2 + k) * 2 + 1 + 1)
                            for s in range(2):
                                load(qc[s][k], b, 0, s, p * 2 + k, q_loaded[k])
                    sp.wait_ge(out_done, b * NCH + NCH + 2)
                    sp.dma_start(d["out"][bass.ds(b, 1), :, :].rearrange("a p n -> p (a n)"), X[:, :]).then_inc(out_stored, 16)
                sp.wait_ge(out_stored, B * 16 + 16)

            @block.tensor
            def _(pe):
                pe.sem_inc(turn_pe, 2)
                pe.sem_inc(nd_pe, 4)
                pe.sem_inc(kv_pe, 2)
                pe.sem_inc(y_pe, 2)
                pe.sem_inc(moe_pe, 2)
                pe.wait_ge(const_loaded, 16 * len(consts))
                pe.wait_ge(small_ready, 1)
                passed(pe)
                with pe.Fori(0, B) as b:
                    for s in range(2):
                        with pe.Fori(0, NCH // 2) as p:
                            n0 = b * 2 * NCH + s * NCH + p * 2
                            for k in range(2):
                                pe.wait_ge(kv_loaded[k], (b * NCH + s * (NCH // 2) + p) * 32 + 32)
                                pe.wait_ge(kt_done, n0 + k + 1)
                                pe.wait_ge(vt_done, n0 + k + 1)
                                for t in range(TPC):
                                    nc.tensor.transpose(bank(k)[:, t * 128:(t + 1) * 128], kc[k][:, t * 128:(t + 1) * 128], ident[:, :])
                                    last = nc.tensor.transpose(bank(2 + k)[:, t * 128:(t + 1) * 128], vc[k][:, t * 128:(t + 1) * 128],
                                                               ident[:, :])
                                last.then_inc(turn_pe, 1)
                            for k in range(2):
                                pe.wait_ge(kt_done, n0 + k + 3)
                                pe.wait_ge(vt_done, n0 + k + 3)
                                pe.wait_ge(kv_added, n0 + k + 1)
                                for t in range(TPC):
                                    last = nc.tensor.matmul(bank(4 + k)[:, 0:129], kt[k][:, t, :], vt[k][:, t, 0:129],
                                                            start=(t == 0), stop=(t == TPC - 1))
                                last.then_inc(kv_pe, 1)
                    pe.wait_ge(kv_ready, b * 2 + 3)
                    passed(pe)
                    with pe.Fori(0, NCH // 2) as p:
                        n0 = b * NCH + p * 2
                        for k in range(2):
                            for s in range(2):
                                u = (n0 + k) * 2 + s
                                pe.wait_ge(qr_done, u + 1 + 4)
                                pe.wait_ge(att_done, u + 1)
                                nc.tensor.matmul(bank(s), num_w[s][:, :], qr[s][k][:, :], start=True, stop=True)
                                nc.tensor.matmul(bank(2 + s), den_w[s][:, :], qr[s][k][:, :], start=True, stop=True).then_inc(nd_pe, 1)
                        for k in range(2):
                            pe.wait_ge(att_done, (n0 + k) * 2 + 2 + 2)
                            pe.wait_ge(fix_done, n0 + k + 1)
                            for s in range(2):
                                last = nc.tensor.matmul(bank(4 + k), wp[:, s, :], att[s][k][:, :], start=(s == 0), stop=(s == 1))
                            last.then_inc(y_pe, 1)
                    pe.wait_ge(x3_done, b * NCH + NCH + 2)
                    passed(pe)
                    with pe.Fori(0, NCH // 2) as p:
                        norm.pair_pe(pe, b * NCH + p * 2, lambda k: chunk(X, p * 2 + k))
                    pe.wait_ge(norm.out_done, b * NCH + NCH + 2)
                    for t in range(NT):
                        last = nc.tensor.matmul(bank(6)[:, t * E:(t + 1) * E], TN[:, t * 128:(t + 1) * 128], wr[:, :], start=True, stop=True)
                    last.then_inc(logit_pe, 1)
                    pe.wait_ge(parts_done, b + 1)
                    for t in range(NT):
                        last = nc.tensor.transpose(turned[:, t * 128:(t + 1) * 128], parts[:, t, :], ident_bf[:, :])
                    last.then_inc(parts_pe, 1)
                    pe.wait_ge(parts_t_done, b + 1)
                    passed(pe)
                    with pe.Fori(0, NCH // 2) as p:
                        c0 = b * NCH + p * 2

                        def up(i):
                            k, e = i // E, i % E
                            pe.wait_ge(scaled_done, c0 * E + i + 1)
                            passed(pe)
                            nc.tensor.matmul(bank(2 + i % 2), spread_bf[:, e, :], chunk(parts_t, p * 2 + k), start=True, stop=True).then_inc(spread_pe, 1)
                            pe.wait_ge(hid_done, c0 * E + i + 1)
                            nc.tensor.matmul(bank(i % 2), w1[:, e, :], chunk(TN, p * 2 + k), start=True, stop=True).then_inc(up_pe, 1)

                        def down(i):
                            k, e = i // E, i % E
                            if e == 0:
                                pe.wait_ge(fin_done, c0 + k + 1)
                                passed(pe)
                                for j in range(3):
                                    nc.tensor.matmul(bank(4 + k), b2s[:, j, :], chunk(parts_t, p * 2 + k), start=(j == 0), stop=False)
                            pe.wait_ge(scaled_done, c0 * E + i + 3)
                            last = nc.tensor.matmul(bank(4 + k), w2[:, e, :], scaled[i % 2][:, :], start=False, stop=(e == E - 1))
                            last.then_inc(moe_pe, 1)

                        for i in range(2 * E):
                            up(i)
                            if i:
                                down(i - 1)
                        down(2 * E - 1)
                    pe.wait_ge(hid_done, (b + 1) * NCH * E + 2)
                    pe.wait_ge(scaled_done, (b + 1) * NCH * E + 2)
                    pe.wait_ge(fin_done, (b + 1) * NCH + 2)

            @block.scalar
            def _(act):
                act.sem_inc(kt_done, 2)
                act.sem_inc(qr_done, 4)
                act.sem_inc(fix_done, 2)
                act.sem_inc(hid_done, 2)
                act.wait_ge(bn_in, 1)
                nc.scalar.activation(bnv[:, 0:1], bn[:, 3:4], ACT.Sqrt, bias=eps_t[:, :]).then_inc(bn_act, 1)
                act.wait_ge(small_ready, 1)
                with act.Fori(0, B) as b:
                    with act.Fori(0, NCH) as p:
                        for k in range(2):
                            n = b * 2 * NCH + p * 2 + k
                            act.wait_ge(turn_pe, n + 3)
                            act.wait_ge(kv_pe, n + 1)
                            nc.scalar.activation(kt[k][:, :, :].rearrange("p t c -> p (t c)"), bank(k), ACT.Relu).then_inc(kt_done, 1)
                    with act.Fori(0, NCH // 2) as p:
                        for k in range(2):
                            act.wait_ge(q_loaded[k], (b * (NCH // 2) + p) * 32 + 32)
                            for s in range(2):
                                u = (b * NCH + p * 2 + k) * 2 + s
                                act.wait_ge(nd_pe, u + 1)
                                nc.scalar.activation(qr[s][k][:, :], qc[s][k][:, :], ACT.Relu).then_inc(qr_done, 1)
                        for k in range(2):
                            for s in range(2):
                                u = (b * NCH + p * 2 + k) * 2 + s
                                act.wait_ge(nd_pe, u + 1 + 4)
                                act.wait_ge(rec_done, u + 1)
                                nc.scalar.activation(den[s][:, :], bank(2 + s), ACT.Identity, bias=eps_a[:, :]).then_inc(den_done, 1)
                        for k in range(2):
                            n = b * NCH + p * 2 + k
                            act.wait_ge(y_pe, n + 3)
                            act.wait_ge(x3_done, n + 1)
                            nc.scalar.activation(fix[k][:, :], bank(4 + k), ACT.Identity, bias=bnv[:, 3:4], scale=bnv[:, 1:2]).then_inc(fix_done, 1)
                    with act.Fori(0, NCH // 2) as p:
                        norm.pair_act(act, b * NCH + p * 2, eps_t[:, :])
                    act.wait_ge(exp_in, b + 1)
                    nc.scalar.activation(exl[:, :, :], exl[:, :, :], ACT.Exp).then_inc(exp_done, 1)
                    with act.Fori(0, NCH) as c:
                        for e in range(E):
                            u = (b * NCH + c) * E + e
                            act.wait_ge(up_pe, u + 1)
                            act.wait_ge(scaled_done, u + 1)
                            nc.scalar.activation(hid[e % 2][:, :], bank(e % 2), ACT.Gelu, bias=b1[:, e:e + 1]).then_inc(hid_done, 1)

            @block.gpsimd
            def _(pool):
                pool.wait_ge(const_loaded, 16 * len(consts))
                pool.sem_inc(x3_done, 2)
                pool.sem_inc(out_done, 2)
                with pool.Fori(0, B) as b:
                    pool.wait_ge(x2_loaded, b * 16 + 16)
                    passed(pool)
                    with pool.Fori(0, NCH // 2) as p:
                        for k in range(2):
                            pool.wait_ge(fix_done, b * NCH + p * 2 + k + 3)
                            nc.gpsimd.tensor_tensor(chunk(X, p * 2 + k), chunk(X, p * 2 + k), fix[k][:, :], ALU.add).then_inc(x3_done, 1)
                    with pool.Fori(0, NCH // 2) as p:
                        for k in range(2):
                            pool.wait_ge(fin_done, b * NCH + p * 2 + k + 3)
                            nc.gpsimd.tensor_tensor(chunk(X, p * 2 + k), chunk(X, p * 2 + k), fix[k][:, :], ALU.add).then_inc(out_done, 1)

            @block.vector
            def _(dve):
                norm.start(dve)
                for sm in (vt_done, kv_added, rec_done, att_done, scaled_done, fin_done):
                    dve.sem_inc(sm, 2)
                dve.sem_inc(kv_ready, 1)
                setup = Chain(dve, set_done)
                setup(nc.vector.memset(eps_t[:, :], EPS_T))
                setup(nc.vector.memset(eps_a[:, :], EPS_ATT))
                for k in range(2):
                    setup(nc.vector.memset(vt[k][:, :, :], 1.0))
                dve.wait_ge(const_loaded, 16 * len(consts))
                dve.sem_inc(bn_in, 1)
                setup(nc.vector.tensor_copy(ident_bf[:, :], ident[:, :]))
                setup(nc.vector.tensor_copy(spread_bf[:, :, :].rearrange("p e c -> p (e c)"), spread[:, :]))
                setup(nc.vector.tensor_copy(b2s[:, 0, :], b2[:, :]))
                setup(nc.vector.tensor_tensor(b2r[:, :], b2[:, :], b2s[:, 0, :], ALU.subtract))
                setup(nc.vector.tensor_copy(b2s[:, 1, :], b2r[:, :]))
                setup(nc.vector.tensor_tensor(b2r[:, :], b2r[:, :], b2s[:, 1, :], ALU.subtract))
                setup(nc.vector.tensor_copy(b2s[:, 2, :], b2r[:, :]))
                dve.wait_ge(bn_act, 1)
                setup(nc.vector.reciprocal(bnv[:, 2:3], bnv[:, 0:1]))
                setup(nc.vector.tensor_tensor(bnv[:, 1:2], bn[:, 0:1], bnv[:, 2:3], ALU.mult))
                setup(nc.vector.tensor_tensor(bnv[:, 2:3], bn[:, 2:3], bnv[:, 1:2], ALU.mult))
                setup(nc.vector.tensor_tensor(bnv[:, 3:4], bn[:, 1:2], bnv[:, 2:3], ALU.subtract))
                dve.sem_inc(small_ready, 1)
                with dve.Fori(0, B) as b:
                    for s in range(2):
                        dve.wait_ge(kv_ready, b * 2 + s + 1)
                        nc.vector.memset(kv[:, :], 0.0).then_inc(kv_zero, 1)
                        dve.wait_ge(kv_zero, b * 2 + s + 1)
                        passed(dve)
                        with dve.Fori(0, NCH // 2) as p:
                            n0 = b * 2 * NCH + s * NCH + p * 2
                            for k in range(2):
                                dve.wait_ge(turn_pe, n0 + k + 3)
                                dve.wait_ge(kv_pe, n0 + k + 1)
                                nc.vector.tensor_copy(vt[k][:, :, 0:128], bank(2 + k).rearrange("p (t c) -> p t c", c=128)).then_inc(vt_done, 1)
                            for k in range(2):
                                dve.wait_ge(kv_pe, n0 + k + 3)
                                dve.wait_ge(kv_added, n0 + k + 2)
                                nc.vector.tensor_tensor(kv[:, :], bank(4 + k)[:, 0:129], kv[:, :], ALU.add).then_inc(kv_added, 1)
                        dve.wait_ge(kv_added, b * 2 * NCH + s * NCH + NCH + 2)
                        nc.vector.tensor_tensor(num_w[s][:, :], kv[:, 0:128], heads[:, :], ALU.mult)
                        nc.vector.tensor_scalar(den_w[s][:, :], heads[:, :], kv[:, 128:129], None, ALU.mult).then_inc(kv_ready, 1)
                    with dve.Fori(0, NCH // 2) as p:
                        for k in range(2):
                            n = b * NCH + p * 2 + k
                            for s in range(2):
                                u = n * 2 + s
                                dve.wait_ge(den_done, u + 1)
                                dve.wait_ge(att_done, u + 1)
                                nc.vector.reciprocal(rec[s][:, :], den[s][:, :]).then_inc(rec_done, 1)
                                dve.wait_ge(rec_done, u + 3)
                                dve.wait_ge(y_pe, n + 1)
                                nc.vector.tensor_tensor(att[s][k][:, :], bank(s), rec[s][:, :], ALU.mult).then_inc(att_done, 1)
                    dve.wait_ge(x3_done, b * NCH + NCH + 2)
                    passed(dve)
                    with dve.Fori(0, NCH // 2) as p:
                        norm.pair_dve(dve, b * NCH + p * 2, lambda k: chunk(X, p * 2 + k), lambda k: chunk(TN, p * 2 + k))
                    link = Chain(dve, own, b * LINKS)
                    dve.wait_ge(logit_pe, b + 1)
                    logits = bank(6)[:, 0:NT * E].rearrange("p (t e) -> p t e", e=E)
                    per_e = lambda t: t[:, :].unsqueeze(2).broadcast_to([128, NT, E])
                    link(nc.vector.tensor_reduce(top[:, :], logits, AX.X, ALU.max))
                    link(nc.vector.tensor_tensor(exl[:, :, :], logits, per_e(top), ALU.subtract))
                    dve.sem_inc(exp_in, 1)
                    dve.wait_ge(exp_done, b + 1)
                    link(nc.vector.tensor_reduce(tot[:, :], exl[:, :, :], AX.X, ALU.add))
                    link(nc.vector.reciprocal(tot[:, :], tot[:, :]))
                    link(nc.vector.tensor_tensor(prob[:, :, :], exl[:, :, :], per_e(tot), ALU.mult))
                    mine = prob[:, :, :].unsqueeze(3).broadcast_to([128, NT, E, E])
                    other = prob[:, :, :].unsqueeze(2).broadcast_to([128, NT, E, E])
                    grid = lambda t: t[:, :, :].rearrange("p t (e f) -> p t e f", f=E)
                    link(nc.vector.tensor_tensor(grid(more), other, mine, ALU.is_gt))
                    link(nc.vector.tensor_tensor(grid(same), other, mine, ALU.is_equal))
                    link(nc.vector.tensor_tensor(same[:, :, :], same[:, :, :], before[:, :].unsqueeze(1).broadcast_to([128, NT, E * E]), ALU.mult))
                    link(nc.vector.tensor_tensor(more[:, :, :], more[:, :, :], same[:, :, :], ALU.add))
                    link(nc.vector.tensor_reduce(rest[:, :, :], grid(more), AX.X, ALU.add))
                    link(nc.vector.scalar_tensor_tensor(out=comb[:, :, :], in0=rest[:, :, :], scalar=1.5, in1=prob[:, :, :],
                                                        op0=ALU.is_lt, op1=ALU.mult))
                    link(nc.vector.tensor_reduce(tot[:, :], comb[:, :, :], AX.X, ALU.add))
                    link(nc.vector.tensor_scalar(tot[:, :], tot[:, :], 1e-12, None, ALU.max))
                    link(nc.vector.reciprocal(tot[:, :], tot[:, :]))
                    link(nc.vector.tensor_tensor(comb[:, :, :], comb[:, :, :], per_e(tot), ALU.mult))
                    link(nc.vector.tensor_copy(parts[:, :, 0:E], comb[:, :, :]))
                    link(nc.vector.tensor_tensor(rest[:, :, :], comb[:, :, :], parts[:, :, 0:E], ALU.subtract))
                    link(nc.vector.tensor_copy(parts[:, :, E:2 * E], rest[:, :, :]))
                    link(nc.vector.tensor_tensor(rest[:, :, :], rest[:, :, :], parts[:, :, E:2 * E], ALU.subtract))
                    link(nc.vector.tensor_copy(parts[:, :, 2 * E:3 * E], rest[:, :, :]))
                    assert link.count == LINKS
                    dve.sem_inc(parts_done, 1)
                    dve.wait_ge(parts_pe, b + 1)
                    nc.vector.tensor_copy(parts_t[:, :], turned).then_inc(parts_t_done, 1)
                    with dve.Fori(0, NCH // 2) as p:
                        for k in range(2):
                            n = b * NCH + p * 2 + k
                            for e in range(E):
                                u = n * E + e
                                dve.wait_ge(hid_done, u + 3)
                                dve.wait_ge(spread_pe, u + 1)
                                dve.wait_ge(moe_pe, u + 1)
                                nc.vector.tensor_tensor(scaled[e % 2][:, :], hid[e % 2][:, :], bank(2 + e % 2), ALU.mult).then_inc(scaled_done, 1)
                            dve.wait_ge(moe_pe, n * E + E + 2)
                            dve.wait_ge(out_done, n + 1)
                            nc.vector.tensor_tensor(fix[k][:, :], bank(4 + k), chunk(TN, p * 2 + k), ALU.add).then_inc(fin_done, 1)


def build(nc, d):
    with ExitStack() as ctx:
        sb = lambda name, shape: ctx.enter_context(nc.sbuf_tensor(name, shape, F32))
        route = sb("pick", [128, B, 2, E]), sb("pickw", [128, B, 2, E]), sb("dense", [128, B, E])
        phase_spectral(nc, d)
        phase_route0(nc, d, route)
        phase_ffn0(nc, d, route)
        phase_conv(nc, d)
        phase_attention(nc, d)


def shape_constants():
    import math

    import numpy as np
    f = np.float32
    i = np.arange(SIDE)
    row = PH * (i % HB) + i // HB
    cos = lambda a, b: np.cos(2 * np.pi * np.outer(a, b) / SIDE) / 8
    sin = lambda a, b: np.sin(2 * np.pi * np.outer(a, b) / SIDE) / 8
    cat = lambda *t: np.concatenate(t, 1)
    dft = cat(cos(row, i), -sin(row, i), cos(i, i), -sin(i, i), sin(i, i), cos(i, i),
              cos(i, row), sin(i, row), -sin(i, row), cos(i, row), cos(i, i), -sin(i, i))
    y, x = (i.astype(f) - SIDE // 2)[:, None], (i.astype(f) - SIDE // 2)[None, :]
    theta = (np.arctan2(y, x).astype(f) + f(math.pi)) % f(math.pi)
    radii = SIDE // 2 // 8 + 1
    ring = np.clip(np.floor(np.sqrt(y * y + x * x) / f(8)).astype(np.int32), 0, radii - 1)
    delta = math.pi / 8
    half = 1.5 * delta / 2.0
    centers = (np.arange(8, dtype=f) * f(delta) + f(delta / 2.0))[:, None, None]
    dist = np.abs(theta[None] - centers)
    w = np.clip(f(1.0) - dist / f(half), 0, None) * (dist < f(half))
    angle = w / (w.sum(0, keepdims=True) + f(1e-8))
    mask = angle[:, None] * (ring[None, None] == np.arange(radii)[None, :, None, None])
    mask = np.roll(mask, (-(SIDE // 2), -(SIDE // 2)), (2, 3)).transpose(0, 1, 3, 2).reshape(8 * radii, HW)
    e = np.arange(E)
    c = np.arange(128)
    spread = np.tile(np.repeat(np.eye(E), 128, 1), (3, 1))
    return {"ones": np.full((128, 128), 1 / 128), "ident": np.eye(128), "dft": dft, "mask": mask,
            "before": np.tile((e[None, :] < e[:, None]).reshape(1, -1), (128, 1)),
            "heads": c[:, None] // 8 == c[None, :] // 8, "spread": spread}


def lay_out(v):
    import numpy as np
    t = lambda a: np.ascontiguousarray(a)
    a = {"x": v["x"].reshape(B, C, HB, PH, SIDE).transpose(0, 1, 3, 2, 4).reshape(B, C, HW)}
    a["w_in"], a["w_out"] = v["L0_conv_w_in"].T, v["L0_conv_w_out"].T
    a["binw"] = v["L0_conv_bin_weights"].reshape(MID, -1).T
    a["wr"], a["br"] = v["L0_ffn_Wr"], np.tile(v["L0_ffn_br"][None], (128, 1))
    a["w1"] = v["L0_ffn_W1"].transpose(1, 0, 2)
    a["w2"] = v["L0_ffn_W2"].reshape(E, 2, 128, C).transpose(2, 0, 1, 3).reshape(128, E, F0)
    a["b1"] = v["L0_ffn_b1"].reshape(E, 2, 128).transpose(2, 0, 1)
    a["b2"] = v["L0_ffn_b2"].T
    a["gb"] = np.stack([v["L0_ffn_gamma"], v["L0_ffn_beta"]], 1)
    order = (24 * np.arange(16)[None, :, None] + 8 * np.arange(3)[:, None, None] + np.arange(8)[None, None, :]).reshape(3, 128)
    a["wq"] = v["L1_conv_w_qkv"][:, :, 0, 0][order].transpose(2, 0, 1)
    flat = order.reshape(GROUPS, GC)
    wdw, wpw = v["L1_conv_w_dw"][:, 0], v["L1_conv_w_pw"][:, :, 0, 0]
    dw = np.zeros((PH, GC, GROUPS, 2, 5, PH), np.float32)
    for r in range(PH):
        for f in range(PH):
            for s in range(2):
                dy = PH * s + r - (f - 2 if f >= 2 else f + 2)
                if 0 <= dy < 5:
                    dw[r, :, :, s, :, f] = wdw[flat][:, :, dy, :].transpose(1, 0, 2)
    a["dw"] = dw.reshape(128, GROUPS, TAPS * PH)
    pw = np.zeros((GC, GROUPS, GC), np.float32)
    for ci in range(GC):
        same = np.arange(ci // 4 * 4, ci // 4 * 4 + 4)
        pw[ci][:, same] = wpw[flat[:, same], ci % 4]
    a["pw"] = np.tile(pw, (PH, 1, 1))
    a["wp"] = v["L1_conv_w_proj"][:, :, 0, 0].reshape(C, 2, 128).transpose(2, 1, 0)
    a["bn"] = np.stack([v["L1_conv_bn_" + n] for n in ("gamma", "beta", "mean", "var")], 1)
    a["wr1"] = v["L1_ffn_router_w"].T
    a["m1"], a["m2"] = v["L1_ffn_w1"].transpose(1, 0, 2), v["L1_ffn_w2"].transpose(1, 0, 2)
    a["mb1"], a["mb2"] = v["L1_ffn_b1"].T, np.tile(v["L1_ffn_b2"], (3, 1))
    return {k: t(x) for k, x in a.items()}


SCRATCH = {"xe": (MID, SIDE, SIDE), "x1": (B, C, HW), "tn": (B, C, HW), "total": (C, B), "x2": (B, C, HW),
           "qkv": (B, 3, C, HW), "agg": (B, 3, C, HW)}


def kernel(**inputs):
    import numpy as np
    import concourse.bacc as bacc
    from concourse.bass_utils import run_bass_kernel_spmd

    arrays = lay_out({k: np.asarray(x) for k, x in inputs.items()})
    arrays.update({k: np.ascontiguousarray(x, dtype=np.float32) for k, x in shape_constants().items()})
    nc = bacc.Bacc("TRN2", target_bir_lowering=False, num_devices=1)
    d = {k: nc.dram_tensor("in_" + k, x.shape, F32, kind="ExternalInput").ap() for k, x in arrays.items()}
    d.update({k: nc.dram_tensor("scratch_" + k, shape, F32, kind="Internal").ap() for k, shape in SCRATCH.items()})
    d["out"] = nc.dram_tensor("out", (B, C, HW), F32, kind="ExternalOutput").ap()
    build(nc, d)
    got = run_bass_kernel_spmd(nc, [{"in_" + k: x for k, x in arrays.items()}], core_ids=[0]).results[0]["out"]
    return got.reshape(B, C, PH, HB, SIDE).transpose(0, 1, 3, 2, 4).reshape(B, C, SIDE, SIDE)
```

```python
from contextlib import ExitStack

import concourse.bass as bass
from concourse import mybir
from concourse.alu_op_type import AluOpType as ALU

F32 = mybir.dt.float32
F32R = mybir.dt.float32r
BF16 = mybir.dt.bfloat16
ACT = mybir.ActivationFunctionType
AX = mybir.AxisListType

B, C, HW, SIDE = 8, 128, 4096, 64
MID = 16
E = 8
F0 = 256
CH = 512
NCH = HW // CH
PH = 4
HB = SIDE // PH
PADW = SIDE + 4
ROWS = CH // SIDE
GROUPS = 12
GC = 32
TAPS = 10
EPS_C, EPS_T, EPS_MAG, EPS_ATT = 1e-6, 1e-5, 1e-8, 1e-15


def chunk(buf, c):
    return buf[:, bass.ds(c * CH, CH)]


def batch_of(t, b):
    return t[bass.ds(b, 1), :, :].rearrange("a p n -> p (a n)")


class Norm:
    LOW = 32

    def __init__(self, nc, ctx, tag, ones, rows, spread, banks):
        sb = lambda name, shape, dt=F32: ctx.enter_context(nc.sbuf_tensor(f"{tag}_{name}", shape, dt))
        sem = lambda name: ctx.enter_context(nc.semaphore(f"{tag}_{name}"))
        self.nc, self.ones, self.rows, self.spread = nc, ones, rows, spread
        self.mean, self.cast, self.stat = banks[0:2], banks[2:4], banks[4][0:NCH]
        self.square = [sb(f"square{k}", [128, CH]) for k in range(2)]
        self.std, self.rstd = sb("std", [NCH, CH]), sb("rstd", [NCH, CH])
        self.parts = sb("parts", [self.LOW + NCH, CH], F32R)
        self.mean_pe, self.centred, self.squared, self.var_pe = sem("mean_pe"), sem("centred"), sem("squared"), sem("var_pe")
        self.std_act, self.cast_pe, self.out_done = sem("std_act"), sem("cast_pe"), sem("out_done")
        self.inverse = sem("inverse")

    def start_pe(self, pe):
        pe.sem_inc(self.var_pe, 2)
        pe.sem_inc(self.cast_pe, 2)

    def start_act(self, act):
        act.sem_inc(self.std_act, 1)

    def start_dve(self, dve):
        for sm, n in ((self.centred, 2), (self.inverse, 3), (self.out_done, 2)):
            dve.sem_inc(sm, n)
        self.nc.vector.memset(self.parts[:, :].bitcast(F32), 0.0).then_inc(self.inverse, 1)

    def first_pe(self, pe, j, src, ready=None):
        for c in range(NCH):
            n = j * NCH + c
            if ready:
                ready(c)
            pe.wait_ge(self.centred, n + 1)
            self.nc.tensor.matmul(self.mean[c % 2], self.ones[:, :], src(c), start=True, stop=True).then_inc(self.mean_pe, 1)
            if c:
                self.variance(pe, j, c - 1)
        self.variance(pe, j, NCH - 1)

    def variance(self, pe, j, c):
        if c == 0:
            pe.wait_ge(self.std_act, j + 1)
        pe.wait_ge(self.squared, j * NCH + c + 1)
        self.nc.tensor.matmul(self.stat, self.rows[:, NCH - 1 - c:2 * NCH - 1 - c], self.square[c % 2][:, :],
                              start=(c == 0), stop=(c == NCH - 1)).then_inc(self.var_pe, 1)

    def first_act(self, act, j, out, eps):
        for c in range(NCH):
            n = j * NCH + c
            act.wait_ge(self.centred, n + 3)
            act.wait_ge(self.var_pe, n + 1)
            self.nc.scalar.activation(self.square[c % 2][:, :], out(c), ACT.Square).then_inc(self.squared, 1)
        act.wait_ge(self.var_pe, j * NCH + NCH + 2)
        act.wait_ge(self.inverse, j * 3 + 2)
        self.nc.scalar.activation(self.std[:, :], self.stat, ACT.Sqrt, bias=eps[0:NCH, :]).then_inc(self.std_act, 1)

    def first_dve(self, dve, j, src, out):
        for c in range(NCH):
            dve.wait_ge(self.mean_pe, j * NCH + c + 1)
            self.nc.vector.tensor_tensor(out(c), src(c), self.mean[c % 2], ALU.subtract).then_inc(self.centred, 1)

    def between_dve(self, dve, j):
        dve.wait_ge(self.std_act, j + 2)
        dve.wait_ge(self.inverse, j * 3 + 4)
        self.nc.vector.reciprocal(self.rstd[:, :], self.std[:, :]).then_inc(self.inverse, 1)
        dve.wait_ge(self.inverse, j * 3 + 5)
        dve.wait_ge(self.cast_pe, j * NCH + 2)
        self.nc.vector.tensor_copy(self.parts[0:NCH, :], self.rstd[:, :]).then_inc(self.inverse, 1)
        dve.wait_ge(self.inverse, j * 3 + 6)
        self.nc.vector.tensor_tensor(self.parts[self.LOW:self.LOW + NCH, :], self.rstd[:, :],
                                     self.parts[0:NCH, :].bitcast(F32), ALU.subtract).then_inc(self.inverse, 1)

    def second_pe(self, pe, j, each=None):
        pe.wait_ge(self.inverse, j * 3 + 7)
        for c in range(NCH):
            pe.wait_ge(self.out_done, j * NCH + c + 1)
            self.nc.tensor.matmul(self.cast[c % 2], self.spread[:, c, :], self.parts[:, :], start=True, stop=True).then_inc(self.cast_pe, 1)
            if each:
                each(c)

    def second_dve(self, dve, j, out, total=None):
        dve.wait_ge(self.centred, j * NCH + NCH + 2)
        for c in range(NCH):
            dve.wait_ge(self.cast_pe, j * NCH + c + 3)
            if total is None:
                self.nc.vector.tensor_tensor(out(c), out(c), self.cast[c % 2], ALU.mult).then_inc(self.out_done, 1)
            else:
                self.nc.vector.scalar_tensor_tensor(out=out(c), in0=out(c), scalar=1.0, in1=self.cast[c % 2],
                                                    op0=ALU.mult, op1=ALU.mult, accum_out=total(c)).then_inc(self.out_done, 1)


class PairNorm:

    def __init__(self, nc, ctx, tag, ones, banks):
        sb = lambda name: [ctx.enter_context(nc.sbuf_tensor(f"{tag}_{name}{k}", [128, CH], F32)) for k in range(2)]
        sem = lambda name: ctx.enter_context(nc.semaphore(f"{tag}_{name}"))
        self.nc, self.ones = nc, ones
        self.mean, self.var = banks[0:2], banks[2:4]
        self.centred, self.square, self.std, self.rstd = sb("centred"), sb("square"), sb("std"), sb("rstd")
        self.mean_done, self.var_done = sem("mean_done"), sem("var_done")
        self.centred_done, self.square_done = sem("centred_done"), sem("square_done")
        self.std_done, self.rstd_done, self.out_done = sem("std_done"), sem("rstd_done"), sem("out_done")

    def start(self, dve):
        dve.sem_inc(self.centred_done, 2)
        dve.sem_inc(self.out_done, 2)

    def pair_pe(self, pe, n, src):
        for k in range(2):
            pe.wait_ge(self.centred_done, n + k + 1)
            self.nc.tensor.matmul(self.mean[k], self.ones[:, :], src(k), start=True, stop=True).then_inc(self.mean_done, 1)
        for k in range(2):
            pe.wait_ge(self.square_done, n + k + 1)
            self.nc.tensor.matmul(self.var[k], self.ones[:, :], self.square[k][:, :], start=True, stop=True).then_inc(self.var_done, 1)

    def pair_act(self, act, n, eps):
        for k in range(2):
            act.wait_ge(self.centred_done, n + k + 3)
            self.nc.scalar.activation(self.square[k][:, :], self.centred[k][:, :], ACT.Square).then_inc(self.square_done, 1)
        for k in range(2):
            act.wait_ge(self.var_done, n + k + 1)
            self.nc.scalar.activation(self.std[k][:, :], self.var[k], ACT.Sqrt, bias=eps).then_inc(self.std_done, 1)

    def pair_dve(self, dve, n, src, out, total=None):
        for k in range(2):
            dve.wait_ge(self.mean_done, n + k + 1)
            dve.wait_ge(self.out_done, n + k + 1)
            self.nc.vector.tensor_tensor(self.centred[k][:, :], src(k), self.mean[k], ALU.subtract).then_inc(self.centred_done, 1)
        for k in range(2):
            dve.wait_ge(self.std_done, n + k + 1)
            self.nc.vector.reciprocal(self.rstd[k][:, :], self.std[k][:, :]).then_inc(self.rstd_done, 1)
        for k in range(2):
            dve.wait_ge(self.rstd_done, n + k + 1)
            if total is None:
                self.nc.vector.tensor_tensor(out(k), self.centred[k][:, :], self.rstd[k][:, :], ALU.mult).then_inc(self.out_done, 1)
            else:
                self.nc.vector.scalar_tensor_tensor(out=out(k), in0=self.centred[k][:, :], scalar=1.0, in1=self.rstd[k][:, :],
                                                    op0=ALU.mult, op1=ALU.mult, accum_out=total(k)).then_inc(self.out_done, 1)


def passing(sem):
    return lambda eng: eng.sem_inc(sem, 1)


class Chain:

    def __init__(self, eng, sem, base=0):
        self.eng, self.sem, self.base, self.count = eng, sem, base, 0

    def __call__(self, ins):
        self.count += 1
        ins.then_inc(self.sem, 1)
        self.eng.wait_ge(self.sem, self.base + self.count)


def norm_consts(nc, ctx, tag):
    sb = lambda name, shape, dt=F32: ctx.enter_context(nc.sbuf_tensor(tag + name, shape, dt))
    ones, rows = sb("ones", [128, 128]), sb("rows", [128, 2 * NCH - 1])
    spread32, spread = sb("spread32", [Norm.LOW + NCH, NCH * 128]), sb("spread", [Norm.LOW + NCH, NCH, 128], F32R)
    return ones, rows, spread32, spread, [(ones[:, :], "ones"), (rows[:, :], "rows"), (spread32[:, :], "spread_rows")]


def phase_project(nc, d, passed):
    with ExitStack() as ctx:
        sb = lambda name, shape, dt=F32: ctx.enter_context(nc.sbuf_tensor("p_" + name, shape, dt))
        sem = lambda name: ctx.enter_context(nc.semaphore("p_" + name))
        banks = [ctx.enter_context(nc.psum_tensor(f"p_ps{i}", [128, CH], F32)) for i in range(7)]
        ones, rows, spread32, spread, consts = norm_consts(nc, ctx, "p_")
        w_in, eps = sb("w_in", [128, MID]), sb("eps", [128, 1])
        consts = consts + [(w_in[:, :], "w_in")]
        X, XN, PM = sb("X", [128, 2 * HW]), sb("XN", [128, 2 * HW]), sb("PM", [MID, 2 * HW])
        norm = Norm(nc, ctx, "p_norm", ones, rows, spread, [t[:, :] for t in banks[0:5]])
        const_loaded, set_done, x_loaded, s_stored, pm_stored = [sem(n) for n in
            ("const_loaded", "set_done", "x_loaded", "s_stored", "pm_stored")]
        pm_pe, pm_done, s_done = sem("pm_pe"), sem("pm_done"), sem("s_done")
        half = lambda buf, b: buf[:, bass.ds((b % 2) * HW, HW)]
        part = lambda buf, b: lambda c: buf[:, bass.ds((b % 2) * HW + c * CH, CH)]

        with nc.Block() as block:
            @block.sync
            def _(sp):
                for dst, name in consts:
                    sp.dma_start(dst, d[name]).then_inc(const_loaded, 16)
                sp.sem_inc(s_stored, 32)
                sp.sem_inc(pm_stored, 32)

                def load(b):
                    sp.wait_ge(s_stored, b * 16 + 16)
                    passed(sp)
                    sp.dma_start(half(X, b), batch_of(d["x"], b)).then_inc(x_loaded, 16)

                def store(b):
                    sp.wait_ge(s_done, b * NCH + NCH)
                    sp.wait_ge(s_stored, b * 16 + 32)
                    passed(sp)
                    sp.dma_start(batch_of(d["s"], b), half(X, b)).then_inc(s_stored, 16)
                    sp.wait_ge(pm_done, b * NCH + NCH + 2)
                    sp.wait_ge(pm_stored, b * 16 + 32)
                    passed(sp)
                    sp.dma_start(batch_of(d["pm"], b), half(PM, b)).then_inc(pm_stored, 16)

                load(0)
                sp.wait_ge(x_loaded, 16)
                load(1)
                with sp.Fori(2, B) as b:
                    sp.wait_ge(x_loaded, b * 16)
                    store(b - 2)
                    load(b)
                store(B - 2)
                store(B - 1)
                sp.wait_ge(s_stored, B * 16 + 32)
                sp.wait_ge(pm_stored, B * 16 + 32)

            @block.tensor
            def _(pe):
                pe.wait_ge(const_loaded, 16 * len(consts))
                norm.start_pe(pe)
                pe.wait_ge(set_done, 2)

                def first(b):
                    pe.wait_ge(x_loaded, b * 16 + 16)
                    norm.first_pe(pe, b, part(X, b))

                def second(b):
                    def project(c):
                        n = b * NCH + c
                        pe.wait_ge(norm.out_done, n + 3)
                        pe.wait_ge(pm_done, n + 1)
                        nc.tensor.matmul(banks[5 + c % 2][0:MID, :], w_in[:, :], part(XN, b)(c), start=True, stop=True).then_inc(pm_pe, 1)

                    norm.second_pe(pe, b, lambda c: project(c - 1) if c else None)
                    project(NCH - 1)

                first(0)
                with pe.Fori(1, B) as b:
                    first(b)
                    second(b - 1)
                second(B - 1)

            @block.scalar
            def _(act):
                norm.start_act(act)
                act.sem_inc(pm_done, 2)
                act.wait_ge(set_done, 2)

                def read(b):
                    for c in range(NCH):
                        act.wait_ge(pm_pe, b * NCH + c + 1)
                        if c == 0:
                            act.wait_ge(pm_stored, b * 16 + 16)
                        nc.scalar.activation(part(PM, b)(c), banks[5 + c % 2][0:MID, :], ACT.Copy).then_inc(pm_done, 1)

                norm.first_act(act, 0, part(XN, 0), eps)
                with act.Fori(1, B) as b:
                    norm.first_act(act, b, part(XN, b), eps)
                    read(b - 1)
                read(B - 1)

            @block.gpsimd
            def _(pool):
                with pool.Fori(0, B) as b:
                    for c in range(NCH):
                        pool.wait_ge(norm.out_done, b * NCH + c + 3)
                        nc.gpsimd.tensor_tensor(part(X, b)(c), part(X, b)(c), part(XN, b)(c), ALU.add).then_inc(s_done, 1)

            @block.vector
            def _(dve):
                norm.start_dve(dve)
                nc.vector.memset(eps[:, :], EPS_C).then_inc(set_done, 1)
                dve.wait_ge(const_loaded, 16 * len(consts))
                nc.vector.tensor_copy(spread[:, :, :].rearrange("p c n -> p (c n)"), spread32[:, :]).then_inc(set_done, 1)

                def first(b):
                    dve.wait_ge(x_loaded, b * 16 + 16)
                    if not isinstance(b, int):
                        dve.wait_ge(s_done, (b - 1) * NCH)
                        dve.wait_ge(pm_pe, (b - 1) * NCH)
                    norm.first_dve(dve, b, part(X, b), part(XN, b))

                first(0)
                norm.between_dve(dve, 0)
                dve.wait_ge(x_loaded, 32)
                norm.first_dve(dve, 1, part(X, 1), part(XN, 1))
                norm.second_dve(dve, 0, part(XN, 0))
                norm.between_dve(dve, 1)
                with dve.Fori(2, B) as b:
                    first(b)
                    norm.second_dve(dve, b - 1, part(XN, b - 1))
                    norm.between_dve(dve, b)
                norm.second_dve(dve, B - 1, part(XN, B - 1))


def phase_dft(nc, d, passed):
    with ExitStack() as ctx:
        sb = lambda name, shape: ctx.enter_context(nc.sbuf_tensor("a_" + name, shape, F32))
        sem = lambda name: ctx.enter_context(nc.semaphore("a_" + name))
        ps = ctx.enter_context(nc.psum_tensor("a_ps", [128, 8 * CH], F32))
        low, high = ps[:, 0:4 * CH], ps[:, 4 * CH:8 * CH]
        dft = sb("dft", [128, 12 * SIDE])
        mask, binw = sb("mask", [40, HW]), sb("binw", [40, MID])
        gain = sb("gain", [128, MID, SIDE])
        proj, image = sb("proj", [128, MID, SIDE]), sb("image", [128, MID, SIDE])
        rows, enh, back, sqz = [sb(n, [128, MID, 128]) for n in ("rows", "enh", "back", "sqz")]
        r2, mag, zero, den, rec, num, fac, shifted = [sb(n, [128, MID, SIDE]) for n in
                                                      ("r2", "mag", "zero", "den", "rec", "num", "fac", "shifted")]
        g1, g2a, g2b, g3a, g3b = [(i * 128, i * 128 + 128) for i in range(5)]
        g4a, g4b = (640, 704), (704, 768)
        const_loaded, gain_pe, gain_ready, pm_loaded, xe_stored = [sem(n) for n in
            ("const_loaded", "gain_pe", "gain_ready", "pm_loaded", "xe_stored")]
        rows_pe, rows_ready, freq_pe, sqz_done, r2_done, mag_done, enh_ready = [sem(n) for n in
            ("rows_pe", "rows_ready", "freq_pe", "sqz_done", "r2_done", "mag_done", "enh_ready")]
        back_pe, back_ready, image_pe, image_ready, own = [sem(n) for n in ("back_pe", "back_ready", "image_pe", "image_ready", "own")]
        flat = lambda t: t[:, :, :].rearrange("p m k -> p (m k)")
        STEPS = B // 2

        with nc.Block() as block:
            @block.sync
            def _(sp):
                for h in range(2):
                    sp.dma_start(dft[h * SIDE:(h + 1) * SIDE, :], d["dft"]).then_inc(const_loaded, 16)
                sp.dma_start(mask[:, :], d["mask"]).then_inc(const_loaded, 16)
                sp.dma_start(binw[:, :], d["binw"]).then_inc(const_loaded, 16)
                sp.sem_inc(xe_stored, 32)

                def load(i):
                    for h in range(2):
                        sp.dma_start(proj[h * SIDE:(h + 1) * SIDE, :, :],
                                     d["pm"][bass.ds(i * 2 + h, 1), :, :].rearrange("a m (h w) -> h (a m) w", w=SIDE)).then_inc(pm_loaded, 16)

                def store(i):
                    sp.wait_ge(image_ready, i + 2)
                    for h in range(2):
                        sp.dma_start(d["xe"][bass.ds(i * 2 + h, 1), :, :].rearrange("a m (h w) -> h (a m) w", w=SIDE),
                                     image[h * SIDE:(h + 1) * SIDE, :, :]).then_inc(xe_stored, 16)

                load(0)
                with sp.Fori(0, STEPS - 1) as i:
                    sp.wait_ge(rows_pe, i + 1)
                    load(i + 1)
                    store(i)
                store(STEPS - 1)
                sp.wait_ge(xe_stored, STEPS * 32 + 32)

            @block.tensor
            def _(pe):
                pe.wait_ge(const_loaded, 64)
                for h in range(2):
                    for kx in range(SIDE):
                        last = nc.tensor.matmul(high[h * SIDE:(h + 1) * SIDE, kx * MID:(kx + 1) * MID],
                                                mask[:, kx * SIDE:(kx + 1) * SIDE], binw[:, :], start=True, stop=True)
                last.then_inc(gain_pe, 1)
                pe.wait_ge(gain_ready, 1)

                def stage(dst, width, src, tables):
                    for m in range(MID):
                        for q, (g, first) in enumerate(tables):
                            for h in range(2):
                                on = slice(h * SIDE, (h + 1) * SIDE)
                                last = nc.tensor.matmul(dst[on, m * width:(m + 1) * width], src[on, m, first:first + SIDE],
                                                        dft[on, g[0]:g[1]], start=(q == 0), stop=(q == len(tables) - 1))
                    return last

                def forward(i):
                    pe.wait_ge(pm_loaded, i * 32 + 32)
                    pe.wait_ge(image_ready, i + 1)
                    passed(pe)
                    stage(low, 128, proj, [(g1, 0)]).then_inc(rows_pe, 1)
                    pe.wait_ge(rows_ready, i + 1)
                    pe.wait_ge(enh_ready, i + 1)
                    passed(pe)
                    stage(high, 128, rows, [(g2a, 0), (g2b, SIDE)]).then_inc(freq_pe, 1)

                def inverse(i):
                    pe.wait_ge(enh_ready, i + 2)
                    passed(pe)
                    stage(low, 128, enh, [(g3a, 0), (g3b, SIDE)]).then_inc(back_pe, 1)
                    pe.wait_ge(back_ready, i + 1)
                    passed(pe)
                    stage(low, SIDE, back, [(g4a, 0), (g4b, SIDE)]).then_inc(image_pe, 1)

                with pe.Fori(0, STEPS) as i:
                    forward(i)
                    inverse(i)

            @block.scalar
            def _(act):
                with act.Fori(0, STEPS) as i:
                    act.wait_ge(rows_pe, i + 1)
                    nc.scalar.activation(flat(rows), low, ACT.Copy).then_inc(rows_ready, 1)
                    act.wait_ge(freq_pe, i + 1)
                    nc.scalar.activation(flat(sqz), high, ACT.Square).then_inc(sqz_done, 1)
                    act.wait_ge(r2_done, i + 1)
                    nc.scalar.activation(flat(mag), flat(r2), ACT.Sqrt).then_inc(mag_done, 1)
                    act.wait_ge(back_pe, i + 1)
                    nc.scalar.activation(flat(back), low, ACT.Copy).then_inc(back_ready, 1)

            @block.vector
            def _(dve):
                dve.sem_inc(enh_ready, 1)
                dve.sem_inc(image_ready, 1)
                dve.wait_ge(gain_pe, 1)
                nc.vector.tensor_copy(gain[:, :, :], high[:, 0:SIDE * MID].rearrange("p (x m) -> p m x", m=MID)).then_inc(gain_ready, 1)
                dve.wait_ge(gain_ready, 1)
                with dve.Fori(0, STEPS) as i:
                    link = Chain(dve, own, i * 8)
                    dve.wait_ge(sqz_done, i + 1)
                    nc.vector.tensor_tensor(r2[:, :, :], sqz[:, :, 0:SIDE], sqz[:, :, SIDE:128], ALU.add).then_inc(r2_done, 1)
                    dve.wait_ge(mag_done, i + 1)
                    link(nc.vector.tensor_scalar(flat(zero), flat(mag), 0.0, None, ALU.is_equal))
                    link(nc.vector.tensor_tensor(flat(den), flat(mag), flat(zero), ALU.add))
                    link(nc.vector.reciprocal(flat(rec), flat(den)))
                    link(nc.vector.scalar_tensor_tensor(out=flat(num), in0=flat(mag), scalar=EPS_MAG, in1=flat(gain),
                                                        op0=ALU.add, op1=ALU.mult))
                    link(nc.vector.tensor_tensor(flat(fac), flat(num), flat(rec), ALU.mult))
                    z = high.rearrange("p (m k) -> p m k", k=128)
                    link(nc.vector.tensor_tensor(shifted[:, :, :], z[:, :, 0:SIDE], zero[:, :, :], ALU.add))
                    link(nc.vector.tensor_tensor(enh[:, :, 0:SIDE], shifted[:, :, :], fac[:, :, :], ALU.mult))
                    link(nc.vector.tensor_tensor(enh[:, :, SIDE:128], z[:, :, SIDE:128], fac[:, :, :], ALU.mult))
                    dve.sem_inc(enh_ready, 1)
                    dve.wait_ge(image_pe, i + 1)
                    dve.wait_ge(xe_stored, i * 32 + 32)
                    nc.vector.tensor_copy(flat(image), low[:, 0:SIDE * MID]).then_inc(image_ready, 1)


def phase_mix(nc, d, passed):
    with ExitStack() as ctx:
        sb = lambda name, shape: ctx.enter_context(nc.sbuf_tensor("m_" + name, shape, F32))
        sem = lambda name: ctx.enter_context(nc.semaphore("m_" + name))
        banks = [ctx.enter_context(nc.psum_tensor(f"m_ps{i}", [128, CH], F32)) for i in range(7)]
        ones, rows, spread32, spread, consts = norm_consts(nc, ctx, "m_")
        w_out, eps = sb("w_out", [MID, 128]), sb("eps", [128, 1])
        consts = consts + [(w_out[:, :], "w_out")]
        X, TN, XE = sb("X", [128, 2 * HW]), sb("TN", [128, 2 * HW]), sb("XE", [MID, 2 * HW])
        sums, total = sb("sums", [128, B * NCH]), sb("total", [128, B])
        norm = Norm(nc, ctx, "m_norm", ones, rows, spread, [t[:, :] for t in banks[0:5]])
        const_loaded, set_done, loaded, x1_stored, tn_stored = [sem(n) for n in
            ("const_loaded", "set_done", "loaded", "x1_stored", "tn_stored")]
        y_pe, x1_done, total_done, total_stored = sem("y_pe"), sem("x1_done"), sem("total_done"), sem("total_stored")
        half = lambda buf, b: buf[:, bass.ds((b % 2) * HW, HW)]
        part = lambda buf, b: lambda c: buf[:, bass.ds((b % 2) * HW + c * CH, CH)]

        with nc.Block() as block:
            @block.sync
            def _(sp):
                for dst, name in consts:
                    sp.dma_start(dst, d[name]).then_inc(const_loaded, 16)
                sp.sem_inc(x1_stored, 32)
                sp.sem_inc(tn_stored, 32)

                def load(b):
                    sp.wait_ge(x1_stored, b * 16 + 16)
                    passed(sp)
                    sp.dma_start(half(X, b), batch_of(d["s"], b)).then_inc(loaded, 16)
                    sp.dma_start(half(XE, b), batch_of(d["xe"], b)).then_inc(loaded, 16)

                def store(b):
                    sp.wait_ge(norm.out_done, b * NCH + NCH + 2)
                    sp.wait_ge(x1_stored, b * 16 + 32)
                    passed(sp)
                    sp.dma_start(batch_of(d["x1"], b), half(X, b)).then_inc(x1_stored, 16)
                    sp.wait_ge(tn_stored, b * 16 + 32)
                    passed(sp)
                    sp.dma_start(batch_of(d["tn"], b), half(TN, b)).then_inc(tn_stored, 16)

                load(0)
                sp.wait_ge(loaded, 32)
                load(1)
                with sp.Fori(2, B) as b:
                    sp.wait_ge(loaded, b * 32)
                    store(b - 2)
                    load(b)
                store(B - 2)
                store(B - 1)
                sp.wait_ge(total_done, 1)
                sp.dma_start(d["total"], total[:, :]).then_inc(total_stored, 16)
                sp.wait_ge(x1_stored, B * 16 + 32)
                sp.wait_ge(tn_stored, B * 16 + 32)
                sp.wait_ge(total_stored, 16)

            @block.tensor
            def _(pe):
                pe.wait_ge(const_loaded, 16 * len(consts))
                norm.start_pe(pe)
                pe.wait_ge(set_done, 2)

                def first(b):
                    def mix(c):
                        pe.wait_ge(x1_done, b * NCH + c + 1)
                        passed(pe)
                        nc.tensor.matmul(banks[5 + c % 2][:, :], w_out[:, :], part(XE, b)(c), start=True, stop=True).then_inc(y_pe, 1)

                    def ready(c):
                        if c + 1 < NCH:
                            mix(c + 1)
                        pe.wait_ge(x1_done, b * NCH + c + 3)

                    pe.wait_ge(loaded, b * 32 + 32)
                    mix(0)
                    norm.first_pe(pe, b, part(X, b), ready)

                first(0)
                with pe.Fori(1, B) as b:
                    first(b)
                    norm.second_pe(pe, b - 1)
                norm.second_pe(pe, B - 1)

            @block.scalar
            def _(act):
                norm.start_act(act)
                act.wait_ge(set_done, 2)
                with act.Fori(0, B) as b:
                    norm.first_act(act, b, part(TN, b), eps)

            @block.vector
            def _(dve):
                norm.start_dve(dve)
                dve.sem_inc(x1_done, 2)
                nc.vector.memset(eps[:, :], EPS_T).then_inc(set_done, 1)
                dve.wait_ge(const_loaded, 16 * len(consts))
                nc.vector.tensor_copy(spread[:, :, :].rearrange("p c n -> p (c n)"), spread32[:, :]).then_inc(set_done, 1)

                def first(b):
                    def add(c):
                        dve.wait_ge(y_pe, b * NCH + c + 1)
                        nc.vector.tensor_tensor(part(X, b)(c), part(X, b)(c), banks[5 + c % 2][:, :], ALU.add).then_inc(x1_done, 1)

                    def centre(c):
                        dve.wait_ge(norm.mean_pe, b * NCH + c + 1)
                        nc.vector.tensor_tensor(part(TN, b)(c), part(X, b)(c), norm.mean[c % 2], ALU.subtract).then_inc(norm.centred, 1)

                    dve.wait_ge(loaded, b * 32 + 32)
                    dve.wait_ge(tn_stored, b * 16 + 16)
                    add(0)
                    for c in range(1, NCH):
                        add(c)
                        centre(c - 1)
                    centre(NCH - 1)

                def second(b):
                    norm.second_dve(dve, b, part(TN, b), lambda c: sums[:, bass.ds(b * NCH + c, 1)])

                first(0)
                norm.between_dve(dve, 0)
                with dve.Fori(1, B) as b:
                    first(b)
                    second(b - 1)
                    norm.between_dve(dve, b)
                second(B - 1)
                dve.wait_ge(norm.out_done, B * NCH + 2)
                nc.vector.tensor_reduce(total[:, :], sums[:, :].rearrange("p (b c) -> p b c", c=NCH), AX.X, ALU.add).then_inc(total_done, 1)


def phase_route0(nc, d, route):
    pick, pickw, dense = route
    with ExitStack() as ctx:
        sb = lambda name, shape: ctx.enter_context(nc.sbuf_tensor("r_" + name, shape, F32))
        sem = lambda name: ctx.enter_context(nc.semaphore("r_" + name))
        total, wide = sb("total", [128, B]), sb("wide", [128, B, 128])
        wr, br, before = sb("wr", [128, E]), sb("br", [128, E]), sb("before", [128, E * E])
        logit, ex, rw, sel = [sb(n, [128, B, E]) for n in ("logit", "ex", "rw", "sel")]
        top, low = sb("top", [128, B]), sb("low", [128, B])
        load, scale = sb("load", [128, E]), sb("scale", [128, E])
        more, same, rank = sb("more", [128, B, E, E]), sb("same", [128, B, E, E]), sb("rank", [128, B, E])
        ps = ctx.enter_context(nc.psum_tensor("r_ps", [128, B * E], F32))
        loaded, wide_ready, logit_pe, own, exp_in, exp_done = [sem(n) for n in
                                                              ("loaded", "wide_ready", "logit_pe", "own", "exp_in", "exp_done")]
        per_e = lambda t: t[:, :].unsqueeze(2).broadcast_to([128, B, E])
        per_b = lambda t: t[:, :].unsqueeze(1).broadcast_to([128, B, E])
        with nc.Block() as block:
            @block.sync
            def _(sp):
                for dst, name in ((total, "total"), (wr, "wr"), (br, "br"), (before, "before")):
                    sp.dma_start(dst[:, :], d[name]).then_inc(loaded, 16)

            @block.tensor
            def _(pe):
                pe.wait_ge(wide_ready, 1)
                for b in range(B):
                    last = nc.tensor.matmul(ps[:, b * E:(b + 1) * E], wide[:, b, :], wr[:, :], start=True, stop=True)
                last.then_inc(logit_pe, 1)

            @block.scalar
            def _(act):
                for i in range(3):
                    act.wait_ge(exp_in, i + 1)
                    nc.scalar.activation(ex[:, :, :], ex[:, :, :], ACT.Exp).then_inc(exp_done, 1)

            @block.vector
            def _(dve):
                link = Chain(dve, own)
                dve.wait_ge(loaded, 64)
                nc.vector.tensor_copy(wide[:, :, :], total[:, :].unsqueeze(2).broadcast_to([128, B, 128])).then_inc(wide_ready, 1)
                dve.wait_ge(logit_pe, 1)
                link(nc.vector.scalar_tensor_tensor(out=logit[:, :, :], in0=ps[:, :].rearrange("p (b e) -> p b e", e=E), scalar=1.0 / HW,
                                                    in1=per_b(br), op0=ALU.mult, op1=ALU.add))

                def softmax(src, dst, i):
                    link(nc.vector.tensor_reduce(top[:, :], src[:, :, :], AX.X, ALU.max))
                    link(nc.vector.tensor_tensor(ex[:, :, :], src[:, :, :], per_e(top), ALU.subtract))
                    dve.sem_inc(exp_in, 1)
                    dve.wait_ge(exp_done, i + 1)
                    if dst is not None:
                        link(nc.vector.tensor_reduce(low[:, :], ex[:, :, :], AX.X, ALU.add))
                        link(nc.vector.reciprocal(low[:, :], low[:, :]))
                        link(nc.vector.tensor_tensor(dst[:, :, :], ex[:, :, :], per_e(low), ALU.mult))

                softmax(logit, rw, 0)
                link(nc.vector.tensor_reduce(load[:, :], rw[:, :, :].rearrange("p b e -> p e b"), AX.X, ALU.add))
                link(nc.vector.tensor_scalar(load[:, :], load[:, :], float(HW), None, ALU.mult))
                link(nc.vector.reciprocal(load[:, :], load[:, :]))
                link(nc.vector.tensor_scalar(scale[:, :], load[:, :], float(-(-B * HW * 5 // (4 * E))), 1.0, ALU.mult, ALU.min))
                link(nc.vector.tensor_tensor(logit[:, :, :], rw[:, :, :], per_b(scale), ALU.mult))
                softmax(logit, rw, 1)
                mine = rw[:, :, :].unsqueeze(3).broadcast_to([128, B, E, E])
                other = rw[:, :, :].unsqueeze(2).broadcast_to([128, B, E, E])
                first = before[:, :].rearrange("p (e f) -> p e f", f=E)
                link(nc.vector.tensor_tensor(more[:, :, :, :], other, mine, ALU.is_gt))
                link(nc.vector.tensor_tensor(same[:, :, :, :], other, mine, ALU.is_equal))
                for b in range(B):
                    link(nc.vector.tensor_tensor(same[:, b, :, :], same[:, b, :, :], first, ALU.mult))
                link(nc.vector.tensor_tensor(more[:, :, :, :], more[:, :, :, :], same[:, :, :, :], ALU.add))
                link(nc.vector.tensor_reduce(rank[:, :, :], more[:, :, :, :], AX.X, ALU.add))
                softmax(rw, None, 2)
                link(nc.vector.tensor_scalar(sel[:, :, :], rank[:, :, :], 1.5, None, ALU.is_lt))
                link(nc.vector.tensor_tensor(ex[:, :, :], ex[:, :, :], sel[:, :, :], ALU.mult))
                link(nc.vector.tensor_reduce(low[:, :], ex[:, :, :], AX.X, ALU.add))
                link(nc.vector.reciprocal(low[:, :], low[:, :]))
                link(nc.vector.tensor_tensor(dense[:, :, :], ex[:, :, :], per_e(low), ALU.mult))
                for j in range(2):
                    link(nc.vector.tensor_scalar(pick[:, :, j, :], rank[:, :, :], float(j), None, ALU.is_equal))
                    link(nc.vector.tensor_tensor(pickw[:, :, j, :], pick[:, :, j, :], dense[:, :, :], ALU.mult))


def phase_ffn0(nc, d, passed, route):
    pick, pickw, dense = route
    with ExitStack() as ctx:
        sb = lambda name, shape: ctx.enter_context(nc.sbuf_tensor("b_" + name, shape, F32))
        sem = lambda name: ctx.enter_context(nc.semaphore("b_" + name))
        banks = [ctx.enter_context(nc.psum_tensor(f"b_ps{i}", [128, CH], F32)) for i in range(8)]
        ones, wq = sb("ones", [128, 128]), sb("wq", [128, 3, 128])
        w1, w2 = sb("w1", [128, E, F0]), sb("w2", [128, E, F0])
        b1, b2, gb = sb("b1", [128, E, 2]), sb("b2", [128, E]), sb("gb", [128, 2])
        w1s, w2s, b1s, b2s = sb("w1s", [128, 2, F0]), sb("w2s", [128, 2, F0]), sb("b1s", [128, 2, 2]), sb("b2s", [128, 1])
        X, TN, Z = sb("X", [128, HW]), sb("TN", [128, HW]), sb("Z", [128, HW])
        hid = [[sb(f"hid{k}{i}", [128, CH]) for i in range(4)] for k in range(2)]
        qkv = [sb(f"qkv{k}", [128, 3, CH]) for k in range(2)]
        eps_c, eps_t = sb("eps_c", [128, 1]), sb("eps_t", [128, 1])
        norm = PairNorm(nc, ctx, "b_norm", ones, [banks[i][:, :] for i in range(4)])
        const_loaded, set_done, xt_loaded, x2_stored = [sem(n) for n in ("const_loaded", "set_done", "xt_loaded", "x2_stored")]
        qkv_stored = [sem(f"qkv_stored{k}") for k in range(2)]
        chosen, hid_pe, hid_done, y_pe, z_done = [sem(n) for n in ("chosen", "hid_pe", "hid_done", "y_pe", "z_done")]
        affine_done, x2_done, qkv_pe, qkv_act, qkv_dve = [sem(n) for n in ("affine_done", "x2_done", "qkv_pe", "qkv_act", "qkv_dve")]
        consts = [(ones[:, :], "ones"), (wq[:, :, :], "wq"), (w1[:, :, :], "w1"), (w2[:, :, :], "w2"), (b1[:, :, :], "b1"),
                  (b2[:, :], "b2"), (gb[:, :], "gb")]
        CHOICES = 2 * 3 * E + E
        qkv_bank = lambda k, j: banks[(5, 1)[k] + j][:, :]

        with nc.Block() as block:
            @block.sync
            def _(sp):
                for dst, name in consts:
                    sp.dma_start(dst, d[name]).then_inc(const_loaded, 16)
                sp.sem_inc(x2_stored, 16)
                sp.sem_inc(qkv_stored[0], 16)
                sp.sem_inc(qkv_stored[1], 16)
                with sp.Fori(0, B) as b:
                    sp.wait_ge(x2_stored, b * 16 + 16)
                    sp.dma_start(X[:, :], d["x1"][bass.ds(b, 1), :, :].rearrange("a p n -> p (a n)")).then_inc(xt_loaded, 16)
                    sp.wait_ge(qkv_pe, b * NCH + 1)
                    sp.dma_start(TN[:, :], d["tn"][bass.ds(b, 1), :, :].rearrange("a p n -> p (a n)")).then_inc(xt_loaded, 16)
                    sp.wait_ge(x2_done, b * NCH + NCH)
                    sp.dma_start(d["x2"][bass.ds(b, 1), :, :].rearrange("a p n -> p (a n)"), X[:, :]).then_inc(x2_stored, 16)
                    with sp.Fori(0, NCH // 2) as p:
                        for k in range(2):
                            n = b * NCH + p * 2 + k
                            sp.wait_ge(qkv_act, n + 3)
                            sp.wait_ge(qkv_dve, n + 3)
                            dst = d["qkv"][bass.ds(b, 1), :, :, bass.ds((p * 2 + k) * CH, CH)].rearrange("a j c n -> c (a j) n")
                            sp.dma_start(dst, qkv[k][:, :, :]).then_inc(qkv_stored[k], 16)
                sp.wait_ge(x2_stored, B * 16 + 16)
                for k in range(2):
                    sp.wait_ge(qkv_stored[k], B * NCH // 2 * 16 + 16)

            @block.tensor
            def _(pe):
                pe.sem_inc(qkv_pe, 1)
                pe.sem_inc(y_pe, 2)
                pe.wait_ge(const_loaded, 16 * len(consts))

                def up(n, src, k):
                    for i in range(4):
                        pe.wait_ge(hid_done, (n - 1) * 4 + i + 1 + 4)
                        nc.tensor.matmul(banks[i][:, :], w1s[:, i // 2, (i % 2) * 128:(i % 2) * 128 + 128], src,
                                         start=True, stop=True).then_inc(hid_pe, 1)

                def down(n, k):
                    pe.wait_ge(z_done, n + 1)
                    for i in range(4):
                        pe.wait_ge(hid_done, n * 4 + i + 1 + 4)
                        last = nc.tensor.matmul(banks[4 + k][:, :], w2s[:, i // 2, (i % 2) * 128:(i % 2) * 128 + 128], hid[k][i][:, :],
                                                start=(i == 0), stop=(i == 3))
                    last.then_inc(y_pe, 1)

                with pe.Fori(0, B) as b:
                    pe.wait_ge(xt_loaded, b * 32 + 32)
                    pe.wait_ge(chosen, b * CHOICES + CHOICES)
                    up(b * NCH, chunk(TN, 0), 0)
                    up(b * NCH + 1, chunk(TN, 1), 1)
                    down(b * NCH, 0)
                    with pe.Fori(1, NCH // 2) as p:
                        n = b * NCH + p * 2
                        up(n, chunk(TN, p * 2), 0)
                        down(n - 1, 1)
                        up(n + 1, chunk(TN, p * 2 + 1), 1)
                        down(n, 0)
                    down(b * NCH + NCH - 1, 1)
                    pe.wait_ge(z_done, b * NCH + NCH + 2)
                    passed(pe)
                    with pe.Fori(0, NCH // 2) as p:
                        norm.pair_pe(pe, b * 2 * NCH + p * 2, lambda k: chunk(Z, p * 2 + k))
                    pe.wait_ge(x2_done, b * NCH + NCH)
                    passed(pe)
                    with pe.Fori(0, NCH // 2) as p:
                        norm.pair_pe(pe, b * 2 * NCH + NCH + p * 2, lambda k: chunk(X, p * 2 + k))
                    pe.wait_ge(norm.out_done, b * 2 * NCH + 2 * NCH + 2)
                    passed(pe)
                    with pe.Fori(0, NCH // 2) as p:
                        for k in range(2):
                            n = b * NCH + p * 2 + k
                            pe.wait_ge(qkv_act, n + 1)
                            pe.wait_ge(qkv_dve, n + 1)
                            for j in range(3):
                                last = nc.tensor.matmul(qkv_bank(k, j), wq[:, j, :], chunk(TN, p * 2 + k), start=True, stop=True)
                            last.then_inc(qkv_pe, 1)
                    pe.wait_ge(qkv_act, b * NCH + NCH + 2)
                    pe.wait_ge(qkv_dve, b * NCH + NCH + 2)

            @block.scalar
            def _(act):
                act.sem_inc(hid_done, 4)
                act.sem_inc(qkv_act, 2)
                act.wait_ge(set_done, 2)
                with act.Fori(0, B) as b:
                    with act.Fori(0, NCH // 2) as p:
                        for k in range(2):
                            n = b * NCH + p * 2 + k
                            act.wait_ge(y_pe, n + 1)
                            for i in range(4):
                                act.wait_ge(hid_pe, n * 4 + i + 1)
                                nc.scalar.activation(hid[k][i][:, :], banks[i][:, :], ACT.Gelu,
                                                     bias=b1s[:, i // 2, i % 2:i % 2 + 1]).then_inc(hid_done, 1)
                    with act.Fori(0, NCH // 2) as p:
                        norm.pair_act(act, b * 2 * NCH + p * 2, eps_t[:, :])
                    with act.Fori(0, NCH) as c:
                        act.wait_ge(norm.out_done, b * 2 * NCH + c + 3)
                        nc.scalar.activation(chunk(Z, c), chunk(Z, c), ACT.Identity, bias=gb[:, 1:2], scale=gb[:, 0:1]).then_inc(affine_done, 1)
                    with act.Fori(0, NCH // 2) as p:
                        norm.pair_act(act, b * 2 * NCH + NCH + p * 2, eps_c[:, :])
                    with act.Fori(0, NCH // 2) as p:
                        for k in range(2):
                            n = b * NCH + p * 2 + k
                            act.wait_ge(qkv_pe, n + 2)
                            act.wait_ge(qkv_stored[k], (b * (NCH // 2) + p) * 16 + 16)
                            nc.scalar.activation(qkv[k][:, 0, :], qkv_bank(k, 0), ACT.Copy)
                            nc.scalar.activation(qkv[k][:, 1, :], qkv_bank(k, 1), ACT.Copy).then_inc(qkv_act, 1)

            @block.gpsimd
            def _(pool):
                pool.wait_ge(const_loaded, 16 * len(consts))
                with pool.Fori(0, B) as b:
                    with pool.Fori(0, NCH) as c:
                        pool.wait_ge(affine_done, b * NCH + c + 1)
                        nc.gpsimd.tensor_tensor(chunk(X, c), chunk(X, c), chunk(Z, c), ALU.add).then_inc(x2_done, 1)

            @block.vector
            def _(dve):
                nc.vector.memset(eps_c[:, :], EPS_C).then_inc(set_done, 1)
                nc.vector.memset(eps_t[:, :], EPS_T).then_inc(set_done, 1)
                norm.start(dve)
                dve.sem_inc(z_done, 2)
                dve.sem_inc(qkv_dve, 2)
                dve.wait_ge(const_loaded, 16 * len(consts))
                picks = pick[:, :, :, :].rearrange("p b j e -> p (b j e)")
                pickws = pickw[:, :, :, :].rearrange("p b j e -> p (b j e)")
                denses = dense[:, :, :].rearrange("p b e -> p (b e)")
                with dve.Fori(0, B) as b:
                    dve.wait_ge(y_pe, b * NCH + 2)
                    for e in range(E):
                        if e:
                            dve.wait_ge(chosen, b * CHOICES + 7 * e)
                        for j in range(2):
                            for dst, src, by in ((w1s[:, j, :], w1[:, e, :], picks), (w2s[:, j, :], w2[:, e, :], pickws),
                                                 (b1s[:, j, :], b1[:, e, :], picks)):
                                f = by[:, bass.ds(b * 2 * E + j * E + e, 1)]
                                if e:
                                    nc.vector.scalar_tensor_tensor(out=dst, in0=src, scalar=f, in1=dst, op0=ALU.mult, op1=ALU.add).then_inc(chosen, 1)
                                else:
                                    nc.vector.tensor_scalar(dst, src, f, None, ALU.mult).then_inc(chosen, 1)
                        f = denses[:, bass.ds(b * E + e, 1)]
                        if e:
                            nc.vector.scalar_tensor_tensor(out=b2s[:, :], in0=b2[:, e:e + 1], scalar=f, in1=b2s[:, :],
                                                           op0=ALU.mult, op1=ALU.add).then_inc(chosen, 1)
                        else:
                            nc.vector.tensor_scalar(b2s[:, :], b2[:, 0:1], f, None, ALU.mult).then_inc(chosen, 1)
                    dve.wait_ge(chosen, b * CHOICES + CHOICES)
                    dve.wait_ge(xt_loaded, b * 32 + 32)
                    passed(dve)
                    with dve.Fori(0, NCH // 2) as p:
                        for k in range(2):
                            n = b * NCH + p * 2 + k
                            dve.wait_ge(y_pe, n + 3)
                            nc.vector.scalar_tensor_tensor(out=chunk(Z, p * 2 + k), in0=banks[4 + k][:, :], scalar=b2s[:, :],
                                                           in1=chunk(TN, p * 2 + k), op0=ALU.add, op1=ALU.add).then_inc(z_done, 1)
                    dve.wait_ge(z_done, b * NCH + NCH + 2)
                    passed(dve)
                    with dve.Fori(0, NCH // 2) as p:
                        norm.pair_dve(dve, b * 2 * NCH + p * 2, lambda k: chunk(Z, p * 2 + k), lambda k: chunk(Z, p * 2 + k))
                    dve.wait_ge(x2_done, b * NCH + NCH)
                    passed(dve)
                    with dve.Fori(0, NCH // 2) as p:
                        norm.pair_dve(dve, b * 2 * NCH + NCH + p * 2, lambda k: chunk(X, p * 2 + k), lambda k: chunk(TN, p * 2 + k))
                    with dve.Fori(0, NCH // 2) as p:
                        for k in range(2):
                            n = b * NCH + p * 2 + k
                            dve.wait_ge(qkv_pe, n + 2)
                            dve.wait_ge(qkv_stored[k], (b * (NCH // 2) + p) * 16 + 16)
                            nc.vector.tensor_copy(qkv[k][:, 2, :], qkv_bank(k, 2)).then_inc(qkv_dve, 1)


def phase_conv(nc, d, passed):
    N_IN, N_OUT = HB * SIDE, (HB + 1) * SIDE
    SPANS = [(0, ROWS), (ROWS, ROWS), (2 * ROWS, 1)]
    with ExitStack() as ctx:
        sb = lambda name, shape, dt=F32: ctx.enter_context(nc.sbuf_tensor("c_" + name, shape, dt))
        sem = lambda name: ctx.enter_context(nc.semaphore("c_" + name))
        banks = [ctx.enter_context(nc.psum_tensor(f"c_ps{i}", [128, CH], F32)) for i in range(6)]
        pw, dw = sb("pw", [128, GROUPS, GC]), sb("dw", [128, GROUPS, TAPS * PH])
        prod = sb("prod", [128, TAPS * PH, GC])
        w_hi = [sb(f"w_hi{k}", [128, TAPS, 128], F32R) for k in range(2)]
        w_lo = [sb(f"w_lo{k}", [128, TAPS, 128], F32R) for k in range(2)]
        P = [sb(f"P{k}", [128, N_IN]) for k in range(2)]
        p_hi = [sb(f"p_hi{k}", [128, HB + 2, PADW], F32R) for k in range(2)]
        p_lo = [sb(f"p_lo{k}", [128, HB + 2, PADW], F32R) for k in range(2)]
        out = [sb(f"out{k}", [128, N_OUT]) for k in range(2)]
        const_loaded, cleared, prod_done, whi_done, wlo_done = [sem(n) for n in
            ("const_loaded", "cleared", "prod_done", "whi_done", "wlo_done")]
        hi_done, lo_done, span_pe, out_done = [sem(n) for n in ("hi_done", "lo_done", "span_pe", "out_done")]
        loaded = [sem(f"loaded{k}") for k in range(2)]
        stored = [sem(f"stored{k}") for k in range(2)]
        flat = lambda t: t[:, :, :].rearrange("p a b -> p (a b)")
        inner = lambda t: t[:, 1:1 + HB, 2:2 + SIDE]
        rows_of = lambda t: t[:, :].rearrange("p (h w) -> p h w", w=SIDE)

        with nc.Block() as block:
            @block.sync
            def _(sp):
                sp.dma_start(pw[:, :, :], d["pw"]).then_inc(const_loaded, 16)
                sp.dma_start(dw[:, :, :], d["dw"]).then_inc(const_loaded, 16)
                by_phase = lambda name: d[name].rearrange("b j c (r n) -> (b j c) r n", r=PH)
                for k in range(2):
                    sp.sem_inc(stored[k], 64)

                def first_row(n):
                    return (n % B) * 3 * C + (n // B) * GC

                def load(n, k):
                    sp.wait_ge(lo_done, n + 1)
                    for r in range(PH):
                        sp.dma_start(P[k][r * GC:(r + 1) * GC, :], by_phase("qkv")[bass.ds(first_row(n), GC), r, :]).then_inc(loaded[k], 16)

                def store(n, k):
                    sp.wait_ge(out_done, n * 3 + 3 + 6)
                    for f in range(PH):
                        skip = SIDE if f >= 2 else 0
                        sp.dma_start(by_phase("agg")[bass.ds(first_row(n), GC), f, :],
                                     out[k][f * GC:(f + 1) * GC, skip:skip + HB * SIDE]).then_inc(stored[k], 16)

                U = GROUPS * B // 2
                load(0, 0)
                load(1, 1)
                with sp.Fori(0, U - 1) as u:
                    for k in range(2):
                        store(u * 2 + k, k)
                        load(u * 2 + k + 2, k)
                for k in range(2):
                    store(2 * U - 2 + k, k)
                for k in range(2):
                    sp.wait_ge(stored[k], U * 64 + 64)

            @block.scalar
            def _(act):
                act.wait_ge(cleared, 4)
                with act.Fori(0, GROUPS * B // 2) as u:
                    for k in range(2):
                        act.wait_ge(loaded[k], u * 64 + 64)
                        act.wait_ge(span_pe, (u * 2 + k) * 3 + 3)
                        nc.scalar.activation(inner(p_hi[k]), rows_of(P[k]), ACT.Copy).then_inc(hi_done, 1)

            @block.gpsimd
            def _(pool):
                for k in range(2):
                    nc.gpsimd.memset(p_hi[k][:, :, :].bitcast(F32), 0.0).then_inc(cleared, 1)
                    nc.gpsimd.memset(p_lo[k][:, :, :].bitcast(F32), 0.0).then_inc(cleared, 1)
                pool.wait_ge(const_loaded, 32)

                def weights(g, k):
                    taps = dw[:, bass.ds(g, 1), :].rearrange("p a t -> p (a t)").unsqueeze(2).broadcast_to([128, TAPS * PH, GC])
                    mix = pw[:, bass.ds(g, 1), :].broadcast_to([128, TAPS * PH, GC])
                    if not isinstance(g, int) or g:
                        pool.wait_ge(span_pe, (g - 1) * B * 3 + 6)
                    nc.gpsimd.tensor_tensor(prod[:, :, :], taps, mix, ALU.mult).then_inc(prod_done, 1)
                    pool.wait_ge(prod_done, g + 1)
                    passed(pool)
                    nc.gpsimd.tensor_copy(flat(w_hi[k]), flat(prod)).then_inc(whi_done, 1)
                    pool.wait_ge(whi_done, g + 1)
                    nc.gpsimd.tensor_tensor(flat(w_lo[k]), flat(prod), flat(w_hi[k]).bitcast(F32), ALU.subtract).then_inc(wlo_done, 1)
                    pool.wait_ge(wlo_done, g + 1)

                weights(0, 0)
                weights(1, 1)
                with pool.Fori(1, GROUPS // 2) as gg:
                    for k in range(2):
                        weights(gg * 2 + k, k)

            @block.tensor
            def _(pe):
                pe.sem_inc(span_pe, 6)
                with pe.Fori(0, GROUPS // 2) as gg:
                    for gk in range(2):
                        g = gg * 2 + gk
                        pe.wait_ge(wlo_done, g + 1)
                        passed(pe)
                        with pe.Fori(0, B // 2) as h:
                            for k in range(2):
                                n = g * B + h * 2 + k
                                pe.wait_ge(lo_done, n + 3)
                                for q, (s0, ns) in enumerate(SPANS):
                                    pe.wait_ge(out_done, n * 3 + q + 1)
                                    i = 0
                                    for wt, src in ((w_hi, p_hi), (w_hi, p_lo), (w_lo, p_hi)):
                                        for t in range(TAPS):
                                            s, x = s0 + t // 5, t % 5
                                            last = nc.tensor.matmul(banks[3 * k + q][:, 0:ns * SIDE], wt[gk][:, t, :],
                                                                    src[k][:, s:s + ns, x:x + SIDE],
                                                                    start=(i == 0), stop=(i == 3 * TAPS - 1))
                                            i += 1
                                    last.then_inc(span_pe, 1)

            @block.vector
            def _(dve):
                dve.sem_inc(lo_done, 2)
                dve.sem_inc(out_done, 6)

                def low(n, k):
                    dve.wait_ge(hi_done, n + 1)
                    nc.vector.tensor_tensor(inner(p_lo[k]), rows_of(P[k]), inner(p_hi[k]).bitcast(F32), ALU.subtract).then_inc(lo_done, 1)

                def read(n, u, k):
                    dve.wait_ge(stored[k], u * 64 + 64)
                    for q, (s0, ns) in enumerate(SPANS):
                        dve.wait_ge(span_pe, n * 3 + q + 1 + 6)
                        nc.vector.tensor_copy(out[k][:, s0 * SIDE:(s0 + ns) * SIDE], banks[3 * k + q][:, 0:ns * SIDE]).then_inc(out_done, 1)

                U = GROUPS * B // 2
                low(0, 0)
                with dve.Fori(0, U - 1) as u:
                    low(u * 2 + 1, 1)
                    read(u * 2, u, 0)
                    low(u * 2 + 2, 0)
                    read(u * 2 + 1, u, 1)
                low(2 * U - 1, 1)
                read(2 * U - 2, U - 1, 0)
                read(2 * U - 1, U - 1, 1)


def phase_attention(nc, d, passed):
    TPC = CH // 128
    NT = HW // 128
    HEADS = 16
    KVS = 2 * NCH
    with ExitStack() as ctx:
        sb = lambda name, shape, dt=F32: ctx.enter_context(nc.sbuf_tensor("d_" + name, shape, dt))
        two = lambda name, shape, dt=F32: [sb(f"{name}{k}", shape, dt) for k in range(2)]
        sem = lambda name: ctx.enter_context(nc.semaphore("d_" + name))
        ps = ctx.enter_context(nc.psum_tensor("d_ps", [128, 8 * CH], F32))
        bank = lambda i: ps[:, i * CH:(i + 1) * CH]
        X, TN, ATT1 = sb("X", [128, HW]), sb("TN", [128, HW]), sb("ATT1", [128, HW])
        ATT = [TN, ATT1]
        sel32, w1_32 = X[:, 0:NCH * 128], X[:, 1024:1024 + E * 128]
        rows32, spread32 = X[0:Norm.LOW + NCH, 2048:2048 + NCH * 128], X[0:3 * E, 3072:3072 + E * 128]
        ones, ident, rows = sb("ones", [128, 128]), sb("ident", [128, 128]), sb("rows", [128, 2 * NCH - 1])
        heads, head_of = sb("heads", [128, 128]), sb("head_of", [128, HEADS])
        ident_bf = sb("ident_bf", [128, 128], BF16)
        sel, row_spread = sb("sel", [128, NCH, 128], F32R), sb("row_spread", [Norm.LOW + NCH, NCH, 128], F32R)
        wp, bn, bnv = sb("wp", [128, 2, 128]), sb("bn", [128, 4]), sb("bnv", [128, 4])
        wr, before = sb("wr", [128, E]), sb("before", [128, E * E])
        w1h, w1l = sb("w1h", [128, E, 128], F32R), sb("w1l", [128, E, 128], F32R)
        w2, b1 = sb("w2", [128, E, 128]), sb("b1", [128, E])
        b2, b2r = sb("b2", [3 * E, 128]), sb("b2r", [3 * E, 128])
        b2s = sb("b2s", [3 * E, 3, 128], BF16)
        spread_bf = sb("spread_bf", [3 * E, E, 128], BF16)
        kvc = [sb(f"kvc{k}", [128, 2, CH]) for k in range(4)]
        qc = two("qc", [128, 2 * CH])
        kt, vt = two("kt", [128, TPC, 128]), two("vt", [128, TPC, 132])
        num_w, den_w = two("num_w", [128, 128]), two("den_w", [128, (2 * NCH - 1) * HEADS])
        den, rec = sb("den", [128, CH]), sb("rec", [128, CH])
        rec_hi, rec_lo = two("rec_hi", [128, CH], F32R), two("rec_lo", [128, CH], F32R)
        fix = two("fix", [128, CH])
        prob, comb, rest, exl = [sb(n, [128, NT, E]) for n in ("prob", "comb", "rest", "exl")]
        top, tot = sb("top", [128, NT]), sb("tot", [128, NT])
        more, same = sb("more", [128, NT, E * E]), sb("same", [128, NT, E * E])
        parts, parts_t = sb("parts", [128, NT, 3 * E], BF16), sb("parts_t", [3 * E, HW], BF16)
        hid, scaled = two("hid", [128, CH]), two("scaled", [128, CH])
        tnh, tnl = two("tnh", [128, CH], F32R), two("tnl", [128, CH], F32R)
        eps_t, eps_a = sb("eps_t", [128, 1]), sb("eps_a", [128, 1])
        norm = Norm(nc, ctx, "d_norm", ones, rows, row_spread, [bank(i) for i in range(5)])
        const_loaded, set_done, own, small_ready, bn_in, bn_act = [sem(n) for n in
            ("const_loaded", "set_done", "own", "small_ready", "bn_in", "bn_act")]
        x2_loaded, out_stored = [sem(f"x2_loaded{p}") for p in range(NCH // 2)], sem("out_stored")
        kv_loaded, q_loaded = [sem(f"kv_loaded{k}") for k in range(4)], [sem(f"q_loaded{k}") for k in range(2)]
        turn_pe, kt_done, vt_done, kv_pe, kv_ready = [sem(n) for n in ("turn_pe", "kt_done", "vt_done", "kv_pe", "kv_ready")]
        qr_done, nd_pe, num_done, den_done, inv_done, hi_done, lo_done = [sem(n) for n in
            ("qr_done", "nd_pe", "num_done", "den_done", "inv_done", "hi_done", "lo_done")]
        cast_pe, att_done, y_pe, fix_done, x3_done = [sem(n) for n in ("cast_pe", "att_done", "y_pe", "fix_done", "x3_done")]
        logit_pe, exp_in, exp_done, parts_done, parts_pe, parts_t_done = [sem(n) for n in
            ("logit_pe", "exp_in", "exp_done", "parts_done", "parts_pe", "parts_t_done")]
        tnh_done, tnl_done, up_pe, spread_pe, hid_done, scaled_done, moe_pe, fin_done, out_done = [sem(n) for n in
            ("tnh_done", "tnl_done", "up_pe", "spread_pe", "hid_done", "scaled_done", "moe_pe", "fin_done", "out_done")]
        consts = [(ones[:, :], "ones"), (rows[:, :], "rows"), (rows32, "spread_rows"), (sel32, "head_rows"), (ident[:, :], "ident"),
                  (heads[:, :], "heads"), (head_of[:, :], "head_of"), (wp[:, :, :], "wp"), (bn[:, :], "bn"), (wr[:, :], "wr1"),
                  (before[:, :], "before"), (w1_32, "m1"), (w2[:, :, :], "m2"), (b1[:, :], "mb1"), (b2[:, :], "mb2"), (spread32, "spread")]
        LINKS = 20
        turned = ps[0:3 * E, 0:HW // 2].bitcast(BF16)
        kv_bank = lambda s: bank(5 + 2 * s)
        moe_bank = lambda k: bank(4 + 2 * k)
        tn = lambda c: chunk(TN, c)
        x = lambda c: chunk(X, c)

        with nc.Block() as block:
            @block.sync
            def _(sp):
                for dst, name in consts:
                    sp.dma_start(dst, d[name]).then_inc(const_loaded, 16)

                def source(b, s, js, c0, n):
                    t = d["agg"] if s else d["qkv"]
                    return t[bass.ds(b, 1), js, :, c0 * CH:c0 * CH + n].rearrange("a j c n -> c (a j) n")

                def load_keys(b):
                    for u in range(KVS):
                        sp.wait_ge(turn_pe, b * KVS + u + 1)
                        passed(sp)
                        sp.dma_start(kvc[u % 4][:, :, :], source(b, u // NCH, slice(1, 3), u % NCH, CH)).then_inc(kv_loaded[u % 4], 16)

                def load_queries(b, pairs):
                    for m in pairs:
                        sp.wait_ge(nd_pe, b * KVS + 2 * m + 2)
                        passed(sp)
                        sp.dma_start(qc[m % 2][:, :].unsqueeze(1), source(b, m // (NCH // 2), slice(0, 1), m % (NCH // 2) * 2, 2 * CH)).then_inc(q_loaded[m % 2], 16)

                pair = lambda t, b, p: t[bass.ds(b, 1), :, p * 2 * CH:(p + 1) * 2 * CH].rearrange("a p n -> p (a n)")
                x_pair = lambda p: X[:, p * 2 * CH:(p + 1) * 2 * CH]

                def body(b, last):
                    load_queries(b, range(2, NCH))
                    if not last:
                        load_keys(b + 1)
                        load_queries(b + 1, range(2))
                    for p in range(NCH // 2):
                        sp.wait_ge(out_done, b * NCH + 2 * p + 2 + 2)
                        passed(sp)
                        sp.dma_start(pair(d["out"], b, p), x_pair(p)).then_inc(out_stored, 16)
                        sp.wait_ge(out_stored, (b * (NCH // 2) + p) * 16 + 16)
                        if not last:
                            passed(sp)
                            sp.dma_start(x_pair(p), pair(d["x2"], b + 1, p)).then_inc(x2_loaded[p], 16)

                load_keys(0)
                load_queries(0, range(2))
                sp.wait_ge(small_ready, 1)
                for p in range(NCH // 2):
                    sp.dma_start(x_pair(p), pair(d["x2"], 0, p)).then_inc(x2_loaded[p], 16)
                with sp.Fori(0, B - 1) as b:
                    body(b, False)
                body(B - 1, True)

            @block.tensor
            def _(pe):
                pe.sem_inc(turn_pe, 4)
                pe.sem_inc(nd_pe, 4)
                pe.sem_inc(moe_pe, 2)
                pe.sem_inc(up_pe, 2 * E)
                norm.start_pe(pe)
                pe.wait_ge(const_loaded, 16 * len(consts))
                pe.wait_ge(small_ready, 1)
                passed(pe)

                def keys(b):
                    def products(u):
                        n, k, s = b * KVS + u, u % 2, u // NCH
                        pe.wait_ge(kt_done, n + 3)
                        pe.wait_ge(vt_done, n + 3)
                        for t in range(TPC):
                            last = nc.tensor.matmul(kv_bank(s)[:, 0:129], kt[k][:, t, :], vt[k][:, t, 0:129],
                                                    start=(u % NCH == 0 and t == 0), stop=(u % NCH == NCH - 1 and t == TPC - 1))
                        last.then_inc(kv_pe, 1)

                    for u in range(KVS):
                        n, k = b * KVS + u, u % 2
                        pe.wait_ge(kv_loaded[u % 4], (b * 4 + u // 4) * 16 + 16)
                        pe.wait_ge(kt_done, n + 1)
                        pe.wait_ge(vt_done, n + 1)
                        for t in range(TPC):
                            nc.tensor.transpose(bank(k)[:, t * 128:(t + 1) * 128], kvc[u % 4][:, 0, t * 128:(t + 1) * 128], ident[:, :])
                            last = nc.tensor.transpose(bank(2 + k)[:, t * 128:(t + 1) * 128], kvc[u % 4][:, 1, t * 128:(t + 1) * 128],
                                                       ident[:, :])
                        last.then_inc(turn_pe, 1)
                        if u:
                            products(u - 1)
                    products(KVS - 1)

                def queries(b):
                    for s in range(2):
                        for c in range(NCH):
                            u = s * NCH + c
                            n = b * KVS + u
                            pe.wait_ge(qr_done, n + 1)
                            pe.wait_ge(num_done, n + 1)
                            q = qc[u // 2 % 2][:, u % 2 * CH:(u % 2 + 1) * CH]
                            nc.tensor.matmul(bank(u % 2), num_w[s][:, :], q, start=True, stop=True)
                            first = (NCH - 1 - c) * HEADS
                            nc.tensor.matmul(bank(2 + s), den_w[s][:, first:first + 128], q, start=(c == 0), stop=(c == NCH - 1)).then_inc(nd_pe, 1)

                def project(b):
                    def out(c):
                        n = b * NCH + c
                        pe.wait_ge(att_done, n * 2 + 2 + 2)
                        pe.wait_ge(fix_done, n + 1)
                        for s in range(2):
                            last = nc.tensor.matmul(bank(6 + c % 2), wp[:, s, :], ATT[s][:, c * CH:(c + 1) * CH], start=(s == 0), stop=(s == 1))
                        last.then_inc(y_pe, 1)

                    for c in range(NCH):
                        for s in range(2):
                            if c == 0:
                                pe.wait_ge(lo_done, b * 2 + s + 1)
                            pe.wait_ge(att_done, (b * NCH + c) * 2 + s + 1)
                            nc.tensor.matmul(bank(4 + s), sel[:, c, :], rec_hi[s][:, :], start=True, stop=False)
                            nc.tensor.matmul(bank(4 + s), sel[:, c, :], rec_lo[s][:, :], start=False, stop=True).then_inc(cast_pe, 1)
                        if c:
                            out(c - 1)
                    out(NCH - 1)

                def experts(b):
                    with pe.Fori(0, NCH // 2) as p:
                        c0 = b * NCH + p * 2

                        def up(i):
                            k, e = i // E, i % E
                            pe.wait_ge(scaled_done, c0 * E + i + 1)
                            passed(pe)
                            nc.tensor.matmul(bank(2 + i % 2), spread_bf[:, e, :], chunk(parts_t, p * 2 + k), start=True, stop=True).then_inc(spread_pe, 1)
                            pe.wait_ge(hid_done, c0 * E + i + 1)
                            if e == 0:
                                pe.wait_ge(tnl_done, c0 + k + 1)
                            nc.tensor.matmul(bank(i % 2), w1h[:, e, :], tnh[k][:, :], start=True, stop=False)
                            nc.tensor.matmul(bank(i % 2), w1h[:, e, :], tnl[k][:, :], start=False, stop=False)
                            nc.tensor.matmul(bank(i % 2), w1l[:, e, :], tnh[k][:, :], start=False, stop=True).then_inc(up_pe, 1)

                        def down(i):
                            k, e = i // E, i % E
                            if e == 0:
                                pe.wait_ge(fin_done, c0 + k + 1)
                                passed(pe)
                                for j in range(3):
                                    nc.tensor.matmul(moe_bank(k), b2s[:, j, :], chunk(parts_t, p * 2 + k), start=(j == 0), stop=False)
                            pe.wait_ge(scaled_done, c0 * E + i + 3)
                            nc.tensor.matmul(moe_bank(k), w2[:, e, :], scaled[i % 2][:, :], start=False, stop=(e == E - 1)).then_inc(moe_pe, 1)

                        for i in range(2 * E):
                            up(i)
                            if i:
                                down(i - 1)
                        down(2 * E - 1)

                def body(b, last):
                    pe.wait_ge(kv_ready, b * 2 + 2)
                    queries(b)
                    project(b)
                    pe.wait_ge(num_done, b * KVS + KVS + 2)
                    norm.first_pe(pe, b, x, lambda c: pe.wait_ge(x3_done, b * NCH + c + 3))
                    norm.second_pe(pe, b)
                    pe.wait_ge(norm.out_done, b * NCH + NCH + 2)
                    pe.wait_ge(fix_done, b * NCH + NCH + 2)
                    for t in range(NT):
                        logit = nc.tensor.matmul(bank(6)[:, t * E:(t + 1) * E], TN[:, t * 128:(t + 1) * 128], wr[:, :], start=True, stop=True)
                    logit.then_inc(logit_pe, 1)
                    if not last:
                        keys(b + 1)
                        pe.wait_ge(kt_done, (b + 1) * KVS + KVS + 2)
                        pe.wait_ge(vt_done, (b + 1) * KVS + KVS + 2)
                    pe.wait_ge(parts_done, b + 1)
                    for t in range(NT):
                        turn = nc.tensor.transpose(turned[:, t * 128:(t + 1) * 128], parts[:, t, :], ident_bf[:, :])
                    turn.then_inc(parts_pe, 1)
                    pe.wait_ge(parts_t_done, b + 1)
                    passed(pe)
                    experts(b)
                    pe.wait_ge(hid_done, (b + 1) * NCH * E + 2)
                    pe.wait_ge(scaled_done, (b + 1) * NCH * E + 2)
                    pe.wait_ge(fin_done, (b + 1) * NCH + 2)

                keys(0)
                with pe.Fori(0, B - 1) as b:
                    body(b, False)
                body(B - 1, True)

            @block.scalar
            def _(act):
                norm.start_act(act)
                for sm in (kt_done, vt_done, num_done, fix_done, hid_done):
                    act.sem_inc(sm, 2)
                act.wait_ge(bn_in, 1)
                nc.scalar.activation(bnv[:, 0:1], bn[:, 3:4], ACT.Sqrt, bias=eps_t[:, :]).then_inc(bn_act, 1)
                act.wait_ge(small_ready, 1)

                def keys(b):
                    for u in range(KVS):
                        n, k = b * KVS + u, u % 2
                        act.wait_ge(turn_pe, n + 5)
                        if u >= 2:
                            act.wait_ge(kv_pe, n - 1)
                        elif not isinstance(b, int):
                            act.wait_ge(kv_pe, n - 1)
                        nc.scalar.activation(kt[k][:, :, :].rearrange("p t c -> p (t c)"), bank(k), ACT.Relu).then_inc(kt_done, 1)
                        nc.scalar.activation(vt[k][:, :, 0:128], bank(2 + k).rearrange("p (t c) -> p t c", c=128), ACT.Copy).then_inc(vt_done, 1)

                def body(b, last):
                    def relu(u):
                        n = b * KVS + u
                        act.wait_ge(q_loaded[u // 2 % 2], (b * (NCH // 2) + u // 4) * 16 + 16)
                        q = qc[u // 2 % 2][:, u % 2 * CH:(u % 2 + 1) * CH]
                        nc.scalar.activation(q, q, ACT.Relu).then_inc(qr_done, 1)

                    relu(0)
                    relu(1)
                    for u in range(KVS):
                        if u + 2 < KVS:
                            relu(u + 2)
                        act.wait_ge(nd_pe, b * KVS + u + 5)
                        nc.scalar.activation(ATT[u // NCH][:, u % NCH * CH:(u % NCH + 1) * CH], bank(u % 2), ACT.Copy).then_inc(num_done, 1)
                    for c in range(NCH):
                        n = b * NCH + c
                        act.wait_ge(y_pe, n + 1)
                        act.wait_ge(x3_done, n + 1)
                        if c < 2:
                            act.wait_ge(out_done, b * NCH + 2)
                        nc.scalar.activation(fix[c % 2][:, :], bank(6 + c % 2), ACT.Identity, bias=bnv[:, 3:4], scale=bnv[:, 1:2]).then_inc(fix_done, 1)
                    norm.first_act(act, b, tn, eps_t)
                    act.wait_ge(exp_in, b + 1)
                    nc.scalar.activation(exl[:, :, :], exl[:, :, :], ACT.Exp).then_inc(exp_done, 1)
                    if not last:
                        keys(b + 1)
                    with act.Fori(0, NCH) as c:
                        for e in range(E):
                            u = (b * NCH + c) * E + e
                            act.wait_ge(up_pe, u + 2 * E + 1)
                            act.wait_ge(scaled_done, u + 1)
                            nc.scalar.activation(hid[e % 2][:, :], bank(e % 2), ACT.Gelu, bias=b1[:, e:e + 1]).then_inc(hid_done, 1)

                keys(0)
                with act.Fori(0, B - 1) as b:
                    body(b, False)
                body(B - 1, True)

            @block.gpsimd
            def _(pool):
                pool.sem_inc(x3_done, 2)
                pool.sem_inc(out_done, 2)
                with pool.Fori(0, B) as b:
                    for c in range(NCH):
                        pool.wait_ge(x2_loaded[c // 2], b * 16 + 16)
                        pool.wait_ge(fix_done, b * NCH + c + 3)
                        nc.gpsimd.tensor_tensor(x(c), x(c), fix[c % 2][:, :], ALU.add).then_inc(x3_done, 1)

                    def split(c):
                        n, k = b * NCH + c, c % 2
                        pool.wait_ge(norm.out_done, b * NCH + c + 3)
                        pool.wait_ge(up_pe, n * E + E)
                        passed(pool)
                        nc.gpsimd.tensor_copy(tnh[k][:, :], tn(c)).then_inc(tnh_done, 1)
                        pool.wait_ge(tnh_done, n + 1)
                        nc.gpsimd.tensor_tensor(tnl[k][:, :], tn(c), tnh[k][:, :].bitcast(F32), ALU.subtract).then_inc(tnl_done, 1)

                    def add(c):
                        pool.wait_ge(fin_done, b * NCH + c + 3)
                        nc.gpsimd.tensor_tensor(x(c), x(c), fix[c % 2][:, :], ALU.add).then_inc(out_done, 1)

                    split(0)
                    split(1)
                    for c in range(NCH):
                        add(c)
                        if c + 2 < NCH:
                            split(c + 2)

            @block.vector
            def _(dve):
                norm.start_dve(dve)
                for sm in (att_done, scaled_done, fin_done):
                    dve.sem_inc(sm, 2)
                setup = Chain(dve, set_done)
                setup(nc.vector.memset(eps_t[:, :], EPS_T))
                setup(nc.vector.memset(eps_a[:, :], EPS_ATT))
                for k in range(2):
                    setup(nc.vector.memset(vt[k][:, :, :], 1.0))
                    setup(nc.vector.memset(den_w[k][:, :], 0.0))
                dve.wait_ge(const_loaded, 16 * len(consts))
                dve.sem_inc(bn_in, 1)
                wide = lambda t: t[:, :, :].rearrange("p e c -> p (e c)")
                setup(nc.vector.tensor_copy(wide(sel), sel32))
                setup(nc.vector.tensor_copy(wide(row_spread), rows32))
                setup(nc.vector.tensor_copy(wide(spread_bf), spread32))
                setup(nc.vector.tensor_copy(wide(w1h), w1_32))
                setup(nc.vector.tensor_tensor(wide(w1l), w1_32, wide(w1h).bitcast(F32), ALU.subtract))
                setup(nc.vector.tensor_copy(ident_bf[:, :], ident[:, :]))
                setup(nc.vector.tensor_copy(b2s[:, 0, :], b2[:, :]))
                setup(nc.vector.tensor_tensor(b2r[:, :], b2[:, :], b2s[:, 0, :], ALU.subtract))
                setup(nc.vector.tensor_copy(b2s[:, 1, :], b2r[:, :]))
                setup(nc.vector.tensor_tensor(b2r[:, :], b2r[:, :], b2s[:, 1, :], ALU.subtract))
                setup(nc.vector.tensor_copy(b2s[:, 2, :], b2r[:, :]))
                dve.wait_ge(bn_act, 1)
                setup(nc.vector.reciprocal(bnv[:, 2:3], bnv[:, 0:1]))
                setup(nc.vector.tensor_tensor(bnv[:, 1:2], bn[:, 0:1], bnv[:, 2:3], ALU.mult))
                setup(nc.vector.tensor_tensor(bnv[:, 2:3], bn[:, 2:3], bnv[:, 1:2], ALU.mult))
                setup(nc.vector.tensor_tensor(bnv[:, 3:4], bn[:, 1:2], bnv[:, 2:3], ALU.subtract))
                dve.sem_inc(small_ready, 1)

                def key_matrices(b):
                    middle = slice((NCH - 1) * HEADS, NCH * HEADS)
                    for s in range(2):
                        dve.wait_ge(kv_pe, b * KVS + (s + 1) * NCH)
                        nc.vector.tensor_tensor(num_w[s][:, :], kv_bank(s)[:, 0:128], heads[:, :], ALU.mult)
                        nc.vector.tensor_scalar(den_w[s][:, middle], head_of[:, :], kv_bank(s)[:, 128:129], None, ALU.mult).then_inc(kv_ready, 1)

                def reciprocals(b):
                    for s in range(2):
                        n = b * 2 + s
                        dve.wait_ge(nd_pe, b * KVS + (s + 1) * NCH + 4)
                        nc.vector.tensor_scalar(den[:, :], bank(2 + s), eps_a[:, :], None, ALU.add).then_inc(den_done, 1)
                        dve.wait_ge(den_done, n + 1)
                        nc.vector.reciprocal(rec[:, :], den[:, :]).then_inc(inv_done, 1)
                        dve.wait_ge(inv_done, n + 1)
                        nc.vector.tensor_copy(rec_hi[s][:, :], rec[:, :]).then_inc(hi_done, 1)
                        dve.wait_ge(hi_done, n + 1)
                        nc.vector.tensor_tensor(rec_lo[s][:, :], rec[:, :], rec_hi[s][:, :].bitcast(F32), ALU.subtract).then_inc(lo_done, 1)
                        dve.wait_ge(lo_done, n + 1)

                def weighted(b):
                    dve.wait_ge(num_done, b * KVS + KVS + 2)
                    for c in range(NCH):
                        for s in range(2):
                            a = ATT[s][:, c * CH:(c + 1) * CH]
                            dve.wait_ge(cast_pe, (b * NCH + c) * 2 + s + 1)
                            nc.vector.tensor_tensor(a, a, bank(4 + s), ALU.mult).then_inc(att_done, 1)

                def router(b):
                    link = Chain(dve, own, b * LINKS)
                    dve.wait_ge(logit_pe, b + 1)
                    logits = bank(6)[:, 0:NT * E].rearrange("p (t e) -> p t e", e=E)
                    per_e = lambda t: t[:, :].unsqueeze(2).broadcast_to([128, NT, E])
                    link(nc.vector.tensor_reduce(top[:, :], logits, AX.X, ALU.max))
                    link(nc.vector.tensor_tensor(exl[:, :, :], logits, per_e(top), ALU.subtract))
                    dve.sem_inc(exp_in, 1)
                    dve.wait_ge(exp_done, b + 1)
                    link(nc.vector.tensor_reduce(tot[:, :], exl[:, :, :], AX.X, ALU.add))
                    link(nc.vector.reciprocal(tot[:, :], tot[:, :]))
                    link(nc.vector.tensor_tensor(prob[:, :, :], exl[:, :, :], per_e(tot), ALU.mult))
                    mine = prob[:, :, :].unsqueeze(3).broadcast_to([128, NT, E, E])
                    other = prob[:, :, :].unsqueeze(2).broadcast_to([128, NT, E, E])
                    grid = lambda t: t[:, :, :].rearrange("p t (e f) -> p t e f", f=E)
                    link(nc.vector.tensor_tensor(grid(more), other, mine, ALU.is_gt))
                    link(nc.vector.tensor_tensor(grid(same), other, mine, ALU.is_equal))
                    link(nc.vector.tensor_tensor(same[:, :, :], same[:, :, :], before[:, :].unsqueeze(1).broadcast_to([128, NT, E * E]), ALU.mult))
                    link(nc.vector.tensor_tensor(more[:, :, :], more[:, :, :], same[:, :, :], ALU.add))
                    link(nc.vector.tensor_reduce(rest[:, :, :], grid(more), AX.X, ALU.add))
                    link(nc.vector.scalar_tensor_tensor(out=comb[:, :, :], in0=rest[:, :, :], scalar=1.5, in1=prob[:, :, :],
                                                        op0=ALU.is_lt, op1=ALU.mult))
                    link(nc.vector.tensor_reduce(tot[:, :], comb[:, :, :], AX.X, ALU.add))
                    link(nc.vector.tensor_scalar(tot[:, :], tot[:, :], 1e-12, None, ALU.max))
                    link(nc.vector.reciprocal(tot[:, :], tot[:, :]))
                    link(nc.vector.tensor_tensor(comb[:, :, :], comb[:, :, :], per_e(tot), ALU.mult))
                    link(nc.vector.tensor_copy(parts[:, :, 0:E], comb[:, :, :]))
                    link(nc.vector.tensor_tensor(rest[:, :, :], comb[:, :, :], parts[:, :, 0:E], ALU.subtract))
                    link(nc.vector.tensor_copy(parts[:, :, E:2 * E], rest[:, :, :]))
                    link(nc.vector.tensor_tensor(rest[:, :, :], rest[:, :, :], parts[:, :, E:2 * E], ALU.subtract))
                    link(nc.vector.tensor_copy(parts[:, :, 2 * E:3 * E], rest[:, :, :]))
                    assert link.count == LINKS
                    dve.sem_inc(parts_done, 1)

                def body(b, last):
                    reciprocals(b)
                    weighted(b)
                    norm.first_dve(dve, b, x, tn)
                    norm.between_dve(dve, b)
                    norm.second_dve(dve, b, tn)
                    router(b)
                    if not last:
                        key_matrices(b + 1)
                    dve.wait_ge(parts_pe, b + 1)
                    nc.vector.tensor_copy(parts_t[:, :], turned).then_inc(parts_t_done, 1)
                    with dve.Fori(0, NCH // 2) as p:
                        for k in range(2):
                            n = b * NCH + p * 2 + k
                            for e in range(E):
                                u = n * E + e
                                dve.wait_ge(hid_done, u + 3)
                                dve.wait_ge(spread_pe, u + 1)
                                dve.wait_ge(moe_pe, u + 1)
                                nc.vector.tensor_tensor(scaled[e % 2][:, :], hid[e % 2][:, :], bank(2 + e % 2), ALU.mult).then_inc(scaled_done, 1)
                            dve.wait_ge(moe_pe, n * E + E + 2)
                            dve.wait_ge(out_done, n + 1)
                            nc.vector.tensor_tensor(fix[k][:, :], moe_bank(k), chunk(TN, p * 2 + k), ALU.add).then_inc(fin_done, 1)

                key_matrices(0)
                with dve.Fori(0, B - 1) as b:
                    body(b, False)
                body(B - 1, True)


def build(nc, d):
    with ExitStack() as ctx:
        sb = lambda name, shape: ctx.enter_context(nc.sbuf_tensor(name, shape, F32))
        route = sb("pick", [128, B, 2, E]), sb("pickw", [128, B, 2, E]), sb("dense", [128, B, E])
        passed = passing(ctx.enter_context(nc.semaphore("passed")))
        phase_project(nc, d, passed)
        phase_dft(nc, d, passed)
        phase_mix(nc, d, passed)
        phase_route0(nc, d, route)
        phase_ffn0(nc, d, passed, route)
        phase_conv(nc, d, passed)
        phase_attention(nc, d, passed)


def shape_constants():
    import math

    import numpy as np
    f = np.float32
    i = np.arange(SIDE)
    row = PH * (i % HB) + i // HB
    cos = lambda a, b: np.cos(2 * np.pi * np.outer(a, b) / SIDE) / 8
    sin = lambda a, b: np.sin(2 * np.pi * np.outer(a, b) / SIDE) / 8
    cat = lambda *t: np.concatenate(t, 1)
    dft = cat(cos(row, i), -sin(row, i), cos(i, i), -sin(i, i), sin(i, i), cos(i, i),
              cos(i, row), sin(i, row), -sin(i, row), cos(i, row), cos(i, i), -sin(i, i))
    y, x = (i.astype(f) - SIDE // 2)[:, None], (i.astype(f) - SIDE // 2)[None, :]
    theta = (np.arctan2(y, x).astype(f) + f(math.pi)) % f(math.pi)
    radii = SIDE // 2 // 8 + 1
    ring = np.clip(np.floor(np.sqrt(y * y + x * x) / f(8)).astype(np.int32), 0, radii - 1)
    delta = math.pi / 8
    half = 1.5 * delta / 2.0
    centers = (np.arange(8, dtype=f) * f(delta) + f(delta / 2.0))[:, None, None]
    dist = np.abs(theta[None] - centers)
    w = np.clip(f(1.0) - dist / f(half), 0, None) * (dist < f(half))
    angle = w / (w.sum(0, keepdims=True) + f(1e-8))
    mask = angle[:, None] * (ring[None, None] == np.arange(radii)[None, :, None, None])
    mask = np.roll(mask, (-(SIDE // 2), -(SIDE // 2)), (2, 3)).transpose(0, 1, 3, 2).reshape(8 * radii, HW)
    e = np.arange(E)
    c = np.arange(128)
    spread = np.tile(np.repeat(np.eye(E), 128, 1), (3, 1))
    rows = np.zeros((128, 2 * NCH - 1))
    rows[:, NCH - 1] = 1 / 128
    spread_rows = np.zeros((Norm.LOW + NCH, NCH, 128))
    for k in range(NCH):
        spread_rows[[k, Norm.LOW + k], k] = 1
    head_rows = (c[:, None, None] // 16 == np.arange(NCH)[None, :, None]) & (c[:, None, None] % 16 == c[None, None, :] // 8)
    return {"ones": np.full((128, 128), 1 / 128), "rows": rows, "spread_rows": spread_rows.reshape(Norm.LOW + NCH, -1), "ident": np.eye(128), "dft": dft, "mask": mask,
            "before": np.tile((e[None, :] < e[:, None]).reshape(1, -1), (128, 1)),
            "heads": c[:, None] // 8 == c[None, :] // 8, "head_of": c[:, None] // 8 == np.arange(16)[None, :],
            "head_rows": head_rows.reshape(128, -1), "spread": spread}


def lay_out(v):
    import numpy as np
    t = lambda a: np.ascontiguousarray(a)
    a = {"x": v["x"].reshape(B, C, HB, PH, SIDE).transpose(0, 1, 3, 2, 4).reshape(B, C, HW)}
    a["w_in"], a["w_out"] = v["L0_conv_w_in"].T, v["L0_conv_w_out"].T
    a["binw"] = v["L0_conv_bin_weights"].reshape(MID, -1).T
    a["wr"], a["br"] = v["L0_ffn_Wr"], np.tile(v["L0_ffn_br"][None], (128, 1))
    a["w1"] = v["L0_ffn_W1"].transpose(1, 0, 2)
    a["w2"] = v["L0_ffn_W2"].reshape(E, 2, 128, C).transpose(2, 0, 1, 3).reshape(128, E, F0)
    a["b1"] = v["L0_ffn_b1"].reshape(E, 2, 128).transpose(2, 0, 1)
    a["b2"] = v["L0_ffn_b2"].T
    a["gb"] = np.stack([v["L0_ffn_gamma"], v["L0_ffn_beta"]], 1)
    order = (24 * np.arange(16)[None, :, None] + 8 * np.arange(3)[:, None, None] + np.arange(8)[None, None, :]).reshape(3, 128)
    a["wq"] = v["L1_conv_w_qkv"][:, :, 0, 0][order].transpose(2, 0, 1)
    flat = order.reshape(GROUPS, GC)
    wdw, wpw = v["L1_conv_w_dw"][:, 0], v["L1_conv_w_pw"][:, :, 0, 0]
    dw = np.zeros((PH, GC, GROUPS, 2, 5, PH), np.float32)
    for r in range(PH):
        for f in range(PH):
            for s in range(2):
                dy = PH * s + r - (f - 2 if f >= 2 else f + 2)
                if 0 <= dy < 5:
                    dw[r, :, :, s, :, f] = wdw[flat][:, :, dy, :].transpose(1, 0, 2)
    a["dw"] = dw.reshape(128, GROUPS, TAPS * PH)
    pw = np.zeros((GC, GROUPS, GC), np.float32)
    for ci in range(GC):
        same = np.arange(ci // 4 * 4, ci // 4 * 4 + 4)
        pw[ci][:, same] = wpw[flat[:, same], ci % 4]
    a["pw"] = np.tile(pw, (PH, 1, 1))
    a["wp"] = v["L1_conv_w_proj"][:, :, 0, 0].reshape(C, 2, 128).transpose(2, 1, 0)
    a["bn"] = np.stack([v["L1_conv_bn_" + n] for n in ("gamma", "beta", "mean", "var")], 1)
    a["wr1"] = v["L1_ffn_router_w"].T
    a["m1"], a["m2"] = v["L1_ffn_w1"].transpose(1, 0, 2), v["L1_ffn_w2"].transpose(1, 0, 2)
    a["mb1"], a["mb2"] = v["L1_ffn_b1"].T, np.tile(v["L1_ffn_b2"], (3, 1))
    return {k: t(x) for k, x in a.items()}


SCRATCH = {"s": (B, C, HW), "pm": (B, MID, HW), "xe": (B, MID, HW), "x1": (B, C, HW), "tn": (B, C, HW), "total": (C, B), "x2": (B, C, HW),
           "qkv": (B, 3, C, HW), "agg": (B, 3, C, HW)}


def kernel(**inputs):
    import numpy as np
    import concourse.bacc as bacc
    from concourse.bass_utils import run_bass_kernel_spmd

    arrays = lay_out({k: np.asarray(x) for k, x in inputs.items()})
    arrays.update({k: np.ascontiguousarray(x, dtype=np.float32) for k, x in shape_constants().items()})
    nc = bacc.Bacc("TRN2", target_bir_lowering=False, num_devices=1)
    d = {k: nc.dram_tensor("in_" + k, x.shape, F32, kind="ExternalInput").ap() for k, x in arrays.items()}
    d.update({k: nc.dram_tensor("scratch_" + k, shape, F32, kind="Internal").ap() for k, shape in SCRATCH.items()})
    d["out"] = nc.dram_tensor("out", (B, C, HW), F32, kind="ExternalOutput").ap()
    build(nc, d)
    got = run_bass_kernel_spmd(nc, [{"in_" + k: x for k, x in arrays.items()}], core_ids=[0]).results[0]["out"]
    return got.reshape(B, C, PH, HB, SIDE).transpose(0, 1, 3, 2, 4).reshape(B, C, SIDE, SIDE)
```

```python
from contextlib import ExitStack

import concourse.bass as bass
from concourse import mybir
from concourse.alu_op_type import AluOpType as ALU

F32 = mybir.dt.float32
F32R = mybir.dt.float32r
BF16 = mybir.dt.bfloat16
ACT = mybir.ActivationFunctionType
AX = mybir.AxisListType

B, C, HW, SIDE = 8, 128, 4096, 64
MID = 16
E = 8
F0 = 256
CH = 512
NCH = HW // CH
PH = 4
HB = SIDE // PH
GC = 8
GROUPS = 3 * C // GC
TAPS = 4
EPS_C, EPS_T, EPS_MAG, EPS_ATT = 1e-6, 1e-5, 1e-8, 1e-15


def chunk(buf, c):
    return buf[:, bass.ds(c * CH, CH)]


def image_part(buf, b, held=2):
    def view(c):
        r, w, f = c // 4, c // 2 % 2, c % 2
        rows = buf[:, bass.ds((b % held) * HW + (2 * r + f) * HB * SIDE, HB * SIDE)].rearrange("m (r w) -> m r w", w=SIDE)
        return rows[:, :, w * 2 * HB:(w + 1) * 2 * HB].rearrange("m r (f w) -> m f r w", f=2)
    return view


def batch_of(t, b):
    return t[bass.ds(b, 1), :, :].rearrange("a p n -> p (a n)")


class Norm:
    LOW = 32

    def __init__(self, nc, ctx, tag, passed, ones, rows, spread, banks):
        sb = lambda name, shape, dt=F32: ctx.enter_context(nc.sbuf_tensor(f"{tag}_{name}", shape, dt))
        sem = lambda name: ctx.enter_context(nc.semaphore(f"{tag}_{name}"))
        self.nc, self.passed, self.ones, self.rows, self.spread = nc, passed, ones, rows, spread
        self.mean, self.cast, self.stat = banks[0:2], banks[2:4], banks[4][0:NCH]
        self.square = [sb(f"square{k}", [128, CH]) for k in range(2)]
        self.std, self.rstd = sb("std", [NCH, CH]), sb("rstd", [NCH, CH])
        self.parts = sb("parts", [self.LOW + NCH, CH], F32R)
        self.mean_pe, self.centred, self.squared, self.var_pe = sem("mean_pe"), sem("centred"), sem("squared"), sem("var_pe")
        self.std_act, self.cast_pe, self.out_done = sem("std_act"), sem("cast_pe"), sem("out_done")
        self.inverse = sem("inverse")

    def start_pe(self, pe):
        pe.sem_inc(self.var_pe, 2)
        pe.sem_inc(self.cast_pe, 2)

    def start_act(self, act):
        act.sem_inc(self.std_act, 1)

    def start_dve(self, dve):
        for sm, n in ((self.centred, 2), (self.inverse, 3), (self.out_done, 2)):
            dve.sem_inc(sm, n)
        self.nc.vector.memset(self.parts[:, :].bitcast(F32), 0.0).then_inc(self.inverse, 1)

    def first_pe(self, pe, j, src, ready=None):
        for c in range(NCH):
            n = j * NCH + c
            if ready:
                ready(c)
            pe.wait_ge(self.centred, n + 1)
            self.nc.tensor.matmul(self.mean[c % 2], self.ones[:, :], src(c), start=True, stop=True).then_inc(self.mean_pe, 1)
            if c:
                self.variance(pe, j, c - 1)
        self.variance(pe, j, NCH - 1)

    def variance(self, pe, j, c):
        if c == 0:
            pe.wait_ge(self.std_act, j + 1)
        pe.wait_ge(self.squared, j * NCH + c + 1)
        self.nc.tensor.matmul(self.stat, self.rows[:, NCH - 1 - c:2 * NCH - 1 - c], self.square[c % 2][:, :],
                              start=(c == 0), stop=(c == NCH - 1)).then_inc(self.var_pe, 1)

    def first_act(self, act, j, out, eps):
        for c in range(NCH):
            n = j * NCH + c
            act.wait_ge(self.centred, n + 3)
            act.wait_ge(self.var_pe, n + 1)
            self.passed(act)
            self.nc.scalar.activation(self.square[c % 2][:, :], out(c), ACT.Square).then_inc(self.squared, 1)
        act.wait_ge(self.var_pe, j * NCH + NCH + 2)
        act.wait_ge(self.inverse, j * 3 + 2)
        self.nc.scalar.activation(self.std[:, :], self.stat, ACT.Sqrt, bias=eps[0:NCH, :]).then_inc(self.std_act, 1)

    def first_dve(self, dve, j, src, out):
        for c in range(NCH):
            dve.wait_ge(self.mean_pe, j * NCH + c + 1)
            self.nc.vector.tensor_tensor(out(c), src(c), self.mean[c % 2], ALU.subtract).then_inc(self.centred, 1)

    def between_dve(self, dve, j):
        dve.wait_ge(self.std_act, j + 2)
        dve.wait_ge(self.inverse, j * 3 + 4)
        self.nc.vector.reciprocal(self.rstd[:, :], self.std[:, :]).then_inc(self.inverse, 1)
        dve.wait_ge(self.inverse, j * 3 + 5)
        dve.wait_ge(self.cast_pe, j * NCH + 2)
        self.nc.vector.tensor_copy(self.parts[0:NCH, :], self.rstd[:, :]).then_inc(self.inverse, 1)
        dve.wait_ge(self.inverse, j * 3 + 6)
        self.nc.vector.tensor_tensor(self.parts[self.LOW:self.LOW + NCH, :], self.rstd[:, :],
                                     self.parts[0:NCH, :].bitcast(F32), ALU.subtract).then_inc(self.inverse, 1)

    def second_pe(self, pe, j, each=None):
        pe.wait_ge(self.inverse, j * 3 + 7)
        for c in range(NCH):
            pe.wait_ge(self.out_done, j * NCH + c + 1)
            self.nc.tensor.matmul(self.cast[c % 2], self.spread[:, c, :], self.parts[:, :], start=True, stop=True).then_inc(self.cast_pe, 1)
            if each:
                each(c)

    def second_dve(self, dve, j, out, total=None, each=None):
        dve.wait_ge(self.centred, j * NCH + NCH + 2)
        for c in range(NCH):
            dve.wait_ge(self.cast_pe, j * NCH + c + 3)
            if total is None:
                self.nc.vector.tensor_tensor(out(c), out(c), self.cast[c % 2], ALU.mult).then_inc(self.out_done, 1)
            else:
                self.nc.vector.scalar_tensor_tensor(out=out(c), in0=out(c), scalar=1.0, in1=self.cast[c % 2],
                                                    op0=ALU.mult, op1=ALU.mult, accum_out=total(c)).then_inc(self.out_done, 1)
            if each:
                each(c)


def passing(sem):
    return lambda eng: eng.sem_inc(sem, 1)


class Chain:

    def __init__(self, eng, sem, base=0):
        self.eng, self.sem, self.base, self.count = eng, sem, base, 0

    def __call__(self, ins):
        self.count += 1
        ins.then_inc(self.sem, 1)
        self.eng.wait_ge(self.sem, self.base + self.count)


def norm_consts(nc, ctx, tag):
    sb = lambda name, shape, dt=F32: ctx.enter_context(nc.sbuf_tensor(tag + name, shape, dt))
    ones, rows = sb("ones", [128, 128]), sb("rows", [128, 2 * NCH - 1])
    spread32, spread = sb("spread32", [Norm.LOW + NCH, NCH * 128]), sb("spread", [Norm.LOW + NCH, NCH, 128], F32R)
    return ones, rows, spread32, spread, [(ones[:, :], "ones"), (rows[:, :], "rows"), (spread32[:, :], "spread_rows")]


def phase_project(nc, d, passed):
    with ExitStack() as ctx:
        sb = lambda name, shape, dt=F32: ctx.enter_context(nc.sbuf_tensor("p_" + name, shape, dt))
        sem = lambda name: ctx.enter_context(nc.semaphore("p_" + name))
        banks = [ctx.enter_context(nc.psum_tensor(f"p_ps{i}", [128, CH], F32)) for i in range(7)]
        ones, rows, spread32, spread, consts = norm_consts(nc, ctx, "p_")
        w_in, eps = sb("w_in", [128, MID]), sb("eps", [128, 1])
        consts = consts + [(w_in[:, :], "w_in")]
        X, XN, PM = sb("X", [128, 3 * HW]), sb("XN", [128, 3 * HW]), sb("PM", [MID, 2 * HW])
        norm = Norm(nc, ctx, "p_norm", passed, ones, rows, spread, [t[:, :] for t in banks[0:5]])
        const_loaded, set_done, x_loaded, s_stored, pm_stored = [sem(n) for n in
            ("const_loaded", "set_done", "x_loaded", "s_stored", "pm_stored")]
        pm_pe, pm_done, s_done = sem("pm_pe"), sem("pm_done"), sem("s_done")
        half = lambda buf, b: buf[:, bass.ds((b % 2) * HW, HW)]
        third = lambda buf, b: buf[:, bass.ds((b % 3) * HW, HW)]
        x_part = lambda b: lambda c: X[:, bass.ds((b % 3) * HW + c * CH, CH)]
        xn_part = lambda b: lambda c: XN[:, bass.ds((b % 3) * HW + c * CH, CH)]

        with nc.Block() as block:
            @block.sync
            def _(sp):
                for dst, name in consts:
                    sp.dma_start(dst, d[name]).then_inc(const_loaded, 16)
                sp.sem_inc(s_stored, 48)
                sp.sem_inc(pm_stored, 32)

                def load(b):
                    sp.wait_ge(s_stored, b * 16 + 16)
                    passed(sp)
                    sp.dma_start(third(X, b), batch_of(d["x"], b)).then_inc(x_loaded, 16)

                def store(b):
                    sp.wait_ge(s_done, b * NCH + 2 * NCH)
                    sp.wait_ge(s_stored, b * 16 + 48)
                    passed(sp)
                    sp.dma_start(batch_of(d["s"], b), third(X, b)).then_inc(s_stored, 16)
                    sp.wait_ge(pm_done, b * NCH + NCH + 2)
                    passed(sp)
                    sp.wait_ge(pm_stored, b * 16 + 32)
                    passed(sp)
                    sp.dma_start(batch_of(d["pm"], b), half(PM, b)).then_inc(pm_stored, 16)

                load(0)
                for b in (1, 2):
                    sp.wait_ge(x_loaded, b * 16)
                    load(b)
                with sp.Fori(3, B) as b:
                    sp.wait_ge(x_loaded, b * 16)
                    store(b - 3)
                    load(b)
                store(B - 3)
                store(B - 2)
                store(B - 1)
                sp.wait_ge(s_stored, B * 16 + 48)
                sp.wait_ge(pm_stored, B * 16 + 32)

            @block.tensor
            def _(pe):
                pe.wait_ge(const_loaded, 16 * len(consts))
                norm.start_pe(pe)
                pe.sem_inc(pm_pe, NCH)
                pe.wait_ge(set_done, 2)

                def first(b):
                    pe.wait_ge(x_loaded, b * 16 + 16)
                    norm.first_pe(pe, b, x_part(b))

                def second(b):
                    def project(c):
                        n = b * NCH + c
                        pe.wait_ge(norm.out_done, n + 3)
                        pe.wait_ge(pm_done, n + 1)
                        nc.tensor.matmul(banks[5 + c % 2][0:MID, :], w_in[:, :], xn_part(b)(c), start=True, stop=True).then_inc(pm_pe, 1)

                    norm.second_pe(pe, b, lambda c: project(c - 1) if c else None)
                    project(NCH - 1)

                first(0)
                with pe.Fori(1, B) as b:
                    first(b)
                    second(b - 1)
                second(B - 1)

            @block.scalar
            def _(act):
                norm.start_act(act)
                act.sem_inc(pm_done, 2)
                act.wait_ge(set_done, 2)

                def read(b):
                    for c in range(NCH):
                        act.wait_ge(pm_pe, b * NCH + c + 1 + NCH)
                        if c == 0:
                            act.wait_ge(pm_stored, b * 16 + 16)
                        passed(act)
                        nc.scalar.activation(image_part(PM, b)(c), banks[5 + c % 2][0:MID, :].rearrange("m (f r w) -> m f r w", f=2, w=HB), ACT.Copy).then_inc(pm_done, 1)

                norm.first_act(act, 0, xn_part(0), eps)
                with act.Fori(1, B) as b:
                    norm.first_act(act, b, xn_part(b), eps)
                    read(b - 1)
                read(B - 1)

            @block.gpsimd
            def _(pool):
                pool.sem_inc(s_done, NCH)
                with pool.Fori(0, B) as b:
                    for c in range(NCH):
                        pool.wait_ge(norm.out_done, b * NCH + c + 3)
                        nc.gpsimd.tensor_tensor(x_part(b)(c), x_part(b)(c), xn_part(b)(c), ALU.add).then_inc(s_done, 1)

            @block.vector
            def _(dve):
                norm.start_dve(dve)
                nc.vector.memset(eps[:, :], EPS_C).then_inc(set_done, 1)
                dve.wait_ge(const_loaded, 16 * len(consts))
                nc.vector.tensor_copy(spread[:, :, :].rearrange("p c n -> p (c n)"), spread32[:, :]).then_inc(set_done, 1)

                def first(b):
                    dve.wait_ge(x_loaded, b * 16 + 16)
                    if not isinstance(b, int):
                        dve.wait_ge(s_done, (b - 1) * NCH)
                        dve.wait_ge(pm_pe, (b - 1) * NCH)
                    norm.first_dve(dve, b, x_part(b), xn_part(b))

                first(0)
                norm.between_dve(dve, 0)
                dve.wait_ge(x_loaded, 32)
                norm.first_dve(dve, 1, x_part(1), xn_part(1))
                norm.second_dve(dve, 0, xn_part(0))
                norm.between_dve(dve, 1)
                with dve.Fori(2, B) as b:
                    first(b)
                    norm.second_dve(dve, b - 1, xn_part(b - 1))
                    norm.between_dve(dve, b)
                norm.second_dve(dve, B - 1, xn_part(B - 1))


def phase_dft(nc, d, passed):
    with ExitStack() as ctx:
        sb = lambda name, shape: ctx.enter_context(nc.sbuf_tensor("a_" + name, shape, F32))
        sem = lambda name: ctx.enter_context(nc.semaphore("a_" + name))
        ps = ctx.enter_context(nc.psum_tensor("a_ps", [128, 8 * CH], F32))
        low, high = ps[:, 0:4 * CH], ps[:, 4 * CH:8 * CH]
        dft = sb("dft", [128, 12 * SIDE])
        mask, binw = sb("mask", [40, HW]), sb("binw", [40, MID])
        gain = sb("gain", [128, MID, SIDE])
        proj, image = sb("proj", [128, MID, SIDE]), sb("image", [128, MID, SIDE])
        rows, enh, back, sqz = [sb(n, [128, MID, 128]) for n in ("rows", "enh", "back", "sqz")]
        r2, mag, zero, den, rec, num, fac, shifted = [sb(n, [128, MID, SIDE]) for n in
                                                      ("r2", "mag", "zero", "den", "rec", "num", "fac", "shifted")]
        g1, g2a, g2b, g3a, g3b = [(i * 128, i * 128 + 128) for i in range(5)]
        g4a, g4b = (640, 704), (704, 768)
        const_loaded, gain_pe, gain_ready, pm_loaded, xe_stored = [sem(n) for n in
            ("const_loaded", "gain_pe", "gain_ready", "pm_loaded", "xe_stored")]
        rows_pe, rows_ready, freq_pe, sqz_done, r2_done, mag_done, enh_ready = [sem(n) for n in
            ("rows_pe", "rows_ready", "freq_pe", "sqz_done", "r2_done", "mag_done", "enh_ready")]
        back_pe, back_ready, image_pe, image_ready, own = [sem(n) for n in ("back_pe", "back_ready", "image_pe", "image_ready", "own")]
        flat = lambda t: t[:, :, :].rearrange("p m k -> p (m k)")
        STEPS = B // 2

        with nc.Block() as block:
            @block.sync
            def _(sp):
                for h in range(2):
                    sp.dma_start(dft[h * SIDE:(h + 1) * SIDE, :], d["dft"]).then_inc(const_loaded, 16)
                sp.dma_start(mask[:, :], d["mask"]).then_inc(const_loaded, 16)
                sp.dma_start(binw[:, :], d["binw"]).then_inc(const_loaded, 16)
                sp.sem_inc(xe_stored, 32)

                def load(i):
                    for h in range(2):
                        sp.dma_start(proj[h * SIDE:(h + 1) * SIDE, :, :],
                                     d["pm"][bass.ds(i * 2 + h, 1), :, :].rearrange("a m (h w) -> h (a m) w", w=SIDE)).then_inc(pm_loaded, 16)

                def store(i):
                    sp.wait_ge(image_ready, i + 3)
                    for h in range(2):
                        sp.dma_start(d["xe"][bass.ds(i * 2 + h, 1), :, :].rearrange("a m (h w) -> h (a m) w", w=SIDE),
                                     image[h * SIDE:(h + 1) * SIDE, :, :]).then_inc(xe_stored, 16)

                load(0)
                with sp.Fori(0, STEPS - 1) as i:
                    sp.wait_ge(rows_pe, i + 1)
                    load(i + 1)
                    store(i)
                store(STEPS - 1)
                sp.wait_ge(xe_stored, STEPS * 32 + 32)

            @block.tensor
            def _(pe):
                pe.sem_inc(back_pe, 1)
                pe.wait_ge(const_loaded, 64)

                def stage(dst, width, src, tables):
                    for m in range(MID):
                        for q, (g, first) in enumerate(tables):
                            for h in range(2):
                                on = slice(h * SIDE, (h + 1) * SIDE)
                                last = nc.tensor.matmul(dst[on, m * width:(m + 1) * width], src[on, m, first:first + SIDE],
                                                        dft[on, g[0]:g[1]], start=(q == 0), stop=(q == len(tables) - 1))
                    return last

                def by_rows(i):
                    pe.wait_ge(pm_loaded, i * 32 + 32)
                    pe.wait_ge(image_ready, i + 1)
                    passed(pe)
                    stage(low, 128, proj, [(g1, 0)]).then_inc(rows_pe, 1)

                def by_columns(i):
                    pe.wait_ge(rows_ready, i + 1)
                    pe.wait_ge(enh_ready, i + 1)
                    passed(pe)
                    stage(high, 128, rows, [(g2a, 0), (g2b, SIDE)]).then_inc(freq_pe, 1)

                def inverse(i):
                    pe.wait_ge(enh_ready, i + 2)
                    pe.wait_ge(image_ready, i + 2)
                    passed(pe)
                    stage(low, 128, enh, [(g3a, 0), (g3b, SIDE)]).then_inc(back_pe, 1)
                    pe.wait_ge(back_ready, i + 1)
                    passed(pe)
                    stage(low, SIDE, back, [(g4a, 0), (g4b, SIDE)]).then_inc(image_pe, 1)

                by_rows(0)
                for h in range(2):
                    for kx in range(SIDE):
                        last = nc.tensor.matmul(high[h * SIDE:(h + 1) * SIDE, kx * MID:(kx + 1) * MID],
                                                mask[:, kx * SIDE:(kx + 1) * SIDE], binw[:, :], start=True, stop=True)
                last.then_inc(gain_pe, 1)
                pe.wait_ge(gain_ready, 1)
                by_columns(0)
                with pe.Fori(0, STEPS - 1) as i:
                    by_rows(i + 1)
                    by_columns(i + 1)
                    inverse(i)
                inverse(STEPS - 1)

            @block.scalar
            def _(act):
                act.sem_inc(image_ready, 2)

                def forward(i):
                    act.wait_ge(rows_pe, i + 1)
                    nc.scalar.activation(flat(rows), low, ACT.Copy).then_inc(rows_ready, 1)
                    act.wait_ge(freq_pe, i + 1)
                    nc.scalar.activation(flat(sqz), high, ACT.Square).then_inc(sqz_done, 1)
                    act.wait_ge(r2_done, i + 1)
                    nc.scalar.activation(flat(mag), flat(r2), ACT.Sqrt).then_inc(mag_done, 1)

                def inverse(i):
                    act.wait_ge(back_pe, i + 2)
                    nc.scalar.activation(flat(back), low, ACT.Copy).then_inc(back_ready, 1)
                    act.wait_ge(image_pe, i + 1)
                    act.wait_ge(xe_stored, i * 32 + 32)
                    nc.scalar.activation(flat(image), low[:, 0:SIDE * MID], ACT.Copy).then_inc(image_ready, 1)

                forward(0)
                with act.Fori(0, STEPS - 1) as i:
                    forward(i + 1)
                    inverse(i)
                inverse(STEPS - 1)

            @block.vector
            def _(dve):
                dve.sem_inc(enh_ready, 1)
                dve.wait_ge(gain_pe, 1)
                nc.vector.tensor_copy(gain[:, :, :], high[:, 0:SIDE * MID].rearrange("p (x m) -> p m x", m=MID)).then_inc(gain_ready, 1)
                dve.wait_ge(gain_ready, 1)
                with dve.Fori(0, STEPS) as i:
                    link = Chain(dve, own, i * 8)
                    dve.wait_ge(sqz_done, i + 1)
                    nc.vector.tensor_tensor(r2[:, :, :], sqz[:, :, 0:SIDE], sqz[:, :, SIDE:128], ALU.add).then_inc(r2_done, 1)
                    dve.wait_ge(mag_done, i + 1)
                    link(nc.vector.tensor_scalar(flat(zero), flat(mag), 0.0, None, ALU.is_equal))
                    link(nc.vector.tensor_tensor(flat(den), flat(mag), flat(zero), ALU.add))
                    link(nc.vector.reciprocal(flat(rec), flat(den)))
                    link(nc.vector.scalar_tensor_tensor(out=flat(num), in0=flat(mag), scalar=EPS_MAG, in1=flat(gain),
                                                        op0=ALU.add, op1=ALU.mult))
                    link(nc.vector.tensor_tensor(flat(fac), flat(num), flat(rec), ALU.mult))
                    z = high.rearrange("p (m k) -> p m k", k=128)
                    link(nc.vector.tensor_tensor(shifted[:, :, :], z[:, :, 0:SIDE], zero[:, :, :], ALU.add))
                    dve.wait_ge(back_pe, i + 1)
                    link(nc.vector.tensor_tensor(enh[:, :, 0:SIDE], shifted[:, :, :], fac[:, :, :], ALU.mult))
                    link(nc.vector.tensor_tensor(enh[:, :, SIDE:128], z[:, :, SIDE:128], fac[:, :, :], ALU.mult))
                    dve.sem_inc(enh_ready, 1)


def phase_mix(nc, d, passed):
    with ExitStack() as ctx:
        sb = lambda name, shape: ctx.enter_context(nc.sbuf_tensor("m_" + name, shape, F32))
        sem = lambda name: ctx.enter_context(nc.semaphore("m_" + name))
        banks = [ctx.enter_context(nc.psum_tensor(f"m_ps{i}", [128, CH], F32)) for i in range(7)]
        ones, rows, spread32, spread, consts = norm_consts(nc, ctx, "m_")
        w_out, eps = sb("w_out", [MID, 128]), sb("eps", [128, 1])
        consts = consts + [(w_out[:, :], "w_out")]
        X, TN, XE = sb("X", [128, 3 * HW]), sb("TN", [128, 3 * HW]), sb("XE", [MID, 3 * HW])
        sums, total = sb("sums", [128, B * NCH]), sb("total", [128, B])
        norm = Norm(nc, ctx, "m_norm", passed, ones, rows, spread, [t[:, :] for t in banks[0:5]])
        const_loaded, set_done, loaded, x1_stored, tn_stored = [sem(n) for n in
            ("const_loaded", "set_done", "loaded", "x1_stored", "tn_stored")]
        y_pe, x1_done, total_done, total_stored = sem("y_pe"), sem("x1_done"), sem("total_done"), sem("total_stored")
        third = lambda buf, b: buf[:, bass.ds((b % 3) * HW, HW)]
        x_part = lambda b: lambda c: X[:, bass.ds((b % 3) * HW + c * CH, CH)]
        part = lambda buf, b: lambda c: buf[:, bass.ds((b % 3) * HW + c * CH, CH)]

        with nc.Block() as block:
            @block.sync
            def _(sp):
                for dst, name in consts:
                    sp.dma_start(dst, d[name]).then_inc(const_loaded, 16)
                sp.sem_inc(tn_stored, 48)

                def load(b):
                    sp.dma_start(third(X, b), batch_of(d["s"], b)).then_inc(loaded, 16)
                    sp.dma_start(third(XE, b), batch_of(d["xe"], b)).then_inc(loaded, 16)

                def store_x1(b):
                    sp.wait_ge(x1_done, b * NCH + NCH + 2)
                    passed(sp)
                    sp.dma_start(batch_of(d["x1"], b), third(X, b)).then_inc(x1_stored, 16)

                def store_tn(b):
                    sp.wait_ge(norm.out_done, b * NCH + NCH + 2)
                    sp.wait_ge(tn_stored, b * 16 + 48)
                    passed(sp)
                    sp.dma_start(batch_of(d["tn"], b), third(TN, b)).then_inc(tn_stored, 16)

                def next_load(b):
                    sp.wait_ge(x1_stored, b * 16 + 16)
                    sp.wait_ge(norm.centred, b * NCH + NCH + 2)
                    sp.wait_ge(loaded, b * 32 + 96)
                    passed(sp)
                    load(b + 3)

                load(0)
                for b in (1, 2):
                    sp.wait_ge(loaded, b * 32)
                    load(b)
                store_x1(0)
                next_load(0)
                with sp.Fori(1, B - 3) as b:
                    store_x1(b)
                    store_tn(b - 1)
                    next_load(b)
                for b in range(B - 3, B):
                    sp.wait_ge(x1_stored, b * 16)
                    store_x1(b)
                    store_tn(b - 1)
                store_tn(B - 1)
                sp.wait_ge(total_done, 1)
                sp.dma_start(d["total"], total[:, :]).then_inc(total_stored, 16)
                sp.wait_ge(x1_stored, B * 16)
                sp.wait_ge(tn_stored, B * 16 + 48)
                sp.wait_ge(total_stored, 16)

            @block.tensor
            def _(pe):
                pe.wait_ge(const_loaded, 16 * len(consts))
                norm.start_pe(pe)
                pe.wait_ge(set_done, 2)

                def first(b):
                    def mix(c):
                        pe.wait_ge(x1_done, b * NCH + c + 1)
                        passed(pe)
                        nc.tensor.matmul(banks[5 + c % 2][:, :], w_out[:, :], image_part(XE, b, 3)(c), start=True, stop=True).then_inc(y_pe, 1)

                    def ready(c):
                        if c + 1 < NCH:
                            mix(c + 1)
                        pe.wait_ge(x1_done, b * NCH + c + 3)

                    pe.wait_ge(loaded, b * 32 + 32)
                    mix(0)
                    norm.first_pe(pe, b, x_part(b), ready)

                first(0)
                with pe.Fori(1, B) as b:
                    first(b)
                    norm.second_pe(pe, b - 1)
                norm.second_pe(pe, B - 1)

            @block.scalar
            def _(act):
                norm.start_act(act)
                act.wait_ge(set_done, 2)
                with act.Fori(0, B) as b:
                    norm.first_act(act, b, part(TN, b), eps)

            @block.vector
            def _(dve):
                norm.start_dve(dve)
                dve.sem_inc(x1_done, 2)
                nc.vector.memset(eps[:, :], EPS_T).then_inc(set_done, 1)
                dve.wait_ge(const_loaded, 16 * len(consts))
                nc.vector.tensor_copy(spread[:, :, :].rearrange("p c n -> p (c n)"), spread32[:, :]).then_inc(set_done, 1)

                def first(b):
                    def add(c):
                        dve.wait_ge(y_pe, b * NCH + c + 1)
                        nc.vector.tensor_tensor(x_part(b)(c), x_part(b)(c), banks[5 + c % 2][:, :], ALU.add).then_inc(x1_done, 1)

                    def centre(c):
                        dve.wait_ge(norm.mean_pe, b * NCH + c + 1)
                        nc.vector.tensor_tensor(part(TN, b)(c), x_part(b)(c), norm.mean[c % 2], ALU.subtract).then_inc(norm.centred, 1)

                    dve.wait_ge(loaded, b * 32 + 32)
                    dve.wait_ge(tn_stored, b * 16 + 16)
                    add(0)
                    for c in range(1, NCH):
                        add(c)
                        centre(c - 1)
                    centre(NCH - 1)

                def second(b):
                    norm.second_dve(dve, b, part(TN, b), lambda c: sums[:, bass.ds(b * NCH + c, 1)])

                first(0)
                norm.between_dve(dve, 0)
                with dve.Fori(1, B) as b:
                    first(b)
                    second(b - 1)
                    norm.between_dve(dve, b)
                second(B - 1)
                dve.wait_ge(norm.out_done, B * NCH + 2)
                nc.vector.tensor_reduce(total[:, :], sums[:, :].rearrange("p (b c) -> p b c", c=NCH), AX.X, ALU.add).then_inc(total_done, 1)


def phase_route0(nc, d, route):
    pick, pickw, dense = route
    with ExitStack() as ctx:
        sb = lambda name, shape: ctx.enter_context(nc.sbuf_tensor("r_" + name, shape, F32))
        sem = lambda name: ctx.enter_context(nc.semaphore("r_" + name))
        total, wide = sb("total", [128, B]), sb("wide", [128, B, 128])
        wr, br, before = sb("wr", [128, E]), sb("br", [128, E]), sb("before", [128, E * E])
        logit, ex, rw, sel = [sb(n, [128, B, E]) for n in ("logit", "ex", "rw", "sel")]
        top, low = sb("top", [128, B]), sb("low", [128, B])
        load, scale = sb("load", [128, E]), sb("scale", [128, E])
        more, same, rank = sb("more", [128, B, E, E]), sb("same", [128, B, E, E]), sb("rank", [128, B, E])
        ps = ctx.enter_context(nc.psum_tensor("r_ps", [128, B * E], F32))
        loaded, wide_ready, logit_pe, own, exp_in, exp_done = [sem(n) for n in
                                                              ("loaded", "wide_ready", "logit_pe", "own", "exp_in", "exp_done")]
        per_e = lambda t: t[:, :].unsqueeze(2).broadcast_to([128, B, E])
        per_b = lambda t: t[:, :].unsqueeze(1).broadcast_to([128, B, E])
        with nc.Block() as block:
            @block.sync
            def _(sp):
                for dst, name in ((total, "total"), (wr, "wr"), (br, "br"), (before, "before")):
                    sp.dma_start(dst[:, :], d[name]).then_inc(loaded, 16)

            @block.tensor
            def _(pe):
                pe.wait_ge(wide_ready, 1)
                for b in range(B):
                    last = nc.tensor.matmul(ps[:, b * E:(b + 1) * E], wide[:, b, :], wr[:, :], start=True, stop=True)
                last.then_inc(logit_pe, 1)

            @block.scalar
            def _(act):
                for i in range(3):
                    act.wait_ge(exp_in, i + 1)
                    nc.scalar.activation(ex[:, :, :], ex[:, :, :], ACT.Exp).then_inc(exp_done, 1)

            @block.vector
            def _(dve):
                link = Chain(dve, own)
                dve.wait_ge(loaded, 64)
                nc.vector.tensor_copy(wide[:, :, :], total[:, :].unsqueeze(2).broadcast_to([128, B, 128])).then_inc(wide_ready, 1)
                dve.wait_ge(logit_pe, 1)
                link(nc.vector.scalar_tensor_tensor(out=logit[:, :, :], in0=ps[:, :].rearrange("p (b e) -> p b e", e=E), scalar=1.0 / HW,
                                                    in1=per_b(br), op0=ALU.mult, op1=ALU.add))

                def softmax(src, dst, i):
                    link(nc.vector.tensor_reduce(top[:, :], src[:, :, :], AX.X, ALU.max))
                    link(nc.vector.tensor_tensor(ex[:, :, :], src[:, :, :], per_e(top), ALU.subtract))
                    dve.sem_inc(exp_in, 1)
                    dve.wait_ge(exp_done, i + 1)
                    if dst is not None:
                        link(nc.vector.tensor_reduce(low[:, :], ex[:, :, :], AX.X, ALU.add))
                        link(nc.vector.reciprocal(low[:, :], low[:, :]))
                        link(nc.vector.tensor_tensor(dst[:, :, :], ex[:, :, :], per_e(low), ALU.mult))

                softmax(logit, rw, 0)
                link(nc.vector.tensor_reduce(load[:, :], rw[:, :, :].rearrange("p b e -> p e b"), AX.X, ALU.add))
                link(nc.vector.tensor_scalar(load[:, :], load[:, :], float(HW), None, ALU.mult))
                link(nc.vector.reciprocal(load[:, :], load[:, :]))
                link(nc.vector.tensor_scalar(scale[:, :], load[:, :], float(-(-B * HW * 5 // (4 * E))), 1.0, ALU.mult, ALU.min))
                link(nc.vector.tensor_tensor(logit[:, :, :], rw[:, :, :], per_b(scale), ALU.mult))
                softmax(logit, rw, 1)
                mine = rw[:, :, :].unsqueeze(3).broadcast_to([128, B, E, E])
                other = rw[:, :, :].unsqueeze(2).broadcast_to([128, B, E, E])
                first = before[:, :].rearrange("p (e f) -> p e f", f=E)
                link(nc.vector.tensor_tensor(more[:, :, :, :], other, mine, ALU.is_gt))
                link(nc.vector.tensor_tensor(same[:, :, :, :], other, mine, ALU.is_equal))
                for b in range(B):
                    link(nc.vector.tensor_tensor(same[:, b, :, :], same[:, b, :, :], first, ALU.mult))
                link(nc.vector.tensor_tensor(more[:, :, :, :], more[:, :, :, :], same[:, :, :, :], ALU.add))
                link(nc.vector.tensor_reduce(rank[:, :, :], more[:, :, :, :], AX.X, ALU.add))
                softmax(rw, None, 2)
                link(nc.vector.tensor_scalar(sel[:, :, :], rank[:, :, :], 1.5, None, ALU.is_lt))
                link(nc.vector.tensor_tensor(ex[:, :, :], ex[:, :, :], sel[:, :, :], ALU.mult))
                link(nc.vector.tensor_reduce(low[:, :], ex[:, :, :], AX.X, ALU.add))
                link(nc.vector.reciprocal(low[:, :], low[:, :]))
                link(nc.vector.tensor_tensor(dense[:, :, :], ex[:, :, :], per_e(low), ALU.mult))
                for j in range(2):
                    link(nc.vector.tensor_scalar(pick[:, :, j, :], rank[:, :, :], float(j), None, ALU.is_equal))
                    link(nc.vector.tensor_tensor(pickw[:, :, j, :], pick[:, :, j, :], dense[:, :, :], ALU.mult))


def phase_ffn0(nc, d, passed, route):
    pick, pickw, dense = route
    UPS = 2 * F0 // 128
    with ExitStack() as ctx:
        sb = lambda name, shape, dt=F32: ctx.enter_context(nc.sbuf_tensor("b_" + name, shape, dt))
        two = lambda name, shape, dt=F32: [sb(f"{name}{k}", shape, dt) for k in range(2)]
        sem = lambda name: ctx.enter_context(nc.semaphore("b_" + name))
        banks = [ctx.enter_context(nc.psum_tensor(f"b_ps{i}", [128, CH], F32)) for i in range(8)]
        ones, rows, spread32, spread, consts = norm_consts(nc, ctx, "b_")
        w1, w2 = sb("w1", [128, E, F0 + 2]), sb("w2", [128, E, F0 + 1])
        w1s, w2s, b2s = sb("w1s", [128, 2, F0 + 2]), sb("w2s", [128, 2, F0 + 1]), sb("b2s", [128, 1])
        w1h, w1l = sb("w1h", [128, 2, F0], F32R), sb("w1l", [128, 2, F0], F32R)
        wq, wqh, wql = sb("wq", [128, 3, 128]), sb("wqh", [128, 3, 128], F32R), sb("wql", [128, 3, 128], F32R)
        gb = sb("gb", [128, 2])
        X, TN = sb("X", [128, 2 * HW]), sb("TN", [128, 2 * HW])
        tnh, tnl = two("tnh", [128, CH], F32R), two("tnl", [128, CH], F32R)
        xh, xl = two("xh", [128, CH], F32R), two("xl", [128, CH], F32R)
        hid = [two(f"hid{i}", [128, CH]) for i in range(UPS)]
        qkv = two("qkv", [128, 3, CH])
        eps_c, eps_t = sb("eps_c", [128, 1]), sb("eps_t", [128, 1])
        norm = Norm(nc, ctx, "b_norm", passed, ones, rows, spread, [t[:, :] for t in banks[0:5]])
        const_loaded, set_done, x_loaded, x2_stored = [sem(n) for n in ("const_loaded", "set_done", "x_loaded", "x2_stored")]
        tn_loaded, qkv_stored = [sem(f"tn_loaded{k}") for k in range(2)], [sem(f"qkv_stored{k}") for k in range(2)]
        chosen, tnh_done, tnl_done, up_pe, hid_done, y_pe, z_done = [sem(n) for n in
            ("chosen", "tnh_done", "tnl_done", "up_pe", "hid_done", "y_pe", "z_done")]
        affine_done, x2_done, xh_done, xl_done, qkv_pe, copied = [sem(n) for n in
            ("affine_done", "x2_done", "xh_done", "xl_done", "qkv_pe", "copied")]
        consts = consts + [(wq[:, :, :], "wq"), (w1[:, :, :], "w1"), (w2[:, :, :], "w2"), (gb[:, :], "gb")]
        SETS = 5
        CHOICES = 4 * E + 3
        half = lambda buf, b: buf[:, bass.ds((b % 2) * HW, HW)]
        part = lambda buf, b: lambda c: buf[:, bass.ds((b % 2) * HW + c * CH, CH)]
        hid_bank = lambda i: banks[(5, 6, 0, 1)[i]][:, :]
        y_bank = lambda c: banks[(3, 7)[c % 2]][:, :]
        qkv_bank = lambda v: banks[(0, 1, 5, 6)[v % 4]][:, :]
        piece = range(NCH // 2), range(NCH // 2, NCH)

        with nc.Block() as block:
            @block.sync
            def _(sp):
                for dst, name in consts:
                    sp.dma_start(dst, d[name]).then_inc(const_loaded, 16)
                sp.sem_inc(x2_stored, 32)
                sp.sem_inc(qkv_stored[0], 16)
                sp.sem_inc(qkv_stored[1], 16)

                def load(b):
                    for k in range(2):
                        dst = TN[:, bass.ds((b % 2) * HW + k * (HW // 2), HW // 2)]
                        src = d["tn"][bass.ds(b, 1), :, k * (HW // 2):(k + 1) * (HW // 2)].rearrange("a p n -> p (a n)")
                        sp.dma_start(dst, src).then_inc(tn_loaded[k], 16)
                    sp.wait_ge(x2_stored, b * 16 + 16)
                    passed(sp)
                    sp.dma_start(half(X, b), batch_of(d["x1"], b)).then_inc(x_loaded, 16)

                def body(b, more):
                    sp.wait_ge(x2_done, b * NCH + NCH)
                    sp.wait_ge(x2_stored, b * 16 + 32)
                    passed(sp)
                    sp.dma_start(batch_of(d["x2"], b), half(X, b)).then_inc(x2_stored, 16)
                    for c in range(NCH):
                        n = b * NCH + c
                        sp.wait_ge(copied, n * 3 + 3 + 4)
                        passed(sp)
                        dst = d["qkv"][bass.ds(b, 1), :, c // 2, :, c % 2 * CH:(c % 2 + 1) * CH].rearrange("a j c n -> c (a j) n")
                        sp.dma_start(dst, qkv[c % 2][:, :, :]).then_inc(qkv_stored[c % 2], 16)
                    if more:
                        sp.wait_ge(x_loaded, b * 16 + 32)
                        for k in range(2):
                            sp.wait_ge(tn_loaded[k], b * 16 + 32)
                        passed(sp)
                        load(b + 2)

                load(0)
                sp.wait_ge(x_loaded, 16)
                for k in range(2):
                    sp.wait_ge(tn_loaded[k], 16)
                load(1)
                with sp.Fori(0, B - 2) as b:
                    body(b, True)
                body(B - 2, False)
                body(B - 1, False)
                sp.wait_ge(x2_stored, B * 16 + 32)
                for k in range(2):
                    sp.wait_ge(qkv_stored[k], B * NCH // 2 * 16 + 16)

            @block.tensor
            def _(pe):
                pe.sem_inc(up_pe, 2 * UPS)
                pe.sem_inc(y_pe, 2)
                pe.sem_inc(qkv_pe, 6)
                norm.start_pe(pe)
                pe.wait_ge(const_loaded, 16 * len(consts))
                pe.wait_ge(set_done, SETS)

                def experts(b, cs):
                    def up(c, i):
                        n, k = b * NCH + c, c % 2
                        if i == 0:
                            pe.wait_ge(tnl_done, n + 1)
                        pe.wait_ge(hid_done, n * UPS + i + 1)
                        at = lambda w: w[:, i // 2, (i % 2) * 128:(i % 2 + 1) * 128]
                        nc.tensor.matmul(hid_bank(i), at(w1h), tnh[k][:, :], start=True, stop=False)
                        nc.tensor.matmul(hid_bank(i), at(w1h), tnl[k][:, :], start=False, stop=False)
                        nc.tensor.matmul(hid_bank(i), at(w1l), tnh[k][:, :], start=False, stop=True).then_inc(up_pe, 1)

                    def down(c, i):
                        n, k = b * NCH + c, c % 2
                        if i == 0:
                            pe.wait_ge(z_done, n + 1)
                        pe.wait_ge(hid_done, n * UPS + i + 5)
                        last = nc.tensor.matmul(y_bank(c), w2s[:, i // 2, (i % 2) * 128:(i % 2 + 1) * 128], hid[i][k][:, :],
                                                start=(i == 0), stop=(i == UPS - 1))
                        if i == UPS - 1:
                            last.then_inc(y_pe, 1)

                    pe.wait_ge(chosen, b * CHOICES + CHOICES)
                    for c in cs:
                        for i in range(UPS):
                            up(c, i)
                            if c > cs[0] and i % 2:
                                down(c - 1, i - 1)
                                down(c - 1, i)
                    for i in range(UPS):
                        down(cs[-1], i)
                    pe.wait_ge(z_done, b * NCH + cs[-1] - 1 + 3)

                def qkv_products(b):
                    def products(c):
                        n, k = b * NCH + c, c % 2
                        pe.wait_ge(xl_done, n + 1)
                        for j in range(3):
                            bank = qkv_bank(c * 3 + j)
                            pe.wait_ge(copied, n * 3 + j + 1)
                            nc.tensor.matmul(bank, wqh[:, j, :], xh[k][:, :], start=True, stop=False)
                            nc.tensor.matmul(bank, wqh[:, j, :], xl[k][:, :], start=False, stop=False)
                            nc.tensor.matmul(bank, wql[:, j, :], xh[k][:, :], start=False, stop=True).then_inc(qkv_pe, 1)

                    norm.second_pe(pe, b * 2 + 1, lambda c: products(c - 2) if c >= 2 else None)
                    products(NCH - 2)
                    products(NCH - 1)

                def body(b, more):
                    pe.wait_ge(copied, b * 24 + 2)
                    norm.first_pe(pe, b * 2, part(TN, b), lambda c: pe.wait_ge(z_done, b * NCH + c + 3))
                    pe.wait_ge(copied, b * 24 + 4)
                    if more:
                        experts(b + 1, piece[0])
                    norm.second_pe(pe, b * 2)
                    norm.first_pe(pe, b * 2 + 1, part(X, b), lambda c: pe.wait_ge(x2_done, b * NCH + c + 1))
                    if more:
                        experts(b + 1, piece[1])
                    qkv_products(b)

                for cs in piece:
                    experts(0, cs)
                with pe.Fori(0, B - 1) as b:
                    body(b, True)
                body(B - 1, False)

            @block.scalar
            def _(act):
                act.sem_inc(hid_done, UPS)
                act.sem_inc(copied, 4)
                norm.start_act(act)
                act.wait_ge(set_done, SETS)

                def experts(b, cs):
                    for c in cs:
                        n, k = b * NCH + c, c % 2
                        act.wait_ge(y_pe, n + 1)
                        for i in range(UPS):
                            act.wait_ge(up_pe, n * UPS + i + 9)
                            nc.scalar.activation(hid[i][k][:, :], hid_bank(i), ACT.Gelu,
                                                 bias=w1s[:, i // 2, F0 + i % 2:F0 + i % 2 + 1]).then_inc(hid_done, 1)

                def high(b, c):
                    n = b * NCH + c
                    act.wait_ge(norm.out_done, b * 2 * NCH + NCH + c + 3)
                    act.wait_ge(qkv_pe, n * 3 + 3)
                    passed(act)
                    nc.scalar.activation(xh[c % 2][:, :], part(TN, b)(c), ACT.Copy).then_inc(xh_done, 1)

                def body(b, more):
                    tn = part(TN, b)
                    norm.first_act(act, b * 2, tn, eps_t)
                    if more:
                        experts(b + 1, piece[0])
                    for c in range(NCH):
                        act.wait_ge(norm.out_done, b * 2 * NCH + c + 3)
                        passed(act)
                        nc.scalar.activation(tn(c), tn(c), ACT.Identity, bias=gb[:, 1:2], scale=gb[:, 0:1]).then_inc(affine_done, 1)
                    norm.first_act(act, b * 2 + 1, tn, eps_c)
                    if more:
                        experts(b + 1, piece[1])
                    high(b, 0)
                    high(b, 1)
                    for c in range(NCH):
                        n = b * NCH + c
                        act.wait_ge(qkv_stored[c % 2], (b * (NCH // 2) + c // 2) * 16 + 16)
                        for j in range(3):
                            act.wait_ge(qkv_pe, n * 3 + j + 7)
                            nc.scalar.activation(qkv[c % 2][:, j, :], qkv_bank(c * 3 + j), ACT.Copy).then_inc(copied, 1)
                        if c + 2 < NCH:
                            high(b, c + 2)

                for cs in piece:
                    experts(0, cs)
                with act.Fori(0, B - 1) as b:
                    body(b, True)
                body(B - 1, False)

            @block.gpsimd
            def _(pool):
                def split(b, c):
                    n, k, tn = b * NCH + c, c % 2, part(TN, b)
                    pool.wait_ge(tn_loaded[c // (NCH // 2)], b * 16 + 16)
                    pool.wait_ge(up_pe, n * UPS + UPS)
                    passed(pool)
                    nc.gpsimd.tensor_copy(tnh[k][:, :], tn(c)).then_inc(tnh_done, 1)
                    pool.wait_ge(tnh_done, n + 1)
                    passed(pool)
                    nc.gpsimd.tensor_tensor(tnl[k][:, :], tn(c), tnh[k][:, :].bitcast(F32), ALU.subtract).then_inc(tnl_done, 1)

                def body(b, more):
                    tn, x = part(TN, b), part(X, b)
                    if more:
                        for c in range(6):
                            split(b + 1, c)
                    pool.wait_ge(x_loaded, b * 16 + 16)
                    for c in range(NCH):
                        pool.wait_ge(affine_done, b * NCH + c + 1)
                        passed(pool)
                        nc.gpsimd.tensor_tensor(x(c), x(c), tn(c), ALU.add).then_inc(x2_done, 1)
                    if more:
                        for c in range(6, NCH):
                            split(b + 1, c)
                    for c in range(NCH):
                        pool.wait_ge(xh_done, b * NCH + c + 1)
                        passed(pool)
                        nc.gpsimd.tensor_tensor(xl[c % 2][:, :], tn(c), xh[c % 2][:, :].bitcast(F32), ALU.subtract).then_inc(xl_done, 1)

                for c in range(NCH):
                    split(0, c)
                with pool.Fori(0, B - 1) as b:
                    body(b, True)
                body(B - 1, False)

            @block.vector
            def _(dve):
                norm.start_dve(dve)
                dve.sem_inc(z_done, 2)
                nc.vector.memset(eps_c[:, :], EPS_C).then_inc(set_done, 1)
                nc.vector.memset(eps_t[:, :], EPS_T).then_inc(set_done, 1)
                dve.wait_ge(const_loaded, 16 * len(consts))
                flat = lambda t: t[:, :, :].rearrange("p c n -> p (c n)")
                nc.vector.tensor_copy(flat(spread), spread32[:, :]).then_inc(set_done, 1)
                nc.vector.tensor_copy(flat(wqh), flat(wq)).then_inc(set_done, 1)
                dve.wait_ge(set_done, 4)
                nc.vector.tensor_tensor(flat(wql), flat(wq), flat(wqh).bitcast(F32), ALU.subtract).then_inc(set_done, 1)
                picks = pick[:, :, :, :].rearrange("p b j e -> p (b j e)")
                pickws = pickw[:, :, :, :].rearrange("p b j e -> p (b j e)")

                def choose(b, e):
                    if e:
                        dve.wait_ge(chosen, b * CHOICES + 4 * e)
                    for j in range(2):
                        for dst, src, by in ((w1s, w1, picks), (w2s, w2, pickws)):
                            f = by[:, bass.ds(b * 2 * E + j * E + e, 1)]
                            if e:
                                nc.vector.scalar_tensor_tensor(out=dst[:, j, :], in0=src[:, e, :], scalar=f, in1=dst[:, j, :],
                                                               op0=ALU.mult, op1=ALU.add).then_inc(chosen, 1)
                            else:
                                nc.vector.tensor_scalar(dst[:, j, :], src[:, e, :], f, None, ALU.mult).then_inc(chosen, 1)
                    if e < E - 1:
                        return
                    dve.wait_ge(chosen, b * CHOICES + 4 * E)
                    nc.vector.tensor_tensor(b2s[:, :], w2s[:, 0, F0:F0 + 1], w2s[:, 1, F0:F0 + 1], ALU.add).then_inc(chosen, 1)
                    nc.vector.tensor_copy(w1h[:, :, :], w1s[:, :, 0:F0]).then_inc(chosen, 1)
                    dve.wait_ge(chosen, b * CHOICES + 4 * E + 2)
                    nc.vector.tensor_tensor(w1l[:, :, :], w1s[:, :, 0:F0], w1h[:, :, :].bitcast(F32), ALU.subtract).then_inc(chosen, 1)

                def experts(b, cs):
                    for c in cs:
                        dve.wait_ge(y_pe, b * NCH + c + 3)
                        nc.vector.scalar_tensor_tensor(out=part(TN, b)(c), in0=y_bank(c), scalar=b2s[:, :], in1=part(TN, b)(c),
                                                       op0=ALU.add, op1=ALU.add).then_inc(z_done, 1)

                def body(b, more, choice):
                    tn, x = part(TN, b), part(X, b)
                    for q, src in enumerate((tn, x)):
                        norm.first_dve(dve, b * 2 + q, src, tn)
                        norm.between_dve(dve, b * 2 + q)
                        if more:
                            experts(b + 1, piece[q])
                        norm.second_dve(dve, b * 2 + q, tn, each=(lambda c: choose(b + 2, c)) if choice and q else None)

                for e in range(E):
                    choose(0, e)
                for cs in piece:
                    experts(0, cs)
                for e in range(E):
                    choose(1, e)
                with dve.Fori(0, B - 2) as b:
                    body(b, True, True)
                body(B - 2, True, False)
                body(B - 1, False, False)


def phase_conv(nc, d, passed):
    OUT, OUTW = HB + 1, HB + 2
    HALF = B // 2
    with ExitStack() as ctx:
        sb = lambda name, shape, dt=F32: ctx.enter_context(nc.sbuf_tensor("c_" + name, shape, dt))
        two = lambda name, shape, dt=F32: [sb(f"{name}{k}", shape, dt) for k in range(2)]
        sem = lambda name: ctx.enter_context(nc.semaphore("c_" + name))
        ps = ctx.enter_context(nc.psum_tensor("c_ps", [128, B * CH], F32))
        pw, dw = sb("pw", [128, GROUPS, GC]), sb("dw", [128, GROUPS, TAPS * PH * PH])
        prod = sb("prod", [128, TAPS, 128])
        w_hi, w_lo = two("w_hi", [128, TAPS, 128], F32R), two("w_lo", [128, TAPS, 128], F32R)
        P, out = two("P", [128, B, HB * HB]), two("out", [128, B, HB * HB])
        p_hi, p_lo = two("p_hi", [128, B, HB + 2, OUTW + 2], F32R), two("p_lo", [128, B, HB + 2, OUTW + 2], F32R)
        const_loaded, cleared, prod_done, whi_done, wlo_done = [sem(n) for n in
            ("const_loaded", "cleared", "prod_done", "whi_done", "wlo_done")]
        hi_done, lo_done, half_pe, read_act, read_dve = [sem(n) for n in ("hi_done", "lo_done", "half_pe", "read_act", "read_dve")]
        loaded = [sem(f"loaded{k}") for k in range(2)]
        stored = [sem(f"stored{k}") for k in range(2)]
        flat = lambda t: t[:, :, :].rearrange("p a b -> p (a b)")
        inner = lambda t: t[:, :, 1:1 + HB, 1:1 + HB]
        blocks = lambda t: t[:, :, :].rearrange("p b (r w) -> p b r w", w=HB)
        on = lambda q: slice(q * GC * PH, (q + 1) * GC * PH)
        U = GROUPS // 2

        with nc.Block() as block:
            @block.sync
            def _(sp):
                sp.dma_start(pw[:, :, :], d["pw"]).then_inc(const_loaded, 16)
                sp.dma_start(dw[:, :, :], d["dw"]).then_inc(const_loaded, 16)
                for k in range(2):
                    sp.sem_inc(stored[k], 64)

                def of_group(t, g, q):
                    per_j = C // GC
                    return t[:, bass.ds(g // per_j, 1), q, bass.ds((g % per_j) * GC, GC), :].rearrange("b j c (f n) -> (j c f) b n", f=PH)

                def load(g, k):
                    sp.wait_ge(lo_done, g + 1)
                    passed(sp)
                    for q in range(4):
                        sp.dma_start(P[k][on(q), :, :], of_group(d["qkv"], g, q)).then_inc(loaded[k], 16)

                def store(g, k):
                    sp.wait_ge(read_act, g * 2 + 2 + 2)
                    sp.wait_ge(read_dve, g * 2 + 2 + 2)
                    passed(sp)
                    for q in range(4):
                        sp.dma_start(of_group(d["agg"], g, q), out[k][on(q), :, :]).then_inc(stored[k], 16)

                load(0, 0)
                load(1, 1)
                with sp.Fori(0, U - 1) as u:
                    for k in range(2):
                        load(u * 2 + k + 2, k)
                        store(u * 2 + k, k)
                for k in range(2):
                    store(2 * U - 2 + k, k)
                for k in range(2):
                    sp.wait_ge(stored[k], U * 64 + 64)

            def read(eng, copy, done, quadrants, g, u, k):
                eng.wait_ge(stored[k], u * 64 + 64)
                for h in range(2):
                    eng.wait_ge(half_pe, g * 2 + h + 1 + 4)
                    for q in quadrants:
                        r, w = q // 2, q % 2
                        bank = ps[on(q), h * HALF * CH:(h + 1) * HALF * CH].rearrange("p (b x) -> p b x", x=CH)
                        window = bank[:, :, 0:OUT * OUTW].rearrange("p b (r w) -> p b r w", w=OUTW)[:, :, r:r + HB, w:w + HB]
                        last = copy(out[k][on(q), h * HALF:(h + 1) * HALF, :].rearrange("p b (r w) -> p b r w", w=HB), window)
                    last.then_inc(done, 1)

            @block.scalar
            def _(act):
                act.sem_inc(read_act, 2)
                act.wait_ge(cleared, 4)

                def high(g, u, k):
                    act.wait_ge(loaded[k], u * 64 + 64)
                    act.wait_ge(half_pe, g * 2 + 2)
                    nc.scalar.activation(inner(p_hi[k]), blocks(P[k]), ACT.Copy).then_inc(hi_done, 1)

                copy = lambda dst, src: nc.scalar.activation(dst, src, ACT.Copy)
                high(0, 0, 0)
                with act.Fori(0, U - 1) as u:
                    high(u * 2 + 1, u, 1)
                    read(act, copy, read_act, (0, 1), u * 2, u, 0)
                    high(u * 2 + 2, u + 1, 0)
                    read(act, copy, read_act, (0, 1), u * 2 + 1, u, 1)
                high(2 * U - 1, U - 1, 1)
                read(act, copy, read_act, (0, 1), 2 * U - 2, U - 1, 0)
                read(act, copy, read_act, (0, 1), 2 * U - 1, U - 1, 1)

            @block.gpsimd
            def _(pool):
                for k in range(2):
                    nc.gpsimd.memset(p_hi[k][:, :, :, :].bitcast(F32), 0.0).then_inc(cleared, 1)
                    nc.gpsimd.memset(p_lo[k][:, :, :, :].bitcast(F32), 0.0).then_inc(cleared, 1)
                pool.wait_ge(const_loaded, 32)

                def weights(g, k):
                    shape = [128, TAPS * 4, GC, PH]
                    taps = dw[:, bass.ds(g, 1), :].rearrange("p a (t f) -> p (a t) f", f=PH).unsqueeze(2).broadcast_to(shape)
                    mix = pw[:, bass.ds(g, 1), :].rearrange("p a c -> p (a c)").unsqueeze(1).unsqueeze(3).broadcast_to(shape)
                    if not isinstance(g, int):
                        pool.wait_ge(half_pe, g * 2 + 2)
                        passed(pool)
                    nc.gpsimd.tensor_tensor(prod[:, :, :].rearrange("p t (q c f) -> p (t q) c f", c=GC, f=PH), taps, mix, ALU.mult).then_inc(prod_done, 1)
                    pool.wait_ge(prod_done, g + 1)
                    passed(pool)
                    nc.gpsimd.tensor_copy(flat(w_hi[k]), flat(prod)).then_inc(whi_done, 1)
                    pool.wait_ge(whi_done, g + 1)
                    nc.gpsimd.tensor_tensor(flat(w_lo[k]), flat(prod), flat(w_hi[k]).bitcast(F32), ALU.subtract).then_inc(wlo_done, 1)
                    pool.wait_ge(wlo_done, g + 1)

                weights(0, 0)
                weights(1, 1)
                with pool.Fori(1, U) as u:
                    for k in range(2):
                        weights(u * 2 + k, k)

            @block.tensor
            def _(pe):
                pe.sem_inc(half_pe, 4)
                with pe.Fori(0, U) as u:
                    for k in range(2):
                        g = u * 2 + k
                        pe.wait_ge(wlo_done, g + 1)
                        pe.wait_ge(lo_done, g + 3)
                        for b in range(B):
                            if b % HALF == 0:
                                pe.wait_ge(read_act, g * 2 + b // HALF + 1)
                                pe.wait_ge(read_dve, g * 2 + b // HALF + 1)
                            passes = [(w, src, t) for w, src in ((w_hi, p_hi), (w_hi, p_lo), (w_lo, p_hi)) for t in range(TAPS)]
                            for i, (w, src, t) in enumerate(passes):
                                r, x = t // 2, t % 2
                                last = nc.tensor.matmul(ps[:, b * CH:b * CH + OUT * OUTW], w[k][:, t, :], src[k][:, b, r:r + OUT, x:x + OUTW],
                                                        start=(i == 0), stop=(i == len(passes) - 1))
                            if b % HALF == HALF - 1:
                                last.then_inc(half_pe, 1)

            @block.vector
            def _(dve):
                dve.sem_inc(lo_done, 2)
                dve.sem_inc(read_dve, 2)
                copy = lambda dst, src: nc.vector.tensor_copy(dst, src)

                def low(g, k):
                    dve.wait_ge(hi_done, g + 1)
                    nc.vector.tensor_tensor(inner(p_lo[k]), blocks(P[k]), inner(p_hi[k]).bitcast(F32), ALU.subtract).then_inc(lo_done, 1)

                low(0, 0)
                with dve.Fori(0, U - 1) as u:
                    low(u * 2 + 1, 1)
                    read(dve, copy, read_dve, (2, 3), u * 2, u, 0)
                    low(u * 2 + 2, 0)
                    read(dve, copy, read_dve, (2, 3), u * 2 + 1, u, 1)
                low(2 * U - 1, 1)
                read(dve, copy, read_dve, (2, 3), 2 * U - 2, U - 1, 0)
                read(dve, copy, read_dve, (2, 3), 2 * U - 1, U - 1, 1)


def phase_attention(nc, d, passed):
    TPC = CH // 128
    NT = HW // 128
    HEADS = 16
    KVS = 2 * NCH
    EARLY, LATE = range(3), range(3, KVS)
    with ExitStack() as ctx:
        sb = lambda name, shape, dt=F32: ctx.enter_context(nc.sbuf_tensor("d_" + name, shape, dt))
        two = lambda name, shape, dt=F32: [sb(f"{name}{k}", shape, dt) for k in range(2)]
        sem = lambda name: ctx.enter_context(nc.semaphore("d_" + name))
        ps = ctx.enter_context(nc.psum_tensor("d_ps", [128, 8 * CH], F32))
        bank = lambda i: ps[:, i * CH:(i + 1) * CH]
        X, TN, ATT1 = sb("X", [128, HW]), sb("TN", [128, HW]), sb("ATT1", [128, HW])
        ATT = [TN, ATT1]
        sel32, w1_32 = X[:, 0:NCH * 128], X[:, 1024:1024 + E * 128]
        rows32, spread32 = X[0:Norm.LOW + NCH, 2048:2048 + NCH * 128], X[0:3 * E, 3072:3072 + E * 128]
        ones, ident, rows = sb("ones", [128, 128]), sb("ident", [128, 128]), sb("rows", [128, 2 * NCH - 1])
        heads, head_of = sb("heads", [128, 128]), sb("head_of", [128, HEADS])
        ident_bf = sb("ident_bf", [128, 128], BF16)
        sel, row_spread = sb("sel", [128, NCH, 128], F32R), sb("row_spread", [Norm.LOW + NCH, NCH, 128], F32R)
        wp, bn, bnv = sb("wp", [128, 2, 128]), sb("bn", [128, 4]), sb("bnv", [128, 4])
        wr, before = sb("wr", [128, E]), sb("before", [128, E * E])
        w1h, w1l = sb("w1h", [128, E, 128], F32R), sb("w1l", [128, E, 128], F32R)
        w2, b1 = sb("w2", [128, E, 128]), sb("b1", [128, E])
        b2, b2r = sb("b2", [3 * E, 128]), sb("b2r", [3 * E, 128])
        b2s = sb("b2s", [3 * E, 3, 128], BF16)
        spread_bf = sb("spread_bf", [3 * E, E, 128], BF16)
        kvc = [sb(f"kvc{k}", [128, 2, CH]) for k in range(4)]
        qc = [sb(f"qc{k}", [128, 2 * CH]) for k in range(4)]
        kt, vt = two("kt", [128, TPC, 128]), two("vt", [128, TPC, 132])
        num_w, den_w = two("num_w", [128, 128]), two("den_w", [128, (2 * NCH - 1) * HEADS])
        den, rec = sb("den", [128, CH]), sb("rec", [128, CH])
        rec_hi, rec_lo = two("rec_hi", [128, CH], F32R), two("rec_lo", [128, CH], F32R)
        fix = two("fix", [128, CH])
        prob, comb, rest, exl = [sb(n, [128, NT, E]) for n in ("prob", "comb", "rest", "exl")]
        top, tot = sb("top", [128, NT]), sb("tot", [128, NT])
        more, same = sb("more", [128, NT, E * E]), sb("same", [128, NT, E * E])
        parts, parts_t = sb("parts", [128, NT, 3 * E], BF16), sb("parts_t", [3 * E, HW], BF16)
        hid, scaled = two("hid", [128, CH]), two("scaled", [128, CH])
        tnh, tnl = two("tnh", [128, CH], F32R), two("tnl", [128, CH], F32R)
        eps_t, eps_a = sb("eps_t", [128, 1]), sb("eps_a", [128, 1])
        norm = Norm(nc, ctx, "d_norm", passed, ones, rows, row_spread, [bank(i) for i in range(5)])
        const_loaded, set_done, own, small_ready, bn_in, bn_act = [sem(n) for n in
            ("const_loaded", "set_done", "own", "small_ready", "bn_in", "bn_act")]
        x2_loaded, out_stored = [sem(f"x2_loaded{p}") for p in range(NCH // 2)], sem("out_stored")
        kv_loaded, q_loaded = [sem(f"kv_loaded{k}") for k in range(4)], [sem(f"q_loaded{k}") for k in range(4)]
        turn_pe, kt_done, vt_done, kv_pe, kv_ready = [sem(n) for n in ("turn_pe", "kt_done", "vt_done", "kv_pe", "kv_ready")]
        qr_done, nd_pe, num_done, rec_own, lo_done = [sem(n) for n in ("qr_done", "nd_pe", "num_done", "rec_own", "lo_done")]
        cast_pe, att_done, y_pe, fix_done, x3_done = [sem(n) for n in ("cast_pe", "att_done", "y_pe", "fix_done", "x3_done")]
        logit_pe, exp_in, exp_done, parts_done, parts_pe, parts_t_done = [sem(n) for n in
            ("logit_pe", "exp_in", "exp_done", "parts_done", "parts_pe", "parts_t_done")]
        tnh_done, tnl_done, up_pe, spread_pe, hid_done, scaled_done, moe_pe, fin_done, out_done = [sem(n) for n in
            ("tnh_done", "tnl_done", "up_pe", "spread_pe", "hid_done", "scaled_done", "moe_pe", "fin_done", "out_done")]
        consts = [(ones[:, :], "ones"), (rows[:, :], "rows"), (rows32, "spread_rows"), (sel32, "head_rows"), (ident[:, :], "ident"),
                  (heads[:, :], "heads"), (head_of[:, :], "head_of"), (wp[:, :, :], "wp"), (bn[:, :], "bn"), (wr[:, :], "wr1"),
                  (before[:, :], "before"), (w1_32, "m1"), (w2[:, :, :], "m2"), (b1[:, :], "mb1"), (b2[:, :], "mb2"), (spread32, "spread")]
        LINKS = 20
        turned = ps[0:3 * E, 0:HW // 2].bitcast(BF16)
        kv_bank = lambda s: bank(5 + 2 * s)
        moe_bank = lambda k: bank(4 + 2 * k)
        tn = lambda c: chunk(TN, c)
        x = lambda c: chunk(X, c)

        with nc.Block() as block:
            @block.sync
            def _(sp):
                for dst, name in consts:
                    sp.dma_start(dst, d[name]).then_inc(const_loaded, 16)

                def source(b, s, js, c0, n):
                    t = d["agg"] if s else d["qkv"]
                    return t[bass.ds(b, 1), js, c0 // 2, :, c0 % 2 * CH:c0 % 2 * CH + n].rearrange("a j c n -> c (a j) n")

                def load_keys(b):
                    for u in range(KVS):
                        sp.wait_ge(turn_pe, b * KVS + u + 1)
                        passed(sp)
                        sp.dma_start(kvc[u % 4][:, :, :], source(b, u // NCH, slice(1, 3), u % NCH, CH)).then_inc(kv_loaded[u % 4], 16)

                def load_queries(b, pairs):
                    for m in pairs:
                        sp.wait_ge(nd_pe, b * KVS + 2 * m + 2)
                        passed(sp)
                        sp.dma_start(qc[m % 4][:, :].unsqueeze(1), source(b, m // (NCH // 2), slice(0, 1), m % (NCH // 2) * 2, 2 * CH)).then_inc(q_loaded[m % 4], 16)

                pair = lambda t, b, p: t[bass.ds(b, 1), :, p * 2 * CH:(p + 1) * 2 * CH].rearrange("a p n -> p (a n)")
                x_pair = lambda p: X[:, p * 2 * CH:(p + 1) * 2 * CH]

                def body(b, last):
                    load_queries(b, range(4, NCH))
                    if not last:
                        load_keys(b + 1)
                        load_queries(b + 1, range(4))
                    for p in range(NCH // 2):
                        sp.wait_ge(out_done, b * NCH + 2 * p + 2 + 2)
                        passed(sp)
                        sp.dma_start(pair(d["out"], b, p), x_pair(p)).then_inc(out_stored, 16)
                        sp.wait_ge(out_stored, (b * (NCH // 2) + p) * 16 + 16)
                        if not last:
                            passed(sp)
                            sp.dma_start(x_pair(p), pair(d["x2"], b + 1, p)).then_inc(x2_loaded[p], 16)

                load_keys(0)
                load_queries(0, range(4))
                sp.wait_ge(small_ready, 1)
                for p in range(NCH // 2):
                    sp.dma_start(x_pair(p), pair(d["x2"], 0, p)).then_inc(x2_loaded[p], 16)
                with sp.Fori(0, B - 1) as b:
                    body(b, False)
                body(B - 1, True)

            @block.tensor
            def _(pe):
                pe.sem_inc(turn_pe, 4)
                pe.sem_inc(nd_pe, 8)
                pe.sem_inc(moe_pe, 2)
                pe.sem_inc(up_pe, 2 * E)
                norm.start_pe(pe)
                pe.wait_ge(const_loaded, 16 * len(consts))
                pe.wait_ge(small_ready, 1)
                passed(pe)

                def keys(b, units):
                    def products(u):
                        n, k, s = b * KVS + u, u % 2, u // NCH
                        pe.wait_ge(kt_done, n + 3)
                        pe.wait_ge(vt_done, n + 3)
                        for t in range(TPC):
                            last = nc.tensor.matmul(kv_bank(s)[:, 0:129], kt[k][:, t, :], vt[k][:, t, 0:129],
                                                    start=(u % NCH == 0 and t == 0), stop=(u % NCH == NCH - 1 and t == TPC - 1))
                        last.then_inc(kv_pe, 1)

                    for u in units:
                        n, k = b * KVS + u, u % 2
                        pe.wait_ge(kv_loaded[u % 4], (b * 4 + u // 4) * 16 + 16)
                        pe.wait_ge(kt_done, n + 1)
                        pe.wait_ge(vt_done, n + 1)
                        for t in range(TPC):
                            nc.tensor.transpose(bank(k)[:, t * 128:(t + 1) * 128], kvc[u % 4][:, 0, t * 128:(t + 1) * 128], ident[:, :])
                            last = nc.tensor.transpose(bank(2 + k)[:, t * 128:(t + 1) * 128], kvc[u % 4][:, 1, t * 128:(t + 1) * 128],
                                                       ident[:, :])
                        last.then_inc(turn_pe, 1)
                        if u > units[0]:
                            products(u - 1)
                    products(units[-1])

                def queries(b):
                    for s in range(2):
                        for c in range(NCH):
                            u = s * NCH + c
                            n = b * KVS + u
                            pe.wait_ge(qr_done, n + 1)
                            pe.wait_ge(num_done, n + 1)
                            q = qc[u // 2 % 4][:, u % 2 * CH:(u % 2 + 1) * CH]
                            nc.tensor.matmul(bank(u % 2), num_w[s][:, :], q, start=True, stop=True)
                            first = (NCH - 1 - c) * HEADS
                            nc.tensor.matmul(bank(2 + s), den_w[s][:, first:first + 128], q, start=(c == 0), stop=(c == NCH - 1)).then_inc(nd_pe, 1)

                def project(b):
                    def out(c):
                        n = b * NCH + c
                        pe.wait_ge(att_done, n * 2 + 2 + 2)
                        pe.wait_ge(fix_done, n + 1)
                        for s in range(2):
                            last = nc.tensor.matmul(bank(6 + c % 2), wp[:, s, :], ATT[s][:, c * CH:(c + 1) * CH], start=(s == 0), stop=(s == 1))
                        last.then_inc(y_pe, 1)

                    for c in range(NCH):
                        for s in range(2):
                            if c == 0:
                                pe.wait_ge(lo_done, b * 2 + s + 1)
                            pe.wait_ge(att_done, (b * NCH + c) * 2 + s + 1)
                            nc.tensor.matmul(bank(4 + s), sel[:, c, :], rec_hi[s][:, :], start=True, stop=False)
                            nc.tensor.matmul(bank(4 + s), sel[:, c, :], rec_lo[s][:, :], start=False, stop=True).then_inc(cast_pe, 1)
                        if c:
                            out(c - 1)
                    out(NCH - 1)

                def experts(b):
                    def up(i):
                        c, e, u = i // E, i % E, b * NCH * E + i
                        pe.wait_ge(scaled_done, u + 1)
                        passed(pe)
                        nc.tensor.matmul(bank(2 + i % 2), spread_bf[:, e, :], chunk(parts_t, c), start=True, stop=True).then_inc(spread_pe, 1)
                        pe.wait_ge(hid_done, u + 1)
                        if e == 0:
                            pe.wait_ge(tnl_done, b * NCH + c + 1)
                        h, l = tnh[c % 2][:, :], tnl[c % 2][:, :]
                        nc.tensor.matmul(bank(i % 2), w1h[:, e, :], h, start=True, stop=False)
                        nc.tensor.matmul(bank(i % 2), w1h[:, e, :], l, start=False, stop=False)
                        nc.tensor.matmul(bank(i % 2), w1l[:, e, :], h, start=False, stop=True).then_inc(up_pe, 1)

                    def down(i):
                        c, e, u = i // E, i % E, b * NCH * E + i
                        if e == 0:
                            pe.wait_ge(fin_done, b * NCH + c + 1)
                            passed(pe)
                            for j in range(3):
                                nc.tensor.matmul(moe_bank(c % 2), b2s[:, j, :], chunk(parts_t, c), start=(j == 0), stop=False)
                        pe.wait_ge(scaled_done, u + 3)
                        nc.tensor.matmul(moe_bank(c % 2), w2[:, e, :], scaled[i % 2][:, :], start=False, stop=(e == E - 1)).then_inc(moe_pe, 1)

                    for i in range(NCH * E):
                        up(i)
                        if i >= 2:
                            down(i - 2)
                    down(NCH * E - 2)
                    down(NCH * E - 1)

                def body(b, last):
                    pe.wait_ge(kv_ready, b * 2 + 2)
                    queries(b)
                    project(b)
                    pe.wait_ge(num_done, b * KVS + KVS + 2)
                    norm.first_pe(pe, b, x, lambda c: pe.wait_ge(x3_done, b * NCH + c + 3))
                    if not last:
                        keys(b + 1, EARLY)
                        pe.wait_ge(kt_done, (b + 1) * KVS + EARLY[-1] + 3)
                        pe.wait_ge(vt_done, (b + 1) * KVS + EARLY[-1] + 3)
                    pe.wait_ge(fix_done, b * NCH + NCH + 2)

                    def logits(c):
                        pe.wait_ge(norm.out_done, b * NCH + c + 3)
                        for t in range(c * TPC, (c + 1) * TPC):
                            last_logit = nc.tensor.matmul(bank(6)[:, t * E:(t + 1) * E], TN[:, t * 128:(t + 1) * 128], wr[:, :], start=True, stop=True)
                        last_logit.then_inc(logit_pe, 1)

                    norm.second_pe(pe, b, lambda c: logits(c - 2) if c >= 2 else None)
                    logits(NCH - 2)
                    logits(NCH - 1)
                    if not last:
                        keys(b + 1, LATE)
                        pe.wait_ge(kt_done, (b + 1) * KVS + KVS + 2)
                        pe.wait_ge(vt_done, (b + 1) * KVS + KVS + 2)
                    pe.wait_ge(parts_done, b + 1)
                    for t in range(NT):
                        turn = nc.tensor.transpose(turned[:, t * 128:(t + 1) * 128], parts[:, t, :], ident_bf[:, :])
                    turn.then_inc(parts_pe, 1)
                    pe.wait_ge(parts_t_done, b + 1)
                    passed(pe)
                    experts(b)
                    pe.wait_ge(hid_done, (b + 1) * NCH * E + 2)
                    pe.wait_ge(scaled_done, (b + 1) * NCH * E + 2)
                    pe.wait_ge(fin_done, (b + 1) * NCH + 2)

                keys(0, range(KVS))
                with pe.Fori(0, B - 1) as b:
                    body(b, False)
                body(B - 1, True)

            @block.scalar
            def _(act):
                norm.start_act(act)
                for sm in (kt_done, vt_done, num_done, fix_done, hid_done):
                    act.sem_inc(sm, 2)
                act.wait_ge(bn_in, 1)
                nc.scalar.activation(bnv[:, 0:1], bn[:, 3:4], ACT.Sqrt, bias=eps_t[:, :]).then_inc(bn_act, 1)
                act.wait_ge(small_ready, 1)

                def keys(b, units):
                    for u in units:
                        n, k = b * KVS + u, u % 2
                        act.wait_ge(turn_pe, n + 5)
                        if u >= 2:
                            act.wait_ge(kv_pe, n - 1)
                        elif not isinstance(b, int):
                            act.wait_ge(kv_pe, n - 1)
                        nc.scalar.activation(kt[k][:, :, :].rearrange("p t c -> p (t c)"), bank(k), ACT.Relu).then_inc(kt_done, 1)
                        nc.scalar.activation(vt[k][:, :, 0:128], bank(2 + k).rearrange("p (t c) -> p t c", c=128), ACT.Copy).then_inc(vt_done, 1)

                def body(b, last):
                    def relu(u):
                        n = b * KVS + u
                        act.wait_ge(q_loaded[u // 2 % 4], (b * 2 + u // 8) * 16 + 16)
                        q = qc[u // 2 % 4][:, u % 2 * CH:(u % 2 + 1) * CH]
                        nc.scalar.activation(q, q, ACT.Relu).then_inc(qr_done, 1)

                    relu(0)
                    relu(1)
                    for u in range(KVS):
                        if u + 2 < KVS:
                            relu(u + 2)
                        act.wait_ge(nd_pe, b * KVS + u + 9)
                        nc.scalar.activation(ATT[u // NCH][:, u % NCH * CH:(u % NCH + 1) * CH], bank(u % 2), ACT.Copy).then_inc(num_done, 1)
                    for c in range(NCH):
                        n = b * NCH + c
                        act.wait_ge(y_pe, n + 1)
                        act.wait_ge(x3_done, n + 1)
                        if c < 2:
                            act.wait_ge(out_done, b * NCH + 2)
                        nc.scalar.activation(fix[c % 2][:, :], bank(6 + c % 2), ACT.Identity, bias=bnv[:, 3:4], scale=bnv[:, 1:2]).then_inc(fix_done, 1)
                    norm.first_act(act, b, tn, eps_t)
                    if not last:
                        keys(b + 1, EARLY)
                    act.wait_ge(exp_in, b + 1)
                    nc.scalar.activation(exl[:, :, :], exl[:, :, :], ACT.Exp).then_inc(exp_done, 1)
                    if not last:
                        keys(b + 1, LATE)
                    for c in range(NCH):
                        for e in range(E):
                            u = (b * NCH + c) * E + e
                            act.wait_ge(up_pe, u + 2 * E + 1)
                            act.wait_ge(scaled_done, u + 1)
                            nc.scalar.activation(hid[e % 2][:, :], bank(e % 2), ACT.Gelu, bias=b1[:, e:e + 1]).then_inc(hid_done, 1)

                keys(0, range(KVS))
                with act.Fori(0, B - 1) as b:
                    body(b, False)
                body(B - 1, True)

            @block.gpsimd
            def _(pool):
                pool.sem_inc(x3_done, 2)
                pool.sem_inc(out_done, 2)
                with pool.Fori(0, B) as b:
                    for c in range(NCH):
                        pool.wait_ge(x2_loaded[c // 2], b * 16 + 16)
                        pool.wait_ge(fix_done, b * NCH + c + 3)
                        nc.gpsimd.tensor_tensor(x(c), x(c), fix[c % 2][:, :], ALU.add).then_inc(x3_done, 1)

                    def split(c):
                        n, k = b * NCH + c, c % 2
                        pool.wait_ge(norm.out_done, b * NCH + c + 3)
                        pool.wait_ge(up_pe, n * E + E)
                        passed(pool)
                        nc.gpsimd.tensor_copy(tnh[k][:, :], tn(c)).then_inc(tnh_done, 1)
                        pool.wait_ge(tnh_done, n + 1)
                        nc.gpsimd.tensor_tensor(tnl[k][:, :], tn(c), tnh[k][:, :].bitcast(F32), ALU.subtract).then_inc(tnl_done, 1)

                    def add(c):
                        pool.wait_ge(fin_done, b * NCH + c + 3)
                        nc.gpsimd.tensor_tensor(x(c), x(c), fix[c % 2][:, :], ALU.add).then_inc(out_done, 1)

                    split(0)
                    split(1)
                    for c in range(NCH):
                        add(c)
                        if c + 2 < NCH:
                            split(c + 2)

            @block.vector
            def _(dve):
                norm.start_dve(dve)
                for sm in (att_done, scaled_done, fin_done):
                    dve.sem_inc(sm, 2)
                setup = Chain(dve, set_done)
                setup(nc.vector.memset(eps_t[:, :], EPS_T))
                setup(nc.vector.memset(eps_a[:, :], EPS_ATT))
                for k in range(2):
                    setup(nc.vector.memset(vt[k][:, :, :], 1.0))
                    setup(nc.vector.memset(den_w[k][:, :], 0.0))
                dve.wait_ge(const_loaded, 16 * len(consts))
                dve.sem_inc(bn_in, 1)
                wide = lambda t: t[:, :, :].rearrange("p e c -> p (e c)")
                setup(nc.vector.tensor_copy(wide(sel), sel32))
                setup(nc.vector.tensor_copy(wide(row_spread), rows32))
                setup(nc.vector.tensor_copy(wide(spread_bf), spread32))
                setup(nc.vector.tensor_copy(wide(w1h), w1_32))
                setup(nc.vector.tensor_tensor(wide(w1l), w1_32, wide(w1h).bitcast(F32), ALU.subtract))
                setup(nc.vector.tensor_copy(ident_bf[:, :], ident[:, :]))
                setup(nc.vector.tensor_copy(b2s[:, 0, :], b2[:, :]))
                setup(nc.vector.tensor_tensor(b2r[:, :], b2[:, :], b2s[:, 0, :], ALU.subtract))
                setup(nc.vector.tensor_copy(b2s[:, 1, :], b2r[:, :]))
                setup(nc.vector.tensor_tensor(b2r[:, :], b2r[:, :], b2s[:, 1, :], ALU.subtract))
                setup(nc.vector.tensor_copy(b2s[:, 2, :], b2r[:, :]))
                dve.wait_ge(bn_act, 1)
                setup(nc.vector.reciprocal(bnv[:, 2:3], bnv[:, 0:1]))
                setup(nc.vector.tensor_tensor(bnv[:, 1:2], bn[:, 0:1], bnv[:, 2:3], ALU.mult))
                setup(nc.vector.tensor_tensor(bnv[:, 2:3], bn[:, 2:3], bnv[:, 1:2], ALU.mult))
                setup(nc.vector.tensor_tensor(bnv[:, 3:4], bn[:, 1:2], bnv[:, 2:3], ALU.subtract))
                dve.sem_inc(small_ready, 1)

                def key_matrices(b):
                    middle = slice((NCH - 1) * HEADS, NCH * HEADS)
                    for s in range(2):
                        dve.wait_ge(kv_pe, b * KVS + (s + 1) * NCH)
                        nc.vector.tensor_tensor(num_w[s][:, :], kv_bank(s)[:, 0:128], heads[:, :], ALU.mult)
                        nc.vector.tensor_scalar(den_w[s][:, middle], head_of[:, :], kv_bank(s)[:, 128:129], None, ALU.mult).then_inc(kv_ready, 1)

                def reciprocals(b):
                    for s in range(2):
                        n = b * 2 + s
                        dve.wait_ge(nd_pe, b * KVS + (s + 1) * NCH + 8)
                        link = Chain(dve, rec_own, n * 3)
                        link(nc.vector.tensor_scalar(den[:, :], bank(2 + s), eps_a[:, :], None, ALU.add))
                        link(nc.vector.reciprocal(rec[:, :], den[:, :]))
                        link(nc.vector.tensor_copy(rec_hi[s][:, :], rec[:, :]))
                        nc.vector.tensor_tensor(rec_lo[s][:, :], rec[:, :], rec_hi[s][:, :].bitcast(F32), ALU.subtract).then_inc(lo_done, 1)
                        dve.wait_ge(lo_done, n + 1)

                def weighted(b):
                    dve.wait_ge(num_done, b * KVS + KVS + 2)
                    for c in range(NCH):
                        for s in range(2):
                            a = ATT[s][:, c * CH:(c + 1) * CH]
                            dve.wait_ge(cast_pe, (b * NCH + c) * 2 + s + 1)
                            nc.vector.tensor_tensor(a, a, bank(4 + s), ALU.mult).then_inc(att_done, 1)

                def router(b):
                    link = Chain(dve, own, b * LINKS)
                    dve.wait_ge(logit_pe, b * NCH + NCH)
                    logits = bank(6)[:, 0:NT * E].rearrange("p (t e) -> p t e", e=E)
                    per_e = lambda t: t[:, :].unsqueeze(2).broadcast_to([128, NT, E])
                    link(nc.vector.tensor_reduce(top[:, :], logits, AX.X, ALU.max))
                    link(nc.vector.tensor_tensor(exl[:, :, :], logits, per_e(top), ALU.subtract))
                    dve.sem_inc(exp_in, 1)
                    dve.wait_ge(exp_done, b + 1)
                    link(nc.vector.tensor_reduce(tot[:, :], exl[:, :, :], AX.X, ALU.add))
                    link(nc.vector.reciprocal(tot[:, :], tot[:, :]))
                    link(nc.vector.tensor_tensor(prob[:, :, :], exl[:, :, :], per_e(tot), ALU.mult))
                    mine = prob[:, :, :].unsqueeze(3).broadcast_to([128, NT, E, E])
                    other = prob[:, :, :].unsqueeze(2).broadcast_to([128, NT, E, E])
                    grid = lambda t: t[:, :, :].rearrange("p t (e f) -> p t e f", f=E)
                    link(nc.vector.tensor_tensor(grid(more), other, mine, ALU.is_gt))
                    link(nc.vector.tensor_tensor(grid(same), other, mine, ALU.is_equal))
                    link(nc.vector.tensor_tensor(same[:, :, :], same[:, :, :], before[:, :].unsqueeze(1).broadcast_to([128, NT, E * E]), ALU.mult))
                    link(nc.vector.tensor_tensor(more[:, :, :], more[:, :, :], same[:, :, :], ALU.add))
                    link(nc.vector.tensor_reduce(rest[:, :, :], grid(more), AX.X, ALU.add))
                    link(nc.vector.scalar_tensor_tensor(out=comb[:, :, :], in0=rest[:, :, :], scalar=1.5, in1=prob[:, :, :],
                                                        op0=ALU.is_lt, op1=ALU.mult))
                    link(nc.vector.tensor_reduce(tot[:, :], comb[:, :, :], AX.X, ALU.add))
                    link(nc.vector.tensor_scalar(tot[:, :], tot[:, :], 1e-12, None, ALU.max))
                    link(nc.vector.reciprocal(tot[:, :], tot[:, :]))
                    link(nc.vector.tensor_tensor(comb[:, :, :], comb[:, :, :], per_e(tot), ALU.mult))
                    link(nc.vector.tensor_copy(parts[:, :, 0:E], comb[:, :, :]))
                    link(nc.vector.tensor_tensor(rest[:, :, :], comb[:, :, :], parts[:, :, 0:E], ALU.subtract))
                    link(nc.vector.tensor_copy(parts[:, :, E:2 * E], rest[:, :, :]))
                    link(nc.vector.tensor_tensor(rest[:, :, :], rest[:, :, :], parts[:, :, E:2 * E], ALU.subtract))
                    link(nc.vector.tensor_copy(parts[:, :, 2 * E:3 * E], rest[:, :, :]))
                    assert link.count == LINKS
                    dve.sem_inc(parts_done, 1)

                def body(b, last):
                    reciprocals(b)
                    weighted(b)
                    norm.first_dve(dve, b, x, tn)
                    norm.between_dve(dve, b)
                    norm.second_dve(dve, b, tn)
                    router(b)
                    if not last:
                        key_matrices(b + 1)
                    dve.wait_ge(parts_pe, b + 1)
                    nc.vector.tensor_copy(parts_t[:, :], turned).then_inc(parts_t_done, 1)
                    def finish(c):
                        n = b * NCH + c
                        dve.wait_ge(moe_pe, n * E + E + 2)
                        dve.wait_ge(out_done, n + 1)
                        nc.vector.tensor_tensor(fix[c % 2][:, :], moe_bank(c % 2), tn(c), ALU.add).then_inc(fin_done, 1)

                    for c in range(NCH):
                        for e in range(E):
                            u = (b * NCH + c) * E + e
                            dve.wait_ge(hid_done, u + 3)
                            dve.wait_ge(spread_pe, u + 1)
                            dve.wait_ge(moe_pe, u + 1)
                            nc.vector.tensor_tensor(scaled[e % 2][:, :], hid[e % 2][:, :], bank(2 + e % 2), ALU.mult).then_inc(scaled_done, 1)
                            if c and e == 2:
                                finish(c - 1)
                    finish(NCH - 1)

                key_matrices(0)
                with dve.Fori(0, B - 1) as b:
                    body(b, False)
                body(B - 1, True)


def build(nc, d):
    with ExitStack() as ctx:
        sb = lambda name, shape: ctx.enter_context(nc.sbuf_tensor(name, shape, F32))
        route = sb("pick", [128, B, 2, E]), sb("pickw", [128, B, 2, E]), sb("dense", [128, B, E])
        passed = passing(ctx.enter_context(nc.semaphore("passed")))
        phase_project(nc, d, passed)
        phase_dft(nc, d, passed)
        phase_mix(nc, d, passed)
        phase_route0(nc, d, route)
        phase_ffn0(nc, d, passed, route)
        phase_conv(nc, d, passed)
        phase_attention(nc, d, passed)


def shape_constants():
    import math

    import numpy as np
    f = np.float32
    i = np.arange(SIDE)
    row = PH * (i % HB) + i // HB
    cos = lambda a, b: np.cos(2 * np.pi * np.outer(a, b) / SIDE) / 8
    sin = lambda a, b: np.sin(2 * np.pi * np.outer(a, b) / SIDE) / 8
    cat = lambda *t: np.concatenate(t, 1)
    dft = cat(cos(row, i), -sin(row, i), cos(row, i), -sin(row, i), sin(row, i), cos(row, i),
              cos(i, row), sin(i, row), -sin(i, row), cos(i, row), cos(i, row), -sin(i, row))
    y, x = (i.astype(f) - SIDE // 2)[:, None], (i.astype(f) - SIDE // 2)[None, :]
    theta = (np.arctan2(y, x).astype(f) + f(math.pi)) % f(math.pi)
    radii = SIDE // 2 // 8 + 1
    ring = np.clip(np.floor(np.sqrt(y * y + x * x) / f(8)).astype(np.int32), 0, radii - 1)
    delta = math.pi / 8
    half = 1.5 * delta / 2.0
    centers = (np.arange(8, dtype=f) * f(delta) + f(delta / 2.0))[:, None, None]
    dist = np.abs(theta[None] - centers)
    w = np.clip(f(1.0) - dist / f(half), 0, None) * (dist < f(half))
    angle = w / (w.sum(0, keepdims=True) + f(1e-8))
    mask = angle[:, None] * (ring[None, None] == np.arange(radii)[None, :, None, None])
    mask = np.roll(mask, (-(SIDE // 2), -(SIDE // 2)), (2, 3)).transpose(0, 1, 3, 2).reshape(8 * radii, HW)
    e = np.arange(E)
    c = np.arange(128)
    spread = np.tile(np.repeat(np.eye(E), 128, 1), (3, 1))
    rows = np.zeros((128, 2 * NCH - 1))
    rows[:, NCH - 1] = 1 / 128
    spread_rows = np.zeros((Norm.LOW + NCH, NCH, 128))
    for k in range(NCH):
        spread_rows[[k, Norm.LOW + k], k] = 1
    head_rows = (c[:, None, None] // 16 == np.arange(NCH)[None, :, None]) & (c[:, None, None] % 16 == c[None, None, :] // 8)
    return {"ones": np.full((128, 128), 1 / 128), "rows": rows, "spread_rows": spread_rows.reshape(Norm.LOW + NCH, -1), "ident": np.eye(128), "dft": dft, "mask": mask,
            "before": np.tile((e[None, :] < e[:, None]).reshape(1, -1), (128, 1)),
            "heads": c[:, None] // 8 == c[None, :] // 8, "head_of": c[:, None] // 8 == np.arange(16)[None, :],
            "head_rows": head_rows.reshape(128, -1), "spread": spread}


def lay_out(v):
    import numpy as np
    t = lambda a: np.ascontiguousarray(a)
    a = {"x": v["x"].reshape(B, C, HB, 2, 2, HB, 2, 2).transpose(0, 1, 3, 6, 4, 7, 2, 5).reshape(B, C, HW)}
    a["w_in"], a["w_out"] = v["L0_conv_w_in"].T, v["L0_conv_w_out"].T
    a["binw"] = v["L0_conv_bin_weights"].reshape(MID, -1).T
    a["wr"], a["br"] = v["L0_ffn_Wr"], np.tile(v["L0_ffn_br"][None], (128, 1))
    a["w1"] = np.concatenate([v["L0_ffn_W1"].transpose(1, 0, 2), v["L0_ffn_b1"].reshape(E, 2, 128).transpose(2, 0, 1)], 2)
    a["w2"] = np.concatenate([v["L0_ffn_W2"].reshape(E, 2, 128, C).transpose(2, 0, 1, 3).reshape(128, E, F0),
                              v["L0_ffn_b2"].T[:, :, None]], 2)
    a["gb"] = np.stack([v["L0_ffn_gamma"], v["L0_ffn_beta"]], 1)
    order = (24 * np.arange(16)[None, :, None] + 8 * np.arange(3)[:, None, None] + np.arange(8)[None, None, :]).reshape(3, 128)
    a["wq"] = v["L1_conv_w_qkv"][:, :, 0, 0][order].transpose(2, 0, 1)
    flat = order.reshape(GROUPS, GC)
    wdw, wpw = v["L1_conv_w_dw"][:, 0], v["L1_conv_w_pw"][:, :, 0, 0]
    dw = np.zeros((2, 2, GC, 2, 2, GROUPS, 2, 2, 2, 2, 2, 2), np.float32)

    def offset(s, p, f):
        return PH * s + p - (f - 2 if f >= 2 else f + 2)

    bits = np.array(list(np.ndindex(2, 2, 2, 2, 2)))
    for hr, fr, sr, gr, er in bits:
        for hc, fc, sc, gc, ec in bits:
            dy, dx = offset(sr, 2 * hr + fr, 2 * gr + er), offset(sc, 2 * hc + fc, 2 * gc + ec)
            if 0 <= dy < 5 and 0 <= dx < 5:
                dw[hr, hc, :, fr, fc, :, sr, sc, gr, gc, er, ec] = wdw[flat][:, :, dy, dx].T
    a["dw"] = dw.reshape(128, GROUPS, TAPS * PH * PH)
    pw = np.zeros((4, GC, PH, GROUPS, GC), np.float32)
    for ci in range(GC):
        same = np.arange(ci // 4 * 4, ci // 4 * 4 + 4)
        pw[:, ci, :, :, same] = wpw[flat[:, same], ci % 4].T[:, None, None]
    a["pw"] = pw.reshape(128, GROUPS, GC)
    a["wp"] = v["L1_conv_w_proj"][:, :, 0, 0].reshape(C, 2, 128).transpose(2, 1, 0)
    a["bn"] = np.stack([v["L1_conv_bn_" + n] for n in ("gamma", "beta", "mean", "var")], 1)
    a["wr1"] = v["L1_ffn_router_w"].T
    a["m1"], a["m2"] = v["L1_ffn_w1"].transpose(1, 0, 2), v["L1_ffn_w2"].transpose(1, 0, 2)
    a["mb1"], a["mb2"] = v["L1_ffn_b1"].T, np.tile(v["L1_ffn_b2"], (3, 1))
    return {k: t(x) for k, x in a.items()}


SCRATCH = {"s": (B, C, HW), "pm": (B, MID, HW), "xe": (B, MID, HW), "x1": (B, C, HW), "tn": (B, C, HW), "total": (C, B), "x2": (B, C, HW),
           "qkv": (B, 3, 4, C, HW // 4), "agg": (B, 3, 4, C, HW // 4)}


def kernel(**inputs):
    import numpy as np
    import concourse.bacc as bacc
    from concourse.bass_utils import run_bass_kernel_spmd

    arrays = lay_out({k: np.asarray(x) for k, x in inputs.items()})
    arrays.update({k: np.ascontiguousarray(x, dtype=np.float32) for k, x in shape_constants().items()})
    nc = bacc.Bacc("TRN2", target_bir_lowering=False, num_devices=1)
    d = {k: nc.dram_tensor("in_" + k, x.shape, F32, kind="ExternalInput").ap() for k, x in arrays.items()}
    d.update({k: nc.dram_tensor("scratch_" + k, shape, F32, kind="Internal").ap() for k, shape in SCRATCH.items()})
    d["out"] = nc.dram_tensor("out", (B, C, HW), F32, kind="ExternalOutput").ap()
    build(nc, d)
    got = run_bass_kernel_spmd(nc, [{"in_" + k: x for k, x in arrays.items()}], core_ids=[0]).results[0]["out"]
    return got.reshape(B, C, 2, 2, 2, 2, HB, HB).transpose(0, 1, 6, 2, 4, 7, 3, 5).reshape(B, C, SIDE, SIDE)
```
